# Optimizing a Trainium2 kernel written in Bass

```python
import numpy as np
import jax
import jax.numpy as jnp

def _softmax(x, axis=-1):
    return jax.nn.softmax(x, axis=axis)

def _gelu(x):
    return jax.nn.gelu(x, approximate=True)

def _silu(x):
    return jax.nn.silu(x)

def _sigmoid(x):
    return jax.nn.sigmoid(x)

def _layernorm(x, axis=-1, eps=1e-05):
    m = jnp.mean(x, axis=axis, keepdims=True)
    v = jnp.var(x, axis=axis, keepdims=True)
    return (x - m) / jnp.sqrt(v + eps)

def _scatter_add(tgt, idx, src, axis=0):
    return tgt.at[idx].add(src)

def _segment_sum(src, seg, n):
    return jax.ops.segment_sum(src, seg, n)
kernel_name = 'mk_gnn_preln_d4_gnn_r64_e9a030'

def setup_inputs(seed: int=0):
    np.random.seed(seed)
    _w = jnp.asarray

    def _rec_inputs():
        import jax
        import jax.numpy as jnp
        _gk = jax.random.key(seed)
        x = -0.000202 + 1 * jax.random.normal(jax.random.fold_in(_gk, 1), (100000, 128), jnp.float32)
        src = jax.random.randint(jax.random.fold_in(_gk, 2), (25000,), 0, 100000, jnp.int32)
        dst = jax.random.randint(jax.random.fold_in(_gk, 3), (25000,), 0, 100000, jnp.int32)
        _o = jnp.argsort(dst, stable=True)
        src = src[_o]
        dst = dst[_o]
        edge_attr_128 = -4.21973e-05 + 0.999841 * jax.random.normal(jax.random.fold_in(_gk, 11), (25000, 128), jnp.float32)
        edge_attr_2 = jax.random.uniform(jax.random.fold_in(_gk, 12), (25000, 2), jnp.float32, 0.0, 0.999999)
        return (x, src, dst, edge_attr_128, edge_attr_2)
    x, src, dst, edge_attr_128, edge_attr_2 = _rec_inputs()

    def _L0_gnn_setup():
        import jax, jax.numpy as jnp
        import numpy as np
        EPS = 1e-08
        BN_EPS = 1e-05
        N_NODES = 50000
        N_EDGES = 9375
        C = 128
        key = jax.random.key(seed)
        k1, k2, k3, k4, k5 = jax.random.split(key, 5)
        x = jax.random.normal(k1, (N_NODES, C), dtype=jnp.float32)
        edge_attr = jax.random.normal(k2, (N_EDGES, C), dtype=jnp.float32)
        edge_index = jax.random.randint(k3, (2, N_EDGES), 0, N_NODES, dtype=jnp.int64)
        W_gea = jax.random.normal(k4, (C, C), dtype=jnp.float32) / np.sqrt(C)
        W_lin = jax.random.normal(k5, (C, C), dtype=jnp.float32) / np.sqrt(C)
        gamma = jnp.ones((C,), dtype=jnp.float32)
        beta = jnp.zeros((C,), dtype=jnp.float32)
        return {'x': x, 'edge_attr': edge_attr, 'edge_index': edge_index, 'W_gea': W_gea, 'W_lin': W_lin, 'gamma': gamma, 'beta': beta}
    _L0_gnn_all = _L0_gnn_setup()
    _L0_gnn_in = {k: v for k, v in _L0_gnn_all.items() if k in ('W_gea', 'W_lin', 'gamma', 'beta')}
    del _L0_gnn_all

    def _L1_gnn_setup():
        import jax, jax.numpy as jnp
        import numpy as np
        NEG_SLOPE = 0.2
        key = jax.random.key(seed)
        ks = jax.random.split(key, 8)
        N, IN, H, C = (50000, 128, 4, 32)
        E = 12500
        TD = H * C
        x = jax.random.normal(ks[0], (N, IN), dtype=jnp.float32)
        edge_index = jax.random.randint(ks[1], (2, E), 0, N, dtype=jnp.int64)
        edge_attr = jax.random.uniform(ks[2], (E, 2), dtype=jnp.float32)
        W_lin = jax.random.normal(ks[3], (TD, IN), dtype=jnp.float32) * (2.0 / (IN + TD)) ** 0.5
        att = jax.random.normal(ks[4], (H, C), dtype=jnp.float32) * (2.0 / (H + C)) ** 0.5
        W_eb = jax.random.normal(ks[5], (H, 1), dtype=jnp.float32) * (2.0 / (H + 1)) ** 0.5
        bias = jnp.zeros((TD,), dtype=jnp.float32)
        W_res = jax.random.normal(ks[6], (TD, IN), dtype=jnp.float32) * (2.0 / (IN + TD)) ** 0.5
        return {'x': x, 'edge_index': edge_index, 'edge_attr': edge_attr, 'W_lin': W_lin, 'att': att, 'W_eb': W_eb, 'bias': bias, 'W_res': W_res}
    _L1_gnn_all = _L1_gnn_setup()
    _L1_gnn_in = {k: v for k, v in _L1_gnn_all.items() if k in ('W_lin', 'att', 'W_eb', 'bias', 'W_res')}
    del _L1_gnn_all

    def _L2_gnn_setup():
        import jax, jax.numpy as jnp
        import numpy as np
        N_NODES = 100000

        def _mean_aggregate(feat, src, dst, num_nodes):
            summed = jax.ops.segment_sum(feat[src], dst, num_segments=num_nodes)
            deg = jax.ops.segment_sum(jnp.ones((src.shape[0],), feat.dtype), dst, num_segments=num_nodes)
            return summed / jnp.maximum(deg, 1.0)[:, None]
        key = jax.random.key(seed)
        k1, k2, k3 = jax.random.split(key, 3)
        feat = jax.random.normal(k1, (N_NODES, 128), dtype=jnp.float32)
        W = jax.random.normal(k2, (128, 384), dtype=jnp.float32) * 0.05
        edge_index = jax.random.randint(k3, (2, 12500), 0, N_NODES, dtype=jnp.int32)
        return {'feat': feat, 'W': W, 'edge_index': edge_index}
    _L2_gnn_all = _L2_gnn_setup()
    _L2_gnn_in = {k: v for k, v in _L2_gnn_all.items() if k in ('W',)}
    del _L2_gnn_all

    def _L3_gnn_setup():
        import jax, jax.numpy as jnp
        import numpy as np
        N_NODES = 100000
        N_EDGES = 25000
        HIDDEN = 128
        key = jax.random.key(seed)
        k1, k2, k3, k4, k5 = jax.random.split(key, 5)
        scale = 1.0 / np.sqrt(HIDDEN)
        return {'smashed_data': jax.random.normal(k1, (N_NODES, HIDDEN), dtype=jnp.float32), 'edge_index': jax.random.randint(k2, (2, N_EDGES), 0, N_NODES, dtype=jnp.int64), 'W_l': jax.random.normal(k3, (HIDDEN, HIDDEN), dtype=jnp.float32) * scale, 'W_r': jax.random.normal(k4, (HIDDEN, HIDDEN), dtype=jnp.float32) * scale, 'b_l': jax.random.normal(k5, (HIDDEN,), dtype=jnp.float32) * scale}
    _L3_gnn_all = _L3_gnn_setup()
    _L3_gnn_in = {k: v for k, v in _L3_gnn_all.items() if k in ('W_l', 'W_r', 'b_l')}
    del _L3_gnn_all
    return {'x': x, 'src': src, 'dst': dst, 'edge_attr_128': edge_attr_128, 'edge_attr_2': edge_attr_2, 'L0_gnn_W_gea': _L0_gnn_in['W_gea'], 'L0_gnn_W_lin': _L0_gnn_in['W_lin'], 'L0_gnn_gamma': _L0_gnn_in['gamma'], 'L0_gnn_beta': _L0_gnn_in['beta'], 'L1_gnn_W_lin': _L1_gnn_in['W_lin'], 'L1_gnn_att': _L1_gnn_in['att'], 'L1_gnn_W_eb': _L1_gnn_in['W_eb'], 'L1_gnn_bias': _L1_gnn_in['bias'], 'L1_gnn_W_res': _L1_gnn_in['W_res'], 'L2_gnn_W': _L2_gnn_in['W'], 'L3_gnn_W_l': _L3_gnn_in['W_l'], 'L3_gnn_W_r': _L3_gnn_in['W_r'], 'L3_gnn_b_l': _L3_gnn_in['b_l']}

def reference(x, src, dst, edge_attr_128, edge_attr_2, L0_gnn_W_gea, L0_gnn_W_lin, L0_gnn_gamma, L0_gnn_beta, L1_gnn_W_lin, L1_gnn_att, L1_gnn_W_eb, L1_gnn_bias, L1_gnn_W_res, L2_gnn_W, L3_gnn_W_l, L3_gnn_W_r, L3_gnn_b_l):
    import jax
    import jax.numpy as jnp

    def _L0_gnn_ref(x, edge_attr, edge_index, W_gea, W_lin, gamma, beta):
        import jax, jax.numpy as jnp
        import numpy as np
        EPS = 1e-08
        BN_EPS = 1e-05
        N_NODES = 50000
        N_EDGES = 9375
        C = 128
        src = edge_index[0]
        tgt = edge_index[1]
        n = x.shape[0]
        ea = jax.nn.sigmoid(edge_attr)
        denom = jax.ops.segment_sum(ea, tgt, num_segments=n)
        atten = ea / (denom[tgt] + EPS)
        msg = atten * (x[src] @ W_gea.T)
        agg = jax.ops.segment_sum(msg, tgt, num_segments=n)
        h = x @ W_lin.T + agg
        mean = jnp.mean(h, axis=0)
        var = jnp.var(h, axis=0)
        h = (h - mean) * jax.lax.rsqrt(var + BN_EPS) * gamma + beta
        return x + jax.nn.relu(h)

    def _L1_gnn_ref(x, edge_index, edge_attr, W_lin, att, W_eb, bias, W_res):
        import jax, jax.numpy as jnp
        import numpy as np
        NEG_SLOPE = 0.2
        N = x.shape[0]
        H, C = att.shape
        reduced = edge_attr[:, 0] + 0.35 * edge_attr[:, 1]
        loops = jnp.arange(N, dtype=edge_index.dtype)
        src = jnp.concatenate([edge_index[0], loops])
        dst = jnp.concatenate([edge_index[1], loops])
        reduced = jnp.concatenate([reduced, jnp.ones((N,), dtype=x.dtype)])
        proj = (x @ W_lin.T).reshape(N, H, C)
        ps = proj[src]
        pd = proj[dst]
        z = jax.nn.leaky_relu(ps + pd, negative_slope=NEG_SLOPE)
        logits = jnp.einsum('ehc,hc->eh', z, att) + reduced[:, None] * W_eb[:, 0][None, :]
        mx = jax.ops.segment_max(logits, dst, num_segments=N)
        e = jnp.exp(logits - mx[dst])
        denom = jax.ops.segment_sum(e, dst, num_segments=N)
        attn = e / jnp.maximum(denom[dst], 1e-12)
        msg = attn[:, :, None] * ps
        out = jax.ops.segment_sum(msg, dst, num_segments=N)
        out = out.reshape(N, H * C)
        out = out + x @ W_res.T
        return out + bias

    def _L2_gnn_ref(feat, W, edge_index):
        import jax, jax.numpy as jnp
        import numpy as np
        N_NODES = 100000

        def _mean_aggregate(feat, src, dst, num_nodes):
            summed = jax.ops.segment_sum(feat[src], dst, num_segments=num_nodes)
            deg = jax.ops.segment_sum(jnp.ones((src.shape[0],), feat.dtype), dst, num_segments=num_nodes)
            return summed / jnp.maximum(deg, 1.0)[:, None]
        src, dst = (edge_index[0], edge_index[1])
        n = feat.shape[0]
        h_self = feat
        fwd_neigh = _mean_aggregate(feat, src, dst, n)
        bwd_neigh = _mean_aggregate(feat, dst, src, n)
        h = jnp.concatenate((h_self, fwd_neigh, bwd_neigh), axis=1)
        rst = h @ W.T
        return jax.nn.relu(rst)

    def _L3_gnn_ref(smashed_data, edge_index, W_l, W_r, b_l):
        import jax, jax.numpy as jnp
        import numpy as np
        N_NODES = 100000
        N_EDGES = 25000
        HIDDEN = 128
        n = smashed_data.shape[0]
        src = edge_index[0]
        dst = edge_index[1]
        msgs = jnp.take(smashed_data, src, axis=0)
        agg = jax.ops.segment_sum(msgs, dst, num_segments=n)
        cnt = jax.ops.segment_sum(jnp.ones((src.shape[0],), dtype=smashed_data.dtype), dst, num_segments=n)
        mean = agg / jnp.maximum(cnt, 1.0)[:, None]
        out = mean @ W_l.T + b_l + smashed_data @ W_r.T
        return out
    edge_index = jnp.stack([src, dst])
    h = jnp.maximum(_layernorm(x, axis=-1), 0.0)
    x = x + _L0_gnn_ref(h, edge_attr_128, edge_index, L0_gnn_W_gea, L0_gnn_W_lin, L0_gnn_gamma, L0_gnn_beta)
    h = jnp.maximum(_layernorm(x, axis=-1), 0.0)
    x = x + _L1_gnn_ref(h, edge_index, edge_attr_2, L1_gnn_W_lin, L1_gnn_att, L1_gnn_W_eb, L1_gnn_bias, L1_gnn_W_res)
    h = jnp.maximum(_layernorm(x, axis=-1), 0.0)
    x = x + _L2_gnn_ref(h, L2_gnn_W, edge_index)
    h = jnp.maximum(_layernorm(x, axis=-1), 0.0)
    x = x + _L3_gnn_ref(h, edge_index, L3_gnn_W_l, L3_gnn_W_r, L3_gnn_b_l)
    return x

_drawn_inputs = setup_inputs


def setup_inputs(seed=0):
    import zlib

    import numpy as np

    out = dict(_drawn_inputs(seed))
    spreads = {'L0_gnn_gamma': (1.0, 0.2), 'L0_gnn_beta': (0.0, 0.1), 'L1_gnn_bias': (0.0, 0.1)}
    factors = {'edge_attr_128': 4.98, 'edge_attr_2': 7.143, 'L1_gnn_W_eb': 8.0}
    for name, (base, spread) in spreads.items():
        noise = np.random.default_rng([zlib.crc32(name.encode()), seed]).standard_normal(out[name].shape)
        drawn = base * np.exp(spread * noise) if base else spread * noise
        out[name] = jnp.asarray(drawn.astype(out[name].dtype))
    for name, factor in factors.items():
        out[name] = (out[name] * factor).astype(out[name].dtype)
    return out
```

```python
import concourse.bass as bass
from concourse import mybir
from contextlib import ExitStack, contextmanager

f32 = mybir.dt.float32
bf16 = mybir.dt.bfloat16
i32 = mybir.dt.int32
ALU = mybir.AluOpType
ACT = mybir.ActivationFunctionType
AX = mybir.AxisListType

P = 125
J = 8
B = P * J
C = 128
H = 4
HC = C // H
HALF = J // 2
LN_EPS = 1e-5
BN_EPS = 1e-5
GATE_EPS = 1e-8
SLOPE = 0.2
FAR = 1e30


class Unit:

    def __init__(self, name, x, parts=(), adds=False, gram=False, ready=None):
        self.name, self.x, self.parts, self.adds, self.gram = name, x, list(parts), adds, gram
        self.ready = ready


class Plan:

    def __init__(self, units):
        self.units = units
        self.n = len(units)
        self.part = []
        for k, u in enumerate(units):
            for half in range(2):
                for q, p in enumerate(u.parts):
                    self.part.append((k, half, q, p[2]))
        self.parts = len(self.part)
        self.by = {c: sum(p[3] == c for p in self.part) for c in "DA"}
        self.adders = sum(u.adds for u in units)
        self.plain = [k for k, u in enumerate(units) if not u.gram]

    def index(self, k, half, q):
        return next(n for n, p in enumerate(self.part) if p[:3] == (k, half, q))

    def consumed(self, n, c):
        return sum(p[3] == c for p in self.part[:n + 1])

    def added(self, k):
        return sum(u.adds for u in self.units[:k + 1])

    def turned(self, k):
        return sum(not u.gram for u in self.units[:k])

    def before(self, k):
        return k - 2 if k >= 2 else None


def split_load(eng, dst, src, sem):
    eng.dma_start(dst[0:112], src[0:112]).then_inc(sem, 16)
    return eng.dma_start(dst[112:P], src[112:P]).then_inc(sem, 16)


def gnn_program(nc, x, src_pt, dst_pt, dst_prev_pt, dst_next_pt, src_row, dst_row, dst_prev_row,
                edge_attr, edge_attr2_pt, w_gea, w_lin0, w_lin0_t, gamma, beta, w_lin1, att, w_eb, bias1, w_res1,
                w_self2, w_fwd2, w_bwd2, w_l3, w_r3, b_l3, out):
    N, E = x.shape[0], edge_attr.shape[0]
    NB, EIT, T = N // B, E // B, E // P
    assert NB * B == N and EIT * B == E and NB == 4 * EIT
    CW = C + 1
    PE_, DV, AC, GP, SP_ = nc.tensor, nc.vector, nc.scalar, nc.gpsimd, nc.sync

    def dram(name, shape, dt=f32):
        return nc.dram_tensor(name, shape, dt, kind="Internal").ap()

    slot_of = dram("slot_of", [N + 1, 1], i32)
    a0 = {s: dram(f"x_plus_h_{s}", [E, C]) for s in "DS"}
    y0 = {s: dram(f"conv_{s}", [E, C]) for s in "DS"}
    proj1 = dram("proj1", [2 * E, C])
    res1 = dram("x1_plus_res", [E, C])
    x2t = {s: dram(f"x2_{s}", [E, C]) for s in "DS"}
    self2 = {s: dram(f"self2_{s}", [E, C]) for s in "DS"}
    fwd2 = dram("fwd2", [2 * E, C])
    bwd2 = dram("bwd2", [2 * E, C])
    back = dram("back_sums", [2 * E + P, CW])
    proj3 = dram("proj3", [2 * E, C])
    x4 = {s: dram(f"x4_{s}", [E, C]) for s in "DS"}

    def own(t, i):
        return t[bass.ds(i * B, B), :].rearrange("(p j) c -> p j c", j=J)

    def rows(t, i, base=0):
        return t[bass.ds(i * B + base, B), :].rearrange("(j p) c -> p j c", p=P)

    top = ExitStack()

    pool_passed = top.enter_context(nc.semaphore("pool_passed"))
    sp_passed = top.enter_context(nc.semaphore("sp_passed"))

    @contextmanager
    def cleared_semaphore(name):
        sem = nc.alloc_semaphore(name)
        used.append(sem)
        yield sem

    used = []

    def sem_of(ctx, name):
        return ctx.enter_context(cleared_semaphore(name))

    def clear_semaphores():
        nc.clear_and_free_semaphores(used)
        nc.all_engine_barrier()
        used.clear()

    def keep(name, shape, dt=f32):
        return top.enter_context(nc.sbuf_tensor(name, shape, dt))

    ident = keep("ident", [128, 128])
    W = {n: keep(f"W_{n}", [C, C]) for n in
         ("gea", "lin0", "lin0_rows", "bn0", "lin1", "res1", "sum1", "self2", "fwd2", "bwd2", "l3", "r3")}
    bias3 = {n: keep(f"bias_{n}", [3, HALF * C], bf16) for n in ("bn0", "l1", "l3")}
    ones3 = keep("ones3", [3, P], bf16)
    eps_col = keep("eps_col", [128, 1])
    gam_col = keep("gam_col", [C, 1])
    bet_col = keep("bet_col", [C, 1])
    gram_sb = keep("gram_sb", [C, CW + 2])
    bn_mul = keep("bn_mul", [P, C])
    bn_add = keep("bn_add", [P, C])
    src_i = keep("src_i", [P, T], i32)
    dst_i = keep("dst_i", [P, T], i32)
    prev_i = keep("prev_i", [P, T], i32)
    leads = keep("leads", [P, T])
    lead_i = keep("lead_i", [P, T], i32)
    again = keep("again", [P, T])
    once_i = keep("once_i", [P, T], i32)
    slot_e = keep("slot_e", [P, T], i32)
    slot_v = keep("slot_v", [P, T], i32)
    reduced = keep("reduced", [P, T])
    slot_s = keep("slot_s", [P, T], i32)
    slot_d = keep("slot_d", [P, T], i32)
    pads = keep("pads", [P, J])
    xl = [keep(f"xl{n}", [P, J, C]) for n in range(4)]

    with ExitStack() as ctx:
        def tile(name, shape, dt=f32):
            return ctx.enter_context(nc.sbuf_tensor(name, shape, dt))

        nxt = tile("nxt", [P, T], i32)
        tmp = tile("tmp", [P, T])
        tmp2 = tile("tmp2", [P, T])
        brow = {n: tile(f"brow_{n}", [1, C]) for n in ("l1", "l3")}
        rest = tile("rest", [1, HALF * C])
        piece = {n: tile(f"piece_{n}", [1, 3, HALF * C], bf16) for n in ("l1", "l3")}
        zero = tile("zero", [P, J * CW])
        ea2 = tile("ea2", [P, T, 2])
        loaded = sem_of(ctx, "c_loaded")
        dve = sem_of(ctx, "c_dve_step")
        idn = sem_of(ctx, "c_ident")
        moved = sem_of(ctx, "c_bias_moved")
        zeroed = sem_of(ctx, "c_back_zeroed")
        zset = sem_of(ctx, "c_zero_set")
        block = ctx.enter_context(nc.Block())
        loads = [(W["gea"][:, :], w_gea), (W["lin0"][:, :], w_lin0_t), (W["lin0_rows"][:, :], w_lin0),
                 (W["lin1"][:, :], w_lin1), (W["res1"][:, :], w_res1), (W["self2"][:, :], w_self2),
                 (W["fwd2"][:, :], w_fwd2), (W["bwd2"][:, :], w_bwd2), (W["l3"][:, :], w_l3),
                 (W["r3"][:, :], w_r3), (gam_col[:, :], gamma), (bet_col[:, :], beta),
                 (src_i[:, :], src_pt), (dst_i[:, :], dst_pt), (prev_i[:, :], dst_prev_pt),
                 (nxt[:, :], dst_next_pt), (ea2[:, :, :], edge_attr2_pt), (brow["l1"][:, :], bias1), (brow["l3"][:, :], b_l3)]
        NBACK = back.shape[0] // P

        @block.sync
        def _(sp):
            for to, of in loads:
                sp.dma_start(to, of).then_inc(loaded, 16)
            sp.wait_ge(dve, 1)
            share = back.rearrange("(p r) c -> p (r c)", p=P)
            with sp.Fori(0, NBACK // J) as i:
                sp.dma_start(share[:, bass.ds(i * (J * CW), J * CW)], zero[:, :]).then_inc(zeroed, 16)
            left = NBACK % J
            if left:
                sp.dma_start(share[:, NBACK // J * J * CW:NBACK * CW], zero[:, 0:left * CW]).then_inc(zeroed, 16)
            sp.wait_ge(zeroed, 16 * (NBACK // J + bool(left)))

        @block.gpsimd
        def _(pool):
            GP.memset(ident[:, :], 0.0).then_inc(idn, 1)
            pool.wait_ge(idn, 1)
            GP.affine_select(out=ident[:, :], in_=ident[:, :], compare_op=ALU.not_equal, fill=1.0, base=0,
                             pattern=[[-1, 128]], channel_multiplier=1).then_inc(idn, 1)
            GP.iota(slot_v[:, :], [[P, T]], base=E, channel_multiplier=1).then_inc(idn, 1)
            GP.iota(slot_e[:, :], [[P, T]], base=0, channel_multiplier=1).then_inc(idn, 1)
            GP.iota(pads[:, :], [[0, J]], base=2 * E, channel_multiplier=1,
                    allow_small_or_imprecise_dtypes=True).then_inc(idn, 1)

        @block.vector
        def _(v):
            n = [0]

            def step(ins):
                n[0] += 1
                ins.then_inc(dve, 1)
                v.wait_ge(dve, n[0])

            step(DV.memset(zero[:, :], 0.0))
            DV.memset(ones3[:, :], 1.0)
            DV.memset(eps_col[:, :], LN_EPS)
            for b in xl:
                DV.memset(b[:, :, :], 0.0)
            v.wait_ge(loaded, 16 * len(loads))
            step(DV.tensor_tensor(W["sum1"][:, :], W["lin1"][:, :], W["res1"][:, :], ALU.add))
            step(DV.tensor_tensor(leads[:, :], dst_i[:, :], nxt[:, :], ALU.not_equal))
            step(DV.tensor_scalar(tmp[:, :], leads[:, :], -float(N), float(N), ALU.mult, ALU.add))
            step(DV.tensor_tensor(lead_i[:, :], tmp[:, :], dst_i[:, :], ALU.add))
            step(DV.scalar_tensor_tensor(out=reduced[:, :], in0=ea2[:, :, 1], scalar=0.35, in1=ea2[:, :, 0],
                                         op0=ALU.mult, op1=ALU.add))
            for name in ("l1", "l3"):
                for r in range(HALF):
                    step(DV.tensor_copy(rest[:, r * C:(r + 1) * C], brow[name][:, :]))
                for q in range(3):
                    step(DV.tensor_copy(piece[name][:, q, :], rest[:, :]))
                    step(DV.tensor_tensor(rest[:, :], rest[:, :], piece[name][:, q, :], ALU.subtract))
            v.sem_inc(zset, 1)

        @block.scalar
        def _(a):
            a.wait_ge(zset, 1)
            for name in ("l1", "l3"):
                for q in range(3):
                    a.dma_start(bias3[name][q:q + 1, :], piece[name][:, q, :]).then_inc(moved, 16)
            a.wait_ge(moved, 16 * 6)

    class Stage:

        def __init__(self, ctx, tag, units, when=None, gram_bank=None, banks=4):
            self.plan = Plan(units)
            self.u = units
            self.gram_bank = gram_bank
            self.when = when or list(range(len(units)))
            self.steps = max(self.when) + 4
            self.banks = banks
            t = lambda n, s, d=f32: ctx.enter_context(nc.sbuf_tensor(f"{tag}_{n}", s, d))
            p = lambda n: ctx.enter_context(nc.psum_tensor(f"{tag}_{n}", [128, 512], f32))
            s = lambda n: sem_of(ctx, f"{tag}_{n}")
            self.tile, self.sem, self.bank = t, s, p
            self.h = [t(f"h{n}", [P, J, CW]) for n in range(2)]
            self.hT = [t(f"hT{n}", [C, B]) for n in range(2)]
            self.st = [t(f"st{n}", [P, J, 6]) for n in range(2)]
            self.sm = [t(f"sm{n}", [P, 6, J]) for n in range(2)]
            self.off = [t(f"off{n}", [P, J]) for n in range(2)]
            self.tp = [p(f"tp{n}") for n in range(2)]
            self.mm = [p(f"mm{n}") for n in range(banks)]
            self.s_step = s("dve_stats_step")
            self.s_stat = s("variance_ready")
            self.s_std = s("std_ready")
            self.s_rec = s("inverse_std_ready")
            self.s_coef = s("scale_shift_ready")
            self.s_norm = s("h_half_ready")
            self.s_tps = s("h_read_by_pe")
            self.s_hT = s("hT_half_ready")
            self.s_mm = s("part_ready")
            self.s_done = {"D": s("part_taken_by_dve"), "A": s("part_taken_by_act")}
            self.s_xh = s("x_plus_h_ready")

        def stats(self, v, i, k):
            st, sm, x, n = self.st[k % 2], self.sm[k % 2], self.u[k].x, self.plan.n
            base = i * (3 * n) + 3 * k
            b = self.plan.before(k)
            v.wait_ge(self.s_norm, i * (2 * n) + (2 * b + 2 if b is not None else 0))
            if self.u[k].ready:
                self.u[k].ready(v, i)
            for j in range(J):
                last = DV.bn_stats(st[:, j, :], x[:, j, :])
            last.then_inc(self.s_step, 1)
            v.wait_ge(self.s_step, base + 1)
            DV.tensor_tensor(sm[:, 0, :], st[:, :, 1], st[:, :, 4], ALU.add)
            DV.tensor_tensor(sm[:, 2, :], st[:, :, 2], st[:, :, 5], ALU.add)
            DV.tensor_tensor(sm[:, 1, :], st[:, :, 1], st[:, :, 4], ALU.subtract).then_inc(self.s_step, 1)
            v.wait_ge(self.s_step, base + 2)
            DV.tensor_tensor(sm[:, 1, :], sm[:, 1, :], sm[:, 1, :], ALU.mult).then_inc(self.s_step, 1)
            v.wait_ge(self.s_step, base + 3)
            DV.scalar_tensor_tensor(out=sm[:, 3, :], in0=sm[:, 1, :], scalar=C / 4, in1=sm[:, 2, :],
                                    op0=ALU.mult, op1=ALU.add).then_inc(self.s_stat, 1)

        def std(self, a, i, k):
            sm = self.sm[k % 2]
            a.wait_ge(self.s_stat, i * self.plan.n + k + 1)
            AC.activation(sm[:, 4, :], sm[:, 3, :], ACT.Sqrt, scale=1.0 / C, bias=eps_col[0:P, :]).then_inc(self.s_std, 1)

        def coef(self, v, i, k):
            sm, n = self.sm[k % 2], self.plan.n
            v.wait_ge(self.s_std, i * n + k + 1)
            DV.reciprocal(sm[:, 5, :], sm[:, 4, :]).then_inc(self.s_rec, 1)
            v.wait_ge(self.s_rec, i * n + k + 1)
            DV.scalar_tensor_tensor(out=self.off[k % 2][:, :], in0=sm[:, 0, :], scalar=-0.5, in1=sm[:, 5, :],
                                    op0=ALU.mult, op1=ALU.mult).then_inc(self.s_coef, 1)

        def norm(self, a, i, k):
            pl, h = self.plan, self.h[k % 2]
            b = pl.before(k)
            a.wait_ge(self.s_coef, i * pl.n + k + 1)
            a.wait_ge(self.s_tps, i * (2 * pl.n) + (2 * b + 2 if b is not None else 0))
            if pl.adders:
                a.wait_ge(self.s_xh, i * pl.adders + (pl.added(b) if b is not None else 0))
            for j in range(J):
                ins = AC.activation(h[:, j, 0:C], self.u[k].x[:, j, :], ACT.Relu,
                                    scale=self.sm[k % 2][:, 5, j:j + 1], bias=self.off[k % 2][:, j:j + 1])
                if j % HALF == HALF - 1:
                    ins.then_inc(self.s_norm, 1)

        def turn(self, pe, i, k):
            pl, u, h = self.plan, self.u[k], self.h[k % 2]
            for half in range(2):
                pe.wait_ge(self.s_norm, i * (2 * pl.n) + 2 * k + half + 1)
                if u.gram:
                    for j in range(half * HALF, half * HALF + HALF):
                        ins = PE_.matmul(self.gram_bank[:, 0:CW], h[:, j, 0:C], h[:, j, :], start=False, stop=False)
                else:
                    m = pl.turned(k)
                    pe.wait_ge(self.s_hT, i * (2 * len(pl.plain)) + (2 * m - 1 + half if m else 0))
                    for j in range(HALF):
                        ins = PE_.transpose(self.tp[half][:, j * P:(j + 1) * P], h[:, half * HALF + j, 0:C],
                                            ident[0:P, 0:P])
                ins.then_inc(self.s_tps, 1)

        def take_turned(self, a, i, k):
            pl, hT = self.plan, self.hT[k % 2]
            if self.u[k].gram:
                return
            b = pl.before(k)
            done = i * pl.parts + (sum(p[0] <= b for p in pl.part) if b is not None else 0)
            for half in range(2):
                a.wait_ge(self.s_tps, i * (2 * pl.n) + 2 * k + half + 1)
                a.wait_ge(self.s_mm, done)
                AC.activation(hT[:, half * HALF * P:(half + 1) * HALF * P], self.tp[half][:, 0:HALF * P],
                              ACT.Copy).then_inc(self.s_hT, 1)

        def multiply(self, pe, i, k):
            pl, u, hT = self.plan, self.u[k], self.hT[k % 2]
            for half in range(2 if u.parts else 0):
                pe.wait_ge(self.s_hT, i * (2 * len(pl.plain)) + 2 * pl.turned(k) + half + 1)
                for q, (w, bias, _) in enumerate(u.parts):
                    n = pl.index(k, half, q)
                    if n >= self.banks:
                        c = pl.part[n - self.banks][3]
                        pe.wait_ge(self.s_done[c], i * pl.by[c] + pl.consumed(n - self.banks, c))
                    else:
                        for c in "DA":
                            if pl.by[c]:
                                pe.wait_ge(self.s_done[c], i * pl.by[c])
                    bank = self.mm[n % self.banks]
                    if bias is not None:
                        PE_.matmul(bank[0:P, :], ones3[:, :], bias[:, :], start=True, stop=False)
                    for j in range(HALF):
                        at = (half * HALF + j) * P
                        ins = PE_.matmul(bank[0:P, j * C:(j + 1) * C], hT[:, at:at + P], W[w][:, :],
                                         start=bias is None, stop=True if bias is None else j == HALF - 1)
                    ins.then_inc(self.s_mm, 1)

        def part(self, eng, i, k, half, q):
            n = self.plan.index(k, half, q)
            eng.wait_ge(self.s_mm, i * self.plan.parts + n + 1)
            return self.mm[n % self.banks][0:P, :].rearrange("p (j c) -> p j c", c=C)

        def at(self, step):
            return [k for k, w in enumerate(self.when) if w == step]

        def vector(self, v, i, ends, extra={}):
            for s in range(self.steps):
                for k in self.at(s):
                    self.stats(v, i, k)
                for k in self.at(s - 1):
                    self.coef(v, i, k)
                for k in self.at(s - 3):
                    ends[k](v, i)
                for do in extra.get(s, ()):
                    do(v, i)

        def scalar(self, a, i, ends={}, extra={}):
            for s in range(self.steps):
                for k in self.at(s):
                    self.std(a, i, k)
                for k in self.at(s - 1):
                    self.norm(a, i, k)
                for k in self.at(s - 2):
                    self.take_turned(a, i, k)
                for k in self.at(s - 3):
                    if k in ends:
                        ends[k](a, i)
                for do in extra.get(s, ()):
                    do(a, i)

        def tensor(self, pe, i, extra={}):
            for s in range(self.steps):
                for k in self.at(s - 1):
                    self.turn(pe, i, k)
                for k in self.at(s - 2):
                    self.multiply(pe, i, k)
                for do in extra.get(s, ()):
                    do(pe, i)

        def copy_part(self, a, i, k, q, to):
            for half in range(2):
                bank = self.part(a, i, k, half, q)
                AC.activation(to[:, half * HALF:(half + 1) * HALF, :], bank, ACT.Copy).then_inc(self.s_done["A"], 1)

    def halves(b, half):
        return b[:, half * HALF:(half + 1) * HALF, :]

    class Tick:

        def __init__(self, x0, final, s_x0, s_stored):
            self.x0, self.final, self.s_x0, self.s_stored = x0, final, s_x0, s_stored

            def from_layer(layer):
                def ready(v, i):
                    s, writer = self.stage, self.writer[layer]
                    if writer is None:
                        v.wait_ge(s.s_done["D"], i * s.plan.by["D"])
                    else:
                        n = s.plan.index(writer, 1, 0)
                        v.wait_ge(s.s_done["D"], i * s.plan.by["D"] + s.plan.consumed(n, "D"))
                return ready

            def loaded(v, i):
                v.wait_ge(self.s_x0, i * 32 + 32)
            self.units = [Unit("l3", xl[3], [("r3", bias3["l3"], "D")], ready=from_layer(3)),
                          Unit("l2", xl[2], [("self2", None, "D")], ready=from_layer(2)),
                          Unit("l1", xl[1], [("sum1", bias3["l1"], "D")], ready=from_layer(1)),
                          Unit("l0", x0, [("bn0", bias3["bn0"], "D")], adds=True, ready=loaded)]

        def place(self, stage, at, before=None):
            self.stage, self.k = stage, dict(zip((3, 2, 1, 0), at))
            self.writer = {n: before and before.k[n - 1] for n in (1, 2, 3)}

        def ends(self):
            return {self.k[n]: (lambda v, i, n=n: self.end(v, i, n)) for n in range(4)}

        def end(self, v, i, layer):
            s, k = self.stage, self.k[layer]
            if layer < 3:
                n = s.plan.index(self.k[layer + 1], 1, 0)
                v.wait_ge(s.s_done["D"], i * s.plan.by["D"] + s.plan.consumed(n, "D"))
            if layer == 3:
                if self.s_stored is not None:
                    v.wait_ge(self.s_stored, i * 32)
            if layer == 0:
                v.wait_ge(s.s_norm, i * (2 * s.plan.n) + 2 * k + 2)
                DV.tensor_tensor(xl[1][:, :, :], self.x0[:, :, :], s.h[k % 2][:, :, 0:C], ALU.add).then_inc(s.s_xh, 1)
                v.wait_ge(s.s_xh, i * s.plan.adders + s.plan.added(k))
            for half in range(2):
                ps = s.part(v, i, k, half, 0)
                if layer == 0:
                    ins = DV.scalar_tensor_tensor(out=halves(xl[1], half), in0=ps, scalar=0.0, in1=halves(xl[1], half),
                                                  op0=ALU.max, op1=ALU.add)
                elif layer == 2:
                    ins = DV.scalar_tensor_tensor(out=halves(xl[3], half), in0=ps, scalar=0.0, in1=halves(xl[2], half),
                                                  op0=ALU.max, op1=ALU.add)
                else:
                    to = xl[2] if layer == 1 else self.final
                    ins = DV.tensor_tensor(halves(to, half), ps, halves(xl[layer], half), ALU.add)
                ins.then_inc(s.s_done["D"], 1)

        def load(self, sp, i, per=1, first=0):
            s = self.stage
            sp.wait_ge(s.s_xh, i * s.plan.adders)
            split_load(sp, self.x0, x[bass.ds(i * (per * B) + first * B, B), :].rearrange("(p j) c -> p j c", j=J),
                       self.s_x0)

        def store(self, sp, i, per=1, first=0):
            s, k = self.stage, self.k[3]
            sp.wait_ge(s.s_done["D"], i * s.plan.by["D"] + s.plan.consumed(s.plan.index(k, 1, 0), "D"))
            split_load(sp, out[bass.ds(i * (per * B) + first * B, B), :].rearrange("(p j) c -> p j c", j=J), self.final, self.s_stored)

    def wait_sw(pool, sem, value):
        pool.wait_ge(sem, value)
        pool.sem_inc(pool_passed, 1)

    def wait_sp(sp, sem, value):
        sp.wait_ge(sem, value)
        sp.sem_inc(sp_passed, 1)

    def gather(to, table, index):
        return GP.indirect_dma_start(out=to, out_offset=None, in_=table,
                                     in_offset=bass.IndirectOffsetOnAxis(ap=index, axis=0))

    def scatter(table, index, of, limit):
        return GP.indirect_dma_start(out=table, out_offset=bass.IndirectOffsetOnAxis(ap=index, axis=0), in_=of,
                                     in_offset=None, bounds_check=limit, oob_is_err=False)

    def bcast_row(t, i, n):
        return t[:, bass.ds(i * B, B)].to_broadcast([n, B])

    class Chain:

        def __init__(self, sem, steps):
            self.sem, self.steps, self.n = sem, steps, 0

        def step(self, eng, i, ins):
            self.n += 1
            assert self.n <= self.steps
            ins.then_inc(self.sem, 1)
            eng.wait_ge(self.sem, i * self.steps + self.n)

        def close(self):
            assert self.n == self.steps, self.n

    with ExitStack() as ctx:
        tile = lambda n, s, d=f32: ctx.enter_context(nc.sbuf_tensor("A_" + n, s, d))
        xu, xv = tile("xu", [P, J, C]), tile("xv", [P, J, C])
        xg = [tile(f"xg{n}", [P, J, C]) for n in range(4)]
        gram_bank = ctx.enter_context(nc.psum_tensor("A_gram", [128, 512], f32))
        t_bank = ctx.enter_context(nc.psum_tensor("A_T", [128, 512], f32))
        s_u, s_v = sem_of(ctx, "A_src_rows"), sem_of(ctx, "A_dst_rows")
        s_xg = [sem_of(ctx, f"A_x_block{n}") for n in range(4)]
        units = [Unit("U", xu, [("gea", None, "D"), ("lin0", None, "A")], adds=True,
                      ready=lambda v, i: v.wait_ge(s_u, i * (16 * J) + 16 * J)),
                 Unit("V", xv, [("lin0", None, "A")], adds=True,
                      ready=lambda v, i: v.wait_ge(s_v, i * (16 * J) + 16 * J))]
        units += [Unit(f"g{n}", xg[n], gram=True, ready=lambda v, i, n=n: v.wait_ge(s_xg[n], i * 32 + 32))
                  for n in range(4)]
        st = Stage(ctx, "A", units, gram_bank=gram_bank)
        pl = st.plan
        gate = tile("gate", [P, J, C])
        V = tile("V", [P, J, 2 * C])
        Tr = tile("Tr", [P, J, 2 * C])
        S = tile("S", [P, J, P])
        M = tile("M", [P, J, P])
        junk = tile("junk", [P, J, P])
        upper = tile("upper", [P, P])
        drow, srow = tile("drow", [P, B], i32), tile("srow", [P, B], i32)
        a0b = {k: tile("a0" + k, [P, J, C]) for k in "DS"}
        yb = {k: tile("y0" + k, [P, J, C]) for k in "DS"}
        agg = tile("agg", [P, J, C])
        cor = tile("cor", [P, J, C])
        hh = tile("hh", [P, J, C])
        none = tile("none", [P, CW + 2])
        d8, p8 = tile("d8", [P, J], i32), tile("p8", [P, J], i32)
        s8, l8 = tile("s8", [P, J], i32), tile("l8", [P, J])
        later = tile("later", [P, J])
        src8, dst8 = tile("src8", [P, J], i32), tile("dst8", [P, J], i32)
        once8, slot8 = tile("once8", [P, J], i32), tile("slot8", [P, J], i32)
        s_upper, s_set = sem_of(ctx, "A_upper_set"), sem_of(ctx, "A_constants_set")
        s_gl, s_dr, s_sr = sem_of(ctx, "A_gate_loaded"), sem_of(ctx, "A_dst_row"), sem_of(ctx, "A_src_row")
        s_gate = sem_of(ctx, "A_gate_ready")
        s_col = sem_of(ctx, "A_columns_ready")
        s_col2 = sem_of(ctx, "A_again_ready")
        s_eq = sem_of(ctx, "A_equalities_ready")
        s_once, s_cnt = sem_of(ctx, "A_once_ready"), sem_of(ctx, "A_later_counted")
        s_T, s_Tr = sem_of(ctx, "A_sum_in_psum"), sem_of(ctx, "A_sum_kept")
        s_ag, s_cr, s_crd = sem_of(ctx, "A_end_step"), sem_of(ctx, "A_correction_ready"), sem_of(ctx, "A_correction_read")
        s_sta = {k: sem_of(ctx, "A_stored_x_plus_h_" + k) for k in "DS"}
        s_sty = {k: sem_of(ctx, "A_stored_y_" + k) for k in "DS"}
        s_cols, s_map = sem_of(ctx, "A_pool_columns"), sem_of(ctx, "A_slot_named")
        s_gram = sem_of(ctx, "A_gram_done")
        s_first = sem_of(ctx, "A_pool_first")
        block = ctx.enter_context(nc.Block())

        @block.gpsimd
        def _(pool):
            GP.memset(upper[:, :], 1.0).then_inc(s_upper, 1)
            pool.wait_ge(s_upper, 1)
            GP.affine_select(out=upper[:, :], in_=upper[:, :], compare_op=ALU.is_gt, fill=0.0, base=0,
                             pattern=[[1, P]], channel_multiplier=-1).then_inc(s_upper, 1)
            pool.dma_start(slot_of[N:N + 1, :], slot_v[0:1, 0:1]).then_inc(s_first, 16)

            def fetch(i, u, v, m):
                if u is not None:
                    pool.wait_ge(st.s_norm, i * (2 * pl.n))
                    pool.wait_ge(st.s_xh, i * pl.adders)
                    pool.wait_ge(s_u, i * (16 * J))
                    pool.wait_ge(s_v, i * (16 * J))
                    GP.tensor_copy(src8[:, :], src_i[:, bass.ds(i * J, J)]).then_inc(s_cols, 1)
                    GP.tensor_copy(dst8[:, :], dst_i[:, bass.ds(i * J, J)]).then_inc(s_cols, 1)
                if m is not None:
                    pool.wait_ge(s_once, m + 1)
                    pool.wait_ge(s_map, m * (16 * J))
                    GP.tensor_copy(once8[:, :], once_i[:, bass.ds(m * J, J)]).then_inc(s_cols, 1)
                    GP.tensor_copy(slot8[:, :], slot_v[:, bass.ds(m * J, J)]).then_inc(s_cols, 1)
                    wait_sw(pool, s_cols, m * 4 + (6 if u is not None else 4))
                elif u is not None:
                    wait_sw(pool, s_cols, 2)
                for j in range(J):
                    if u is not None:
                        gather(xu[:, j, :], x[:, :], src8[:, j:j + 1]).then_inc(s_u, 16)
                        gather(xv[:, j, :], x[:, :], dst8[:, j:j + 1]).then_inc(s_v, 16)
                    if m is not None:
                        wait_sw(pool, s_map, m * (16 * J) + 16 * j)
                        scatter(slot_of[:, :], once8[:, j:j + 1], slot8[:, j:j + 1], N - 1).then_inc(s_map, 16)
            fetch(0, 0, 0, None)
            with pool.Fori(1, EIT) as i:
                fetch(i, i, i, i - 1)
            fetch(EIT - 1, None, None, EIT - 1)
            pool.wait_ge(s_map, 16 * T)

        @block.sync
        def _(sp):
            def loads(i):
                sp.wait_ge(s_gate, i)
                split_load(sp, gate, rows(edge_attr, i), s_gl)
                sp.wait_ge(s_eq, i * 2)
                wait_sp(sp, s_cnt, i)
                sp.dma_start(drow[:, :], bcast_row(dst_row, i, P)).then_inc(s_dr, 16)
                sp.dma_start(srow[:, :], bcast_row(src_row, i, P)).then_inc(s_sr, 16)
                for n in range(4):
                    sp.wait_ge(st.s_norm, i * (2 * pl.n))
                    split_load(sp, xg[n], x[bass.ds(i * (4 * B) + n * B, B), :].rearrange("(p j) c -> p j c", j=J),
                               s_xg[n])

            def stores(i):
                sp.wait_ge(st.s_xh, i * 2 + 2)
                split_load(sp, own(a0["S"], i), a0b["S"], s_sta["S"])
                split_load(sp, own(a0["D"], i), a0b["D"], s_sta["D"])
                sp.wait_ge(st.s_done["A"], i * pl.by["A"] + 4)
                split_load(sp, own(y0["S"], i), yb["S"], s_sty["S"])
                sp.wait_ge(s_ag, i * 6 + 5)
                split_load(sp, own(y0["D"], i), hh, s_sty["D"])
            loads(0)
            with sp.Fori(1, EIT) as i:
                loads(i)
                stores(i - 1)
            stores(EIT - 1)
            for k in "DS":
                sp.wait_ge(s_sta[k], 32 * EIT)
                sp.wait_ge(s_sty[k], 32 * EIT)

        @block.vector
        def _(v):
            DV.memset(none[:, :], 0.0)
            DV.memset(Tr[:, :, :], 0.0)
            for n in range(2):
                last = DV.memset(st.h[n][:, :, C:CW], 1.0)
            last.then_inc(s_set, 1)
            v.wait_ge(s_upper, 2)

            def columns(v, i):
                v.wait_ge(s_T, i * J)
                v.wait_ge(s_crd, i * (2 * J))
                DV.tensor_copy(d8[:, :], dst_i[:, bass.ds(i * J, J)])
                DV.tensor_copy(p8[:, :], prev_i[:, bass.ds(i * J, J)])
                DV.tensor_copy(l8[:, :], leads[:, bass.ds(i * J, J)])
                DV.tensor_copy(s8[:, :], src_i[:, bass.ds(i * J, J)]).then_inc(s_col, 1)
                v.wait_ge(s_col, i + 1)
                v.wait_ge(s_dr, i * 16 + 16)
                for j in range(J):
                    ins = DV.tensor_scalar(S[:, j, :], drow[:, j * P:(j + 1) * P], d8[:, j:j + 1], None, ALU.is_equal)
                ins.then_inc(s_eq, 1)

            def previous(v, i):
                for j in range(J):
                    ins = DV.tensor_scalar(M[:, j, :], drow[:, j * P:(j + 1) * P], p8[:, j:j + 1], None, ALU.is_equal)
                ins.then_inc(s_eq, 1)

            def repeats(v, i):
                v.wait_ge(s_sr, i * 16 + 16)
                for j in range(J):
                    ins = DV.scalar_tensor_tensor(out=junk[:, j, :], in0=srow[:, j * P:(j + 1) * P], scalar=s8[:, j:j + 1],
                                                  in1=upper[:, :], op0=ALU.is_equal, op1=ALU.mult,
                                                  accum_out=later[:, j:j + 1])
                ins.then_inc(s_cnt, 1)
                v.wait_ge(s_cnt, i + 1)
                DV.tensor_scalar(again[:, bass.ds(i * J, J)], later[:, :], 1.0, None, ALU.min).then_inc(s_col2, 1)
                v.wait_ge(s_col2, i + 1)
                DV.scalar_tensor_tensor(out=once_i[:, bass.ds(i * J, J)], in0=again[:, bass.ds(i * J, J)],
                                        scalar=float(N), in1=s8[:, :], op0=ALU.mult, op1=ALU.add).then_inc(s_once, 1)

            def add_h(v, i, k, to, x_, s_stored):
                v.wait_ge(s_stored, i * 32)
                v.wait_ge(st.s_norm, i * (2 * pl.n) + 2 * k + 2)
                DV.tensor_tensor(to[:, :, :], x_[:, :, :], st.h[k % 2][:, :, 0:C], ALU.add).then_inc(st.s_xh, 1)

            def end_u(v, i):
                add_h(v, i, 0, a0b["S"], xu, s_sta["S"])
                v.wait_ge(s_gate, i + 1)
                for half in range(2):
                    ps = st.part(v, i, 0, half, 0)
                    sl = slice(half * HALF, half * HALF + HALF)
                    DV.tensor_tensor(V[:, sl, C:2 * C], ps, V[:, sl, 0:C], ALU.mult).then_inc(st.s_done["D"], 1)

            def end_v(v, i):
                add_h(v, i, 1, a0b["D"], xv, s_sta["D"])

            def keep_sums(j0):
                def do(v, i):
                    for j in (j0, j0 + 1):
                        v.wait_ge(s_T, i * J + j + 1)
                        DV.tensor_copy(Tr[:, j, :], t_bank[0:P, 0:2 * C]).then_inc(s_Tr, 1)
                return do

            def finish(v, i):
                v.wait_ge(s_Tr, i * J + J)
                v.wait_ge(s_sty["D"], i * 32)
                DV.tensor_scalar(agg[:, :, :], Tr[:, :, 0:C], GATE_EPS, None, ALU.add).then_inc(s_ag, 1)
                v.wait_ge(s_ag, i * 6 + 1)
                DV.reciprocal(agg[:, :, :], agg[:, :, :]).then_inc(s_ag, 1)
                v.wait_ge(s_ag, i * 6 + 2)
                DV.tensor_tensor(agg[:, :, :], agg[:, :, :], Tr[:, :, C:2 * C], ALU.mult).then_inc(s_ag, 1)
                v.wait_ge(s_ag, i * 6 + 3)
                v.wait_ge(st.s_done["A"], i * pl.by["A"] + 4)
                DV.tensor_tensor(hh[:, :, :], agg[:, :, :], yb["D"][:, :, :], ALU.add).then_inc(s_ag, 2)
                v.wait_ge(s_ag, i * 6 + 5)
                DV.tensor_tensor(cor[:, :, :], hh[:, :, :], yb["D"][:, :, :], ALU.add).then_inc(s_ag, 1)
                v.wait_ge(s_ag, i * 6 + 6)
                DV.tensor_tensor(cor[:, :, :], cor[:, :, :], agg[:, :, :], ALU.mult).then_inc(s_cr, 1)
            ends = {0: end_u, 1: end_v, 2: lambda v, i: None, 3: lambda v, i: None, 4: lambda v, i: None,
                    5: lambda v, i: None}
            extra = {0: [columns], 1: [previous], 2: [repeats], 5: [keep_sums(0)], 6: [keep_sums(2)],
                     7: [keep_sums(4)], 8: [keep_sums(6), finish]}
            with v.Fori(0, EIT) as i:
                st.vector(v, i, ends, extra)
            v.wait_ge(s_gram, 1)
            DV.tensor_copy(gram_sb[:, :], gram_bank[:, 0:CW + 2])

        @block.scalar
        def _(a):
            a.wait_ge(s_set, 1)

            def gates(a, i):
                a.wait_ge(s_gl, i * 32 + 32)
                a.wait_ge(s_T, i * J)
                AC.activation(V[:, :, 0:C], gate[:, :, :], ACT.Sigmoid).then_inc(s_gate, 1)

            def take_u(a, i):
                a.wait_ge(s_sty["S"], i * 32)
                st.copy_part(a, i, 0, 1, yb["S"])

            def take_v(a, i):
                a.wait_ge(s_cr, i)
                st.copy_part(a, i, 1, 0, yb["D"])
            with a.Fori(0, EIT) as i:
                gates(a, i)
                st.scalar(a, i, {0: take_u, 1: take_v})

        @block.tensor
        def _(pe):
            pe.wait_ge(s_set, 1)
            PE_.matmul(gram_bank[:, 0:CW + 2], none[:, 0:C], none[:, :], start=True, stop=False)

            def sums(j0):
                def do(pe, i):
                    for j in (j0, j0 + 1):
                        if j == 0:
                            pe.wait_ge(st.s_done["D"], i * pl.by["D"] + 2)
                            pe.wait_ge(s_eq, i * 2 + 2)
                        pe.wait_ge(s_Tr, i * J + j)
                        PE_.matmul(t_bank[0:P, 0:2 * C], S[:, j, :], V[:, j, :], start=True, stop=False)
                        PE_.matmul(t_bank[0:P, 0:2 * C], M[:, j, :], Tr[:, (j - 1) % J, :], start=False, stop=True)\
                            .then_inc(s_T, 1)
                return do

            def corrections(pe, i):
                pe.wait_ge(s_cr, i + 1)
                for j in range(J):
                    PE_.matmul(gram_bank[:, CW:CW + 1], agg[:, j, :], l8[:, j:j + 1], start=False, stop=False)\
                        .then_inc(s_crd, 1)
                    PE_.matmul(gram_bank[:, CW + 1:CW + 2], cor[:, j, :], l8[:, j:j + 1], start=False, stop=False)\
                        .then_inc(s_crd, 1)
            with pe.Fori(0, EIT) as i:
                st.tensor(pe, i, {4: [sums(0)], 5: [sums(2)], 6: [sums(4)], 7: [sums(6)], 8: [corrections]})
            PE_.matmul(gram_bank[:, 0:CW + 2], none[:, 0:C], none[:, :], start=False, stop=True).then_inc(s_gram, 1)

    clear_semaphores()

    with ExitStack() as ctx:
        tile = lambda n, s, d=f32: ctx.enter_context(nc.sbuf_tensor("N_" + n, s, d))
        bank = [ctx.enter_context(nc.psum_tensor(f"N_p{n}", [128, 512], f32)) for n in range(4)]
        col = tile("col", [C, 12])
        ws = tile("ws", [C, C])
        junk = tile("junk", [C, C])
        full = [tile(f"full{n}", [C, P]) for n in range(2)]
        rest = tile("rest", [1, HALF * C])
        piece = tile("piece", [1, 3, HALF * C], bf16)
        step_ = sem_of(ctx, "N_dve_step")
        s_mm, s_std, s_moved = sem_of(ctx, "N_matmul"), sem_of(ctx, "N_std"), sem_of(ctx, "N_bias_moved")
        s_full = sem_of(ctx, "N_scaled")
        s_piece = sem_of(ctx, "N_pieces")
        block = ctx.enter_context(nc.Block())

        VAR_STEP = 7

        @block.tensor
        def _(pe):
            PE_.matmul(bank[0][:, 0:1], W["lin0"][:, :], gram_sb[:, C:C + 1], start=True, stop=True)
            PE_.matmul(bank[1][:, 0:C], W["lin0"][:, :], gram_sb[:, 0:C], start=True, stop=True).then_inc(s_mm, 1)
            pe.wait_ge(s_full, 1)
            PE_.transpose(bank[2][:, 0:C], ws[:, :], ident[:, :])
            PE_.matmul(bank[3][0:P, 0:C], full[0][:, :], ident[:, :], start=True, stop=True)
            PE_.matmul(bank[3][0:P, C:2 * C], full[1][:, :], ident[:, :], start=True, stop=True).then_inc(s_mm, 1)

        @block.scalar
        def _(a):
            a.wait_ge(step_, VAR_STEP)
            AC.activation(col[:, 5:6], col[:, 4:5], ACT.Sqrt, bias=col[:, 11:12]).then_inc(s_std, 1)
            a.wait_ge(s_piece, 1)
            for q in range(3):
                a.dma_start(bias3["bn0"][q:q + 1, :], piece[:, q, :]).then_inc(s_moved, 16)
            a.wait_ge(s_moved, 48)

        @block.vector
        def _(v):
            n = [0]

            def step(ins):
                n[0] += 1
                ins.then_inc(step_, 1)
                v.wait_ge(step_, n[0])

            v.wait_ge(s_mm, 1)
            step(DV.memset(col[:, 11:12], BN_EPS))
            step(DV.tensor_tensor(col[:, 0:1], bank[0][:, 0:1], gram_sb[:, CW:CW + 1], ALU.add))
            step(DV.scalar_tensor_tensor(out=junk[:, :], in0=bank[1][:, 0:C], scalar=1.0, in1=W["lin0_rows"][:, :],
                                         op0=ALU.mult, op1=ALU.mult, accum_out=col[:, 1:2]))
            step(DV.tensor_tensor(col[:, 1:2], col[:, 1:2], gram_sb[:, CW + 1:CW + 2], ALU.add))
            step(DV.tensor_scalar(col[:, 2:3], col[:, 0:1], 1.0 / N, None, ALU.mult))
            step(DV.tensor_tensor(col[:, 3:4], col[:, 2:3], col[:, 2:3], ALU.mult))
            step(DV.scalar_tensor_tensor(out=col[:, 4:5], in0=col[:, 1:2], scalar=1.0 / N, in1=col[:, 3:4],
                                         op0=ALU.mult, op1=ALU.subtract))
            assert n[0] == VAR_STEP
            v.wait_ge(s_std, 1)
            step(DV.reciprocal(col[:, 6:7], col[:, 5:6]))
            step(DV.tensor_tensor(col[:, 7:8], col[:, 6:7], gam_col[:, :], ALU.mult))
            step(DV.tensor_tensor(col[:, 8:9], col[:, 7:8], col[:, 2:3], ALU.mult))
            step(DV.tensor_tensor(col[:, 9:10], bet_col[:, :], col[:, 8:9], ALU.subtract))
            step(DV.tensor_scalar(ws[:, :], W["lin0_rows"][:, :], col[:, 7:8], None, ALU.mult))
            for q in range(2):
                step(DV.memset(full[q][:, :], 1.0))
                step(DV.tensor_scalar(full[q][:, :], full[q][:, :], col[:, 7 + 2 * q:8 + 2 * q], None, ALU.mult))
            v.sem_inc(s_full, 1)
            v.wait_ge(s_mm, 2)
            DV.tensor_copy(W["bn0"][:, :], bank[2][:, 0:C])
            DV.tensor_copy(bn_mul[:, :], bank[3][0:P, 0:C])
            step(DV.tensor_copy(bn_add[:, :], bank[3][0:P, C:2 * C]))
            for r in range(HALF):
                step(DV.tensor_copy(rest[:, r * C:(r + 1) * C], bn_add[0:1, :]))
            for q in range(3):
                step(DV.tensor_copy(piece[:, q, :], rest[:, :]))
                step(DV.tensor_tensor(rest[:, :], rest[:, :], piece[:, q, :], ALU.subtract))
            v.sem_inc(s_piece, 1)

    with ExitStack() as ctx:
        tile = lambda n, s, d=f32: ctx.enter_context(nc.sbuf_tensor("W_" + n, s, d))
        x0, final = tile("x0", [P, J, C]), tile("final", [P, J, C])
        s_x0 = sem_of(ctx, "W_x_block")
        tick = Tick(x0, final, s_x0, None)
        st = Stage(ctx, "W", tick.units)
        tick.place(st, range(4))
        block = ctx.enter_context(nc.Block())

        @block.sync
        def _(sp):
            with sp.Fori(0, 3) as i:
                tick.load(sp, i)

        @block.vector
        def _(v):
            with v.Fori(0, 3) as i:
                st.vector(v, i, tick.ends())

        @block.scalar
        def _(a):
            with a.Fori(0, 3) as i:
                st.scalar(a, i)

        @block.tensor
        def _(pe):
            with pe.Fori(0, 3) as i:
                st.tensor(pe, i)

    with ExitStack() as ctx:
        tile = lambda n, s, d=f32: ctx.enter_context(nc.sbuf_tensor("B_" + n, s, d))
        sem = lambda n: sem_of(ctx, "B_" + n)
        x0 = [tile(f"x0{n}", [P, J, C]) for n in range(2)]
        final = [tile(f"final{n}", [P, J, C]) for n in range(2)]
        s_x0 = [sem(f"x_block{n}") for n in range(2)]
        s_fin = [sem(f"out_stored{n}") for n in range(2)]
        a0b = {k: tile("a0" + k, [P, J, C]) for k in "DS"}
        yb = {k: tile("y0" + k, [P, J, C]) for k in "DS"}
        pj = {k: tile("proj" + k, [P, J, C]) for k in "DS"}
        res = tile("res", [P, J, C])
        x2s = tile("x2s", [P, J, C])
        part2 = [tile(f"part2{n}", [P, J, C]) for n in range(3)]
        lead8, slot8 = tile("lead8", [P, J], i32), tile("slot8", [P, J], i32)
        s_in = {k: sem("loaded_" + k) for k in "DS"}
        s_x1 = {k: sem("x1_ready_" + k) for k in "DS"}
        s_mul = sem("bn_step")
        s_pst = {k: sem("stored_proj_" + k) for k in "DS"}
        s_rst, s_xst = sem("stored_res"), sem("stored_x2")
        s_2st = [sem(f"stored_part2{n}") for n in range(3)]
        s_cols, s_map, s_first = sem("pool_columns"), sem("slot_named"), sem("pool_first")
        ticks = [Tick(x0[n], final[n], s_x0[n], s_fin[n]) for n in range(2)]
        a3, a2, a1, a0_ = ticks[0].units
        b3, b2, b1, b0 = ticks[1].units
        uD = Unit("D1", a0b["D"], [("lin1", None, "A"), ("res1", bias3["l1"], "D")],
                  ready=lambda v, i: v.wait_ge(s_x1["D"], i + 1))
        uS = Unit("S1", a0b["S"], [("lin1", None, "A"), ("sum1", bias3["l1"], "D")],
                  ready=lambda v, i: v.wait_ge(s_x1["S"], i + 1))
        uT = Unit("S2", x2s, [("self2", None, "A"), ("fwd2", None, "A"), ("bwd2", None, "A")],
                  ready=lambda v, i: v.wait_ge(st.s_done["D"], i * st.plan.by["D"]
                                               + st.plan.consumed(st.plan.index(1, 1, 1), "D")))
        st = Stage(ctx, "B", [a3, uS, a2, a1, a0_, uD, b3, b2, b1, uT, b0])
        kS, kD, kT = 1, 5, 9
        ticks[0].place(st, (0, 2, 3, 4))
        ticks[1].place(st, (6, 7, 8, 10), before=ticks[0])
        pl = st.plan
        block = ctx.enter_context(nc.Block())

        @block.gpsimd
        def _(pool):
            pool.dma_start(slot_of[N:N + 1, :], slot_v[0:1, 0:1]).then_inc(s_first, 16)
            pool.wait_ge(s_first, 16)
            with pool.Fori(0, EIT) as i:
                pool.wait_ge(s_map, i * (16 * J))
                GP.tensor_copy(lead8[:, :], lead_i[:, bass.ds(i * J, J)]).then_inc(s_cols, 1)
                GP.tensor_copy(slot8[:, :], slot_e[:, bass.ds(i * J, J)]).then_inc(s_cols, 1)
                wait_sw(pool, s_cols, i * 2 + 2)
                for j in range(J):
                    if j:
                        wait_sw(pool, s_map, i * (16 * J) + 16 * j)
                    scatter(slot_of[:, :], lead8[:, j:j + 1], slot8[:, j:j + 1], N - 1).then_inc(s_map, 16)
            pool.wait_ge(s_map, 16 * T)

        @block.sync
        def _(sp):
            def loads(i):
                for k in "SD":
                    wait_sp(sp, st.s_done["D"], i * pl.by["D"])
                    wait_sp(sp, st.s_norm, i * (2 * pl.n))
                    split_load(sp, a0b[k], own(a0[k], i), s_in[k])
                    split_load(sp, yb[k], own(y0[k], i), s_in[k])
                for n in range(2):
                    ticks[n].load(sp, i, 2, 3 + n)

            def stores(i):
                ticks[0].store(sp, i, 2)
                for k, unit in (("S", kS), ("D", kD)):
                    sp.wait_ge(st.s_done["A"], i * pl.by["A"] + pl.consumed(pl.index(unit, 1, 0), "A"))
                    split_load(sp, rows(proj1, i, E if k == "S" else 0), pj[k], s_pst[k])
                sp.wait_ge(st.s_done["D"], i * pl.by["D"] + pl.consumed(pl.index(kS, 1, 1), "D"))
                split_load(sp, own(x2t["S"], i), x2s, s_xst)
                sp.wait_ge(st.s_done["D"], i * pl.by["D"] + pl.consumed(pl.index(kD, 1, 1), "D"))
                split_load(sp, own(res1, i), res, s_rst)
                ticks[1].store(sp, i, 2, 1)
                for q, to in enumerate((own(self2["S"], i), rows(fwd2, i, E), rows(bwd2, i, E))):
                    sp.wait_ge(st.s_done["A"], i * pl.by["A"] + pl.consumed(pl.index(kT, 1, q), "A"))
                    split_load(sp, to, part2[q], s_2st[q])
            loads(0)
            with sp.Fori(1, EIT) as i:
                loads(i)
                stores(i - 1)
            stores(EIT - 1)
            for s_ in (s_fin[0], s_fin[1], s_pst["D"], s_pst["S"], s_rst, s_xst, *s_2st):
                sp.wait_ge(s_, 32 * EIT)

        @block.vector
        def _(v):
            def start(k, nk):
                def do(v, i):
                    v.wait_ge(s_in[k], i * 64 + 64)
                    mul = bn_mul[:, :].unsqueeze(1).to_broadcast([P, J, C])
                    add = bn_add[:, :].unsqueeze(1).to_broadcast([P, J, C])
                    DV.tensor_tensor(yb[k][:, :, :], yb[k][:, :, :], mul, ALU.mult).then_inc(s_mul, 1)
                    v.wait_ge(s_mul, i * 4 + 2 * nk + 1)
                    DV.tensor_tensor(yb[k][:, :, :], yb[k][:, :, :], add, ALU.add).then_inc(s_mul, 1)
                    v.wait_ge(s_mul, i * 4 + 2 * nk + 2)
                    DV.scalar_tensor_tensor(out=a0b[k][:, :, :], in0=yb[k][:, :, :], scalar=0.0, in1=a0b[k][:, :, :],
                                            op0=ALU.max, op1=ALU.add).then_inc(s_x1[k], 1)
                return do

            def end(k, unit, to, s_stored):
                def do(v, i):
                    v.wait_ge(s_stored, i * 32)
                    for half in range(2):
                        ps = st.part(v, i, unit, half, 1)
                        DV.tensor_tensor(halves(to, half), ps, halves(a0b[k], half), ALU.add)\
                            .then_inc(st.s_done["D"], 1)
                return do
            ends = {kS: end("S", kS, x2s, s_xst), kD: end("D", kD, res, s_rst), kT: lambda v, i: None,
                    **ticks[0].ends(), **ticks[1].ends()}
            with v.Fori(0, EIT) as i:
                st.vector(v, i, ends, {0: [start("S", 0)], 4: [start("D", 1)]})

        @block.scalar
        def _(a):
            def proj(k, unit):
                def do(a, i):
                    a.wait_ge(s_pst[k], i * 32)
                    st.copy_part(a, i, unit, 0, pj[k])
                return do

            def second(a, i):
                for half in range(2):
                    for q in range(3):
                        if half == 0:
                            a.wait_ge(s_2st[q], i * 32)
                        bank = st.part(a, i, kT, half, q)
                        AC.activation(halves(part2[q], half), bank, ACT.Copy).then_inc(st.s_done["A"], 1)
            with a.Fori(0, EIT) as i:
                st.scalar(a, i, {kS: proj("S", kS), kD: proj("D", kD), kT: second})

        @block.tensor
        def _(pe):
            with pe.Fori(0, EIT) as i:
                st.tensor(pe, i)

    clear_semaphores()

    with ExitStack() as ctx:
        tile = lambda n, s, d=f32: ctx.enter_context(nc.sbuf_tensor("C_" + n, s, d))
        sem = lambda n: sem_of(ctx, "C_" + n)
        psum = lambda n, w=512: ctx.enter_context(nc.psum_tensor("C_" + n, [128, w], f32))
        x0, final = tile("x0", [P, J, C]), tile("final", [P, J, C])
        s_x0, s_fin = sem("x_block"), sem("out_stored")
        pu, pv = tile("pu", [P, J, C]), tile("pv", [P, J, C])
        pv_kept = tile("pv_kept", [P, J, C])
        z, mixed = tile("z", [P, J, C]), tile("mixed", [P, J, C])
        CH = C + H
        V, Tr = tile("V", [P, J, CH]), tile("Tr", [P, J, CH])
        S, M = tile("S", [P, J, P]), tile("M", [P, J, P])
        drow, dprev = tile("drow", [P, B], i32), tile("dprev", [H, B], i32)
        apart = tile("apart", [H, B + 1])
        lgT, F, G = tile("lgT", [H, B]), tile("F", [H, B]), tile("G", [H, B])
        f_last, f_diff, f_diag = tile("f_last", [H, 1]), tile("f_diff", [H, 1]), tile("f_diag", [H, H])
        ones_h = tile("ones_h", [H, P])
        att_b, eb_b = tile("att_b", [P, C]), tile("eb_b", [P, H])
        lg, ls, ew, mf = (tile(n, [P, J, H]) for n in ("lg", "ls", "ew", "mf"))
        red8 = tile("red8", [P, J])
        JH = J * H
        arg, ex = tile("arg", [P, 3 * JH + H]), tile("ex", [P, 3 * JH + H])
        den, gd, ed = (tile(n, [P, J, H]) for n in ("den", "gd", "ed"))
        resb, x2b = tile("resb", [P, J, C]), tile("x2b", [P, J, C])
        part2 = [tile(f"part2{n}", [P, J, C]) for n in range(3)]
        d8, p8 = tile("d8", [P, J], i32), tile("p8", [P, J], i32)
        src8, dst8 = tile("src8", [P, J], i32), tile("dst8", [P, J], i32)
        ss8, sd8 = tile("ss8", [P, J], i32), tile("sd8", [P, J], i32)
        t_bank, r_bank = psum("T"), psum("R")
        l_bank = [psum("L0"), psum("L1")]
        s_con, s_con2, s_set = sem("att_loaded"), sem("eb_loaded"), sem("constants_set")
        s_pu, s_pv, s_slots, s_cols = sem("src_rows"), sem("dst_rows"), sem("slots_fetched"), sem("pool_columns")
        s_dr, s_rl = sem("index_rows"), sem("res_loaded")
        s_ch, s_lg, s_ls, s_kept = sem("dve_step"), sem("logits_ready"), sem("self_logits_ready"), sem("pv_kept")
        s_lT, s_lgT, s_G, s_R = sem("logits_turned"), sem("logits_row_ready"), sem("maximum_ready"), sem("maximum_turned")
        s_arg, s_ex, s_V, s_eq = sem("exponents_ready"), sem("exp_ready"), sem("values_ready"), sem("equalities_ready")
        s_T, s_Tr, s_x2 = sem("sum_in_psum"), sem("sum_kept"), sem("x2_ready")
        s_xst, s_2st = sem("stored_x2"), [sem(f"stored_part2{n}") for n in range(3)]
        tick = Tick(x0, final, s_x0, s_fin)
        uD = Unit("D2", x2b, [("self2", None, "A"), ("fwd2", None, "A"), ("bwd2", None, "A")],
                  ready=lambda v, i: v.wait_ge(s_x2, i + 1))
        st = Stage(ctx, "C", tick.units + [uD], when=[0, 2, 4, 5, 7], banks=2)
        kD = 4
        tick.place(st, range(4))
        pl = st.plan
        chain = Chain(s_ch, 20)
        block = ctx.enter_context(nc.Block())

        @block.gpsimd
        def _(pool):
            pool.wait_ge(s_con, 16)

            def fetch(i):
                pool.wait_ge(s_pu, i * (16 * J))
                pool.wait_ge(s_pv, i * (16 * J))
                pool.wait_ge(s_slots, i * (32 * J))
                GP.tensor_copy(src8[:, :], src_i[:, bass.ds(i * J, J)]).then_inc(s_cols, 1)
                GP.tensor_copy(dst8[:, :], dst_i[:, bass.ds(i * J, J)]).then_inc(s_cols, 1)
                wait_sw(pool, s_cols, i * 4 + 2)
                for j in range(J):
                    gather(ss8[:, j:j + 1], slot_of[:, :], src8[:, j:j + 1]).then_inc(s_slots, 16)
                    gather(sd8[:, j:j + 1], slot_of[:, :], dst8[:, j:j + 1]).then_inc(s_slots, 16)
                wait_sw(pool, s_slots, i * (32 * J) + 32 * J)
                GP.tensor_copy(slot_s[:, bass.ds(i * J, J)], ss8[:, :]).then_inc(s_cols, 1)
                GP.tensor_copy(slot_d[:, bass.ds(i * J, J)], sd8[:, :]).then_inc(s_cols, 1)
                pool.wait_ge(s_kept, i)
                wait_sw(pool, s_ls, i)
                for j in range(J):
                    gather(pv[:, j, :], proj1[:, :], sd8[:, j:j + 1]).then_inc(s_pv, 16)
                wait_sw(pool, s_V, i)
                for j in range(J):
                    gather(pu[:, j, :], proj1[:, :], ss8[:, j:j + 1]).then_inc(s_pu, 16)
            with pool.Fori(0, EIT) as i:
                fetch(i)
            pool.wait_ge(s_cols, 4 * EIT)

        @block.sync
        def _(sp):
            sp.dma_start(att_b[:, :], att.to_broadcast([P, C])).then_inc(s_con, 16)
            sp.dma_start(eb_b[:, :], w_eb.to_broadcast([P, H])).then_inc(s_con2, 16)

            def loads(i):
                sp.wait_ge(s_eq, i * 2)
                sp.dma_start(drow[:, :], bcast_row(dst_row, i, P)).then_inc(s_dr, 16)
                sp.dma_start(dprev[:, :], bcast_row(dst_prev_row, i, H)).then_inc(s_dr, 16)
                tick.load(sp, i, 1, 3 + 2 * EIT)
                sp.wait_ge(s_x2, i)
                split_load(sp, resb, own(res1, i), s_rl)

            def stores(i):
                tick.store(sp, i, 1, 2 * EIT)
                sp.wait_ge(s_x2, i + 1)
                split_load(sp, own(x2t["D"], i), x2b, s_xst)
                for q, to in enumerate((own(self2["D"], i), rows(fwd2, i), rows(bwd2, i))):
                    sp.wait_ge(st.s_done["A"], i * pl.by["A"] + pl.consumed(pl.index(kD, 1, q), "A"))
                    split_load(sp, to, part2[q], s_2st[q])
            loads(0)
            with sp.Fori(1, EIT) as i:
                loads(i)
                stores(i - 1)
            stores(EIT - 1)
            for s_ in (s_fin, s_xst, *s_2st):
                sp.wait_ge(s_, 32 * EIT)

        @block.vector
        def _(v):
            DV.memset(Tr[:, :, :], 0.0)
            DV.memset(ones_h[:, :], 1.0)
            DV.memset(apart[:, B:B + 1], -FAR)
            DV.memset(f_last[:, :], -FAR).then_inc(s_set, 1)
            v.wait_ge(s_set, 1)
            v.wait_ge(s_con, 16)
            v.wait_ge(s_con2, 16)
            heads = lambda t: t.rearrange("p j (h c) -> p j h c", c=HC)
            spread = lambda t: t.unsqueeze(3).to_broadcast([P, J, H, HC])
            a_row = att_b[:, :].unsqueeze(1).to_broadcast([P, J, C])
            e_row = eb_b[:, :].unsqueeze(1).to_broadcast([P, J, H])
            part = lambda t, n: t[:, n * JH:(n + 1) * JH].rearrange("p (j h) -> p j h", h=H)

            def logits(v, i):
                step = lambda ins: chain.step(v, i, ins)
                v.wait_ge(s_pv, i * (16 * J) + 16 * J)
                v.wait_ge(s_pu, i * (16 * J) + 16 * J)
                DV.tensor_copy(red8[:, :], reduced[:, bass.ds(i * J, J)])
                step(DV.tensor_tensor(z[:, :, :], pu[:, :, :], pv[:, :, :], ALU.add))
                step(DV.scalar_tensor_tensor(out=z[:, :, :], in0=z[:, :, :], scalar=SLOPE, in1=z[:, :, :],
                                             op0=ALU.mult, op1=ALU.max))
                DV.tensor_tensor(ew[:, :, :], red8[:, :].unsqueeze(2).to_broadcast([P, J, H]), e_row, ALU.mult)
                step(DV.tensor_tensor(z[:, :, :], z[:, :, :], a_row, ALU.mult))
                step(DV.tensor_reduce(lg[:, :, :], heads(z[:, :, :]), AX.X, ALU.add))
                DV.tensor_tensor(lg[:, :, :], lg[:, :, :], ew[:, :, :], ALU.add).then_inc(s_lg, 1)
                step(DV.scalar_tensor_tensor(out=z[:, :, :], in0=pv[:, :, :], scalar=SLOPE, in1=pv[:, :, :],
                                             op0=ALU.mult, op1=ALU.max))
                step(DV.tensor_tensor(z[:, :, :], z[:, :, :], a_row, ALU.mult))
                step(DV.tensor_reduce(ls[:, :, :], heads(z[:, :, :]), AX.X, ALU.add))
                DV.scalar_tensor_tensor(out=ls[:, :, :], in0=ls[:, :, :], scalar=2.0, in1=e_row,
                                        op0=ALU.mult, op1=ALU.add).then_inc(s_ls, 1)

            def equalities(v, i):
                v.wait_ge(s_T, i * J)
                step = lambda ins: chain.step(v, i, ins)
                DV.tensor_copy(d8[:, :], dst_i[:, bass.ds(i * J, J)])
                step(DV.tensor_copy(p8[:, :], prev_i[:, bass.ds(i * J, J)]))
                v.wait_ge(s_dr, i * 32 + 32)
                for t, c8 in ((S, d8), (M, p8)):
                    for j in range(J):
                        ins = DV.tensor_scalar(t[:, j, :], drow[:, j * P:(j + 1) * P], c8[:, j:j + 1], None, ALU.is_equal)
                    if t is S:
                        ins.then_inc(s_eq, 1)
                step(DV.tensor_tensor(apart[:, 0:B], drow[0:H, :], dprev[:, :], ALU.not_equal))
                DV.tensor_scalar(apart[:, 0:B], apart[:, 0:B], -FAR, None, ALU.mult).then_inc(s_eq, 1)
                v.wait_ge(s_eq, i * 2 + 2)

            def maxima(v, i):
                step = lambda ins: chain.step(v, i, ins)
                v.wait_ge(s_lgT, i * 2 + 2)
                step(DV.tensor_tensor_scan(F[:, :], apart[:, 0:B], lgT[:, :], f_last[:, 0:1], ALU.add, ALU.max))
                step(DV.tensor_tensor_scan(G[:, ::-1], apart[:, B:0:-1], F[:, ::-1], -FAR, ALU.add, ALU.max))
                step(DV.tensor_tensor(f_diff[:, :], f_last[:, :], G[:, 0:1], ALU.subtract))
                DV.tensor_copy(f_last[:, :], F[:, B - 1:B])
                DV.tensor_scalar(f_diag[:, :], ident[0:H, 0:H], f_diff[:, 0:1], None, ALU.mult).then_inc(s_G, 1)

            def exponents(v, i):
                step = lambda ins: chain.step(v, i, ins)
                v.wait_ge(s_lg, i + 1)
                v.wait_ge(s_ls, i + 1)
                v.wait_ge(s_R, i + 1)
                m = part(r_bank[0:P, :], 0)
                step(DV.tensor_tensor(mf[:, :, :], m, ls[:, :, :], ALU.max))
                DV.tensor_tensor(part(arg, 0), lg[:, :, :], m, ALU.subtract)
                DV.tensor_tensor(part(arg, 1), m, mf[:, :, :], ALU.subtract)
                DV.tensor_tensor(part(arg, 2), ls[:, :, :], mf[:, :, :], ALU.subtract)
                DV.tensor_scalar(arg[:, 3 * JH:], r_bank[0:P, JH:JH + H], 0.0, None, ALU.min).then_inc(s_arg, 1)

            def values(v, i):
                v.wait_ge(s_ex, i + 1)
                DV.tensor_tensor(heads(V[:, :, 0:C]), heads(pu[:, :, :]), spread(part(ex, 0)), ALU.mult)
                DV.tensor_copy(V[:, :, C:CH], part(ex, 0))
                f = ex[:, 3 * JH:3 * JH + H]
                DV.tensor_tensor(Tr[:, J - 1, C:CH], Tr[:, J - 1, C:CH], f, ALU.mult)
                before = Tr[:, J - 1, 0:C].rearrange("p (h c) -> p h c", c=HC)
                DV.tensor_tensor(before, before, f.unsqueeze(2).to_broadcast([P, H, HC]), ALU.mult).then_inc(s_V, 1)

            def finish(v, i):
                step = lambda ins: chain.step(v, i, ins)
                g, es, total = part(ex, 1), part(ex, 2), Tr[:, :, C:CH]
                v.wait_ge(s_Tr, i * J + J)
                step(DV.tensor_tensor(den[:, :, :], total, g, ALU.mult))
                step(DV.tensor_tensor(den[:, :, :], den[:, :, :], es, ALU.add))
                step(DV.tensor_scalar(den[:, :, :], den[:, :, :], 1e-12, None, ALU.max))
                step(DV.reciprocal(den[:, :, :], den[:, :, :]))
                DV.tensor_tensor(gd[:, :, :], den[:, :, :], g, ALU.mult)
                step(DV.tensor_tensor(ed[:, :, :], den[:, :, :], es, ALU.mult))
                v.wait_ge(s_kept, i + 1)
                DV.tensor_tensor(heads(mixed[:, :, :]), heads(Tr[:, :, 0:C]), spread(gd[:, :, :]), ALU.mult)
                step(DV.tensor_tensor(heads(z[:, :, :]), heads(pv_kept[:, :, :]), spread(ed[:, :, :]), ALU.mult))
                v.wait_ge(s_rl, i * 32 + 32)
                step(DV.tensor_tensor(z[:, :, :], z[:, :, :], resb[:, :, :], ALU.add))
                v.wait_ge(s_xst, i * 32)
                v.wait_ge(st.s_norm, i * (2 * pl.n))
                DV.tensor_tensor(x2b[:, :, :], mixed[:, :, :], z[:, :, :], ALU.add).then_inc(s_x2, 1)
            with v.Fori(0, EIT) as i:
                st.vector(v, i, {kD: lambda v, i: None, **tick.ends()},
                          {0: [logits], 1: [equalities, maxima], 2: [exponents], 3: [values], 6: [finish]})
            chain.close()

        @block.scalar
        def _(a):
            def keep_pv(a, i):
                a.wait_ge(s_pv, i * (16 * J) + 16 * J)
                a.wait_ge(s_x2, i)
                AC.activation(pv_kept[:, :, :], pv[:, :, :], ACT.Copy).then_inc(s_kept, 1)

            def logit_rows(a, i):
                for n in range(2):
                    a.wait_ge(s_lT, i * 2 + n + 1)
                    AC.activation(lgT[:, n * (B // 2):(n + 1) * (B // 2)], l_bank[n][0:H, 0:B // 2], ACT.Copy)\
                        .then_inc(s_lgT, 1)

            def exponentials(a, i):
                a.wait_ge(s_arg, i + 1)
                AC.activation(ex[:, :], arg[:, :], ACT.Exp).then_inc(s_ex, 1)

            def keep_sums(j0):
                def do(a, i):
                    for j in range(j0, j0 + 4):
                        a.wait_ge(s_T, i * J + j + 1)
                        AC.activation(Tr[:, j, :], t_bank[0:P, 0:CH], ACT.Copy).then_inc(s_Tr, 1)
                return do

            def second(a, i):
                for half in range(2):
                    for q in range(3):
                        if half == 0:
                            a.wait_ge(s_2st[q], i * 32)
                        bank = st.part(a, i, kD, half, q)
                        AC.activation(halves(part2[q], half), bank, ACT.Copy).then_inc(st.s_done["A"], 1)
            with a.Fori(0, EIT) as i:
                st.scalar(a, i, {kD: second}, {0: [keep_pv, logit_rows], 2: [exponentials], 4: [keep_sums(0)],
                                               5: [keep_sums(4)]})

        @block.tensor
        def _(pe):
            pe.wait_ge(s_set, 1)

            def turn_logits(pe, i):
                pe.wait_ge(s_lg, i + 1)
                for j in range(J):
                    ins = PE_.transpose(l_bank[j // HALF][0:H, j % HALF * P:(j % HALF + 1) * P], lg[:, j, :],
                                        ident[0:P, 0:P])
                    if j % HALF == HALF - 1:
                        ins.then_inc(s_lT, 1)

            def turn_maxima(pe, i):
                pe.wait_ge(s_set, 1)
                pe.wait_ge(s_G, i + 1)
                for j in range(J):
                    PE_.transpose(r_bank[0:P, j * H:(j + 1) * H], G[:, j * P:(j + 1) * P], ident[0:H, 0:H])
                PE_.matmul(r_bank[0:P, JH:JH + H], ones_h[:, :], f_diag[:, :], start=True, stop=True).then_inc(s_R, 1)

            def sums(j0):
                def do(pe, i):
                    if j0 == 0:
                        pe.wait_ge(s_V, i + 1)
                        pe.wait_ge(s_eq, i * 2 + 2)
                    for j in range(j0, j0 + 4):
                        pe.wait_ge(s_Tr, i * J + j)
                        PE_.matmul(t_bank[0:P, 0:CH], S[:, j, :], V[:, j, :], start=True, stop=False)
                        PE_.matmul(t_bank[0:P, 0:CH], M[:, j, :], Tr[:, (j - 1) % J, :], start=False, stop=True)\
                            .then_inc(s_T, 1)
                return do
            with pe.Fori(0, EIT) as i:
                st.tensor(pe, i, {0: [turn_logits], 1: [turn_maxima], 4: [sums(0)], 5: [sums(4)]})

    clear_semaphores()

    with ExitStack() as ctx:
        tile = lambda n, s, d=f32: ctx.enter_context(nc.sbuf_tensor("D_" + n, s, d))
        sem = lambda n: sem_of(ctx, "D_" + n)
        psum = lambda n: ctx.enter_context(nc.psum_tensor("D_" + n, [128, 512], f32))
        x0, final = tile("x0", [P, J, C]), tile("final", [P, J, C])
        s_x0, s_fin = sem("x_block"), sem("out_stored")
        fu, bv = tile("fu", [P, J, CW]), tile("bv", [P, J, CW])
        Tr, bs = tile("Tr", [P, J, CW]), tile("bs", [P, J, CW])
        S, M, Q = tile("S", [P, J, P]), tile("M", [P, J, P]), tile("Q", [P, J, P])
        drow, srow = tile("drow", [P, B], i32), tile("srow", [P, B], i32)
        d8, p8, s8, ss8 = (tile(n, [P, J], i32) for n in ("d8", "p8", "s8", "ss8"))
        a8, pd8, rc8 = (tile(n, [P, J]) for n in ("a8", "pd8", "rc8"))
        idx8 = tile("idx8", [P, J], i32)
        from8, to8 = tile("from8", [P, J], i32), tile("to8", [P, J], i32)
        selfb, meanb, sumb = tile("selfb", [P, J, C]), tile("meanb", [P, J, C]), tile("sumb", [P, J, C])
        PER = 3
        GROUPS = [range(g, min(g + PER, J)) for g in range(0, J, PER)]
        t_bank, b_bank = psum("T"), [psum(f"B{n}") for n in range(len(GROUPS))]
        s_set, s_fu, s_bv, s_cols = sem("constants_set"), sem("src_rows"), sem("dst_rows"), sem("pool_columns")
        s_dr, s_sr, s_sl, s_ch, s_eq = sem("dst_row"), sem("src_row"), sem("self_loaded"), sem("dve_step"), sem("equalities_ready")
        s_T, s_Tr, s_B, s_Bs = sem("sum_in_psum"), sem("sum_kept"), sem("back_in_psum"), sem("back_kept")
        s_idx, s_add, s_sum, s_sst = sem("back_index_ready"), sem("back_added"), sem("self_plus_mean"), sem("stored_self")
        tick = Tick(x0, final, s_x0, s_fin)
        st = Stage(ctx, "D", tick.units, when=[0, 2, 4, 5], banks=2)
        tick.place(st, range(4))
        pl = st.plan
        chain = Chain(s_ch, 6)
        block = ctx.enter_context(nc.Block())

        @block.gpsimd
        def _(pool):
            pool.wait_ge(s_set, 1)

            def fetch(i, g, m):
                if g:
                    pool.wait_ge(s_T, i * J)
                    pool.wait_ge(s_B, i * len(GROUPS))
                    pool.wait_ge(s_fu, i * (16 * J))
                    pool.wait_ge(s_bv, i * (16 * J))
                    GP.tensor_copy(from8[:, :], slot_s[:, bass.ds(i * J, J)]).then_inc(s_cols, 1)
                    GP.tensor_copy(to8[:, :], slot_d[:, bass.ds(i * J, J)]).then_inc(s_cols, 1)
                    wait_sw(pool, s_cols, i * 2 + 2)
                if m is not None:
                    pool.wait_ge(s_idx, m + 1)
                    wait_sw(pool, s_Bs, m * len(GROUPS) + len(GROUPS))
                for j in range(J):
                    if g:
                        gather(fu[:, j, 0:C], fwd2[:, :], from8[:, j:j + 1]).then_inc(s_fu, 16)
                        gather(bv[:, j, 0:C], bwd2[:, :], to8[:, j:j + 1]).then_inc(s_bv, 16)
                    if m is not None:
                        wait_sw(pool, s_add, m * (16 * J) + 16 * j)
                        GP.indirect_dma_start(out=back[:, :], in_=bs[:, j, :], in_offset=None, compute_op=ALU.add,
                                              out_offset=bass.IndirectOffsetOnAxis(ap=idx8[:, j:j + 1], axis=0))\
                            .then_inc(s_add, 16)
            fetch(0, True, None)
            with pool.Fori(1, EIT) as i:
                fetch(i, True, i - 1)
            fetch(EIT - 1, False, EIT - 1)
            pool.wait_ge(s_add, 16 * T)

        @block.sync
        def _(sp):
            def loads(i, per=1, first=3 + 3 * EIT):
                wait_sp(sp, s_eq, i * 3)
                sp.dma_start(drow[:, :], bcast_row(dst_row, i, P)).then_inc(s_dr, 16)
                sp.dma_start(srow[:, :], bcast_row(src_row, i, P)).then_inc(s_sr, 16)
                tick.load(sp, i, per, first)
                wait_sp(sp, s_sum, i)
                split_load(sp, selfb, own(self2["D"], i), s_sl)

            def stores(i):
                tick.store(sp, i, 1, 3 * EIT)
                wait_sp(sp, s_sum, i + 1)
                split_load(sp, own(self2["D"], i), sumb, s_sst)
            loads(0)
            with sp.Fori(1, EIT - 3) as i:
                loads(i)
                stores(i - 1)
            for i in range(EIT - 3, EIT):
                loads(i, 0, NB - 1)
                stores(i - 1)
            stores(EIT - 1)
            for s_ in (s_fin, s_sst):
                sp.wait_ge(s_, 32 * EIT)

        @block.vector
        def _(v):
            DV.memset(Tr[:, :, :], 0.0)
            DV.memset(fu[:, :, C:CW], 1.0)
            DV.memset(bv[:, :, C:CW], 1.0).then_inc(s_set, 1)
            v.wait_ge(s_set, 1)

            def equalities(v, i):
                v.wait_ge(s_T, i * J)
                v.wait_ge(s_B, i * len(GROUPS))
                DV.tensor_copy(d8[:, :], dst_i[:, bass.ds(i * J, J)])
                DV.tensor_copy(p8[:, :], prev_i[:, bass.ds(i * J, J)])
                DV.tensor_copy(a8[:, :], again[:, bass.ds(i * J, J)])
                DV.tensor_copy(ss8[:, :], slot_s[:, bass.ds(i * J, J)])
                chain.step(v, i, DV.tensor_copy(s8[:, :], src_i[:, bass.ds(i * J, J)]))
                v.wait_ge(s_dr, i * 16 + 16)
                v.wait_ge(s_sr, i * 16 + 16)
                for t, row, c8 in ((S, drow, d8), (M, drow, p8), (Q, srow, s8)):
                    for j in range(J):
                        ins = DV.tensor_scalar(t[:, j, :], row[:, j * P:(j + 1) * P], c8[:, j:j + 1], None, ALU.is_equal)
                    ins.then_inc(s_eq, 1)

            def back_index(v, i):
                v.wait_ge(s_add, i * (16 * J))
                chain.step(v, i, DV.tensor_tensor(pd8[:, :], pads[:, :], ss8[:, :], ALU.subtract))
                chain.step(v, i, DV.tensor_tensor(pd8[:, :], pd8[:, :], a8[:, :], ALU.mult))
                DV.tensor_tensor(idx8[:, :], pd8[:, :], ss8[:, :], ALU.add).then_inc(s_idx, 1)

            def finish(v, i):
                v.wait_ge(s_Tr, i * J + J)
                chain.step(v, i, DV.tensor_scalar(rc8[:, :], Tr[:, :, C], 1.0, None, ALU.max))
                chain.step(v, i, DV.reciprocal(rc8[:, :], rc8[:, :]))
                chain.step(v, i, DV.tensor_tensor(meanb[:, :, :], Tr[:, :, 0:C],
                                                  rc8[:, :].unsqueeze(2).to_broadcast([P, J, C]), ALU.mult))
                v.wait_ge(s_sl, i * 32 + 32)
                v.wait_ge(s_sst, i * 32)
                DV.tensor_tensor(sumb[:, :, :], meanb[:, :, :], selfb[:, :, :], ALU.add).then_inc(s_sum, 1)
            with v.Fori(0, EIT) as i:
                st.vector(v, i, tick.ends(), {0: [equalities], 5: [finish, back_index]})
            chain.close()

        @block.scalar
        def _(a):
            def keep_sums(j0):
                def do(a, i):
                    if j0 == 0:
                        a.wait_ge(s_sum, i)
                    for j in range(j0, j0 + 4):
                        a.wait_ge(s_T, i * J + j + 1)
                        AC.activation(Tr[:, j, :], t_bank[0:P, 0:CW], ACT.Copy).then_inc(s_Tr, 1)
                return do

            def keep_back(a, i):
                a.wait_ge(s_add, i * (16 * J))
                for n, g in enumerate(GROUPS):
                    a.wait_ge(s_B, i * len(GROUPS) + n + 1)
                    AC.activation(bs[:, g[0]:g[-1] + 1, :],
                                  b_bank[n][0:P, 0:len(g) * CW].rearrange("p (j c) -> p j c", c=CW), ACT.Copy)\
                        .then_inc(s_Bs, 1)
            with a.Fori(0, EIT) as i:
                st.scalar(a, i, {}, {1: [keep_sums(0)], 2: [keep_sums(4)], 4: [keep_back]})

        @block.tensor
        def _(pe):
            pe.wait_ge(s_set, 1)

            def sums(j0):
                def do(pe, i):
                    if j0 == 0:
                        pe.wait_ge(s_fu, i * (16 * J) + 16 * J)
                        pe.wait_ge(s_eq, i * 3 + 2)
                    for j in range(j0, j0 + 4):
                        pe.wait_ge(s_Tr, i * J + j)
                        PE_.matmul(t_bank[0:P, 0:CW], S[:, j, :], fu[:, j, :], start=True, stop=False)
                        PE_.matmul(t_bank[0:P, 0:CW], M[:, j, :], Tr[:, (j - 1) % J, :], start=False, stop=True)\
                            .then_inc(s_T, 1)
                return do

            def backs(pe, i):
                pe.wait_ge(s_bv, i * (16 * J) + 16 * J)
                pe.wait_ge(s_eq, i * 3 + 3)
                pe.wait_ge(s_Bs, i * len(GROUPS))
                for n, g in enumerate(GROUPS):
                    for j in g:
                        at = (j - g[0]) * CW
                        ins = PE_.matmul(b_bank[n][0:P, at:at + CW], Q[:, j, :], bv[:, j, :], start=True, stop=True)
                    ins.then_inc(s_B, 1)
            with pe.Fori(0, EIT) as i:
                st.tensor(pe, i, {1: [sums(0)], 2: [sums(4)], 3: [backs]})

    with ExitStack() as ctx:
        tile = lambda n, s, d=f32: ctx.enter_context(nc.sbuf_tensor("E_" + n, s, d))
        sem = lambda n: sem_of(ctx, "E_" + n)
        x2b = {k: tile("x2" + k, [P, J, C]) for k in "DS"}
        selfb = {k: tile("self" + k, [P, J, C]) for k in "DS"}
        backb = {k: tile("back" + k, [P, J, CW]) for k in "DS"}
        x3b = {k: tile("x3" + k, [P, J, C]) for k in "DS"}
        x4b = {k: tile("x4" + k, [P, J, C]) for k in "DS"}
        pj = {k: tile("proj" + k, [P, J, C]) for k in "DS"}
        rc8 = {k: tile("rc8" + k, [P, J]) for k in "DS"}
        s_in = {k: sem("loaded_" + k) for k in "DS"}
        s_x3 = {k: sem("x3_ready_" + k) for k in "DS"}
        s_pst = {k: sem("stored_proj_" + k) for k in "DS"}
        s_xst = {k: sem("stored_x4_" + k) for k in "DS"}
        s_ch = sem("dve_step")
        units = [Unit(k + "3", x3b[k], [("l3", None, "A"), ("r3", bias3["l3"], "D")],
                      ready=lambda v, i, k=k: v.wait_ge(s_x3[k], i + 1)) for k in "DS"]
        st = Stage(ctx, "E", units, when=[1, 2])
        pl = st.plan
        chain = Chain(s_ch, 8)
        block = ctx.enter_context(nc.Block())

        @block.sync
        def _(sp):
            def loads(i):
                for k, base in (("D", 0), ("S", E)):
                    wait_sp(sp, s_x3[k], i)
                    split_load(sp, x2b[k], own(x2t[k], i), s_in[k])
                    split_load(sp, selfb[k], own(self2[k], i), s_in[k])
                    split_load(sp, backb[k], rows(back, i, base), s_in[k])

            def stores(i):
                for n, (k, base) in enumerate((("D", 0), ("S", E))):
                    wait_sp(sp, st.s_done["A"], i * pl.by["A"] + pl.consumed(pl.index(n, 1, 0), "A"))
                    split_load(sp, rows(proj3, i, base), pj[k], s_pst[k])
                    wait_sp(sp, st.s_done["D"], i * pl.by["D"] + pl.consumed(pl.index(n, 1, 1), "D"))
                    split_load(sp, own(x4[k], i), x4b[k], s_xst[k])
            loads(0)
            with sp.Fori(1, EIT) as i:
                loads(i)
                stores(i - 1)
            stores(EIT - 1)
            for k in "DS":
                sp.wait_ge(s_pst[k], 32 * EIT)
                sp.wait_ge(s_xst[k], 32 * EIT)

        @block.vector
        def _(v):
            def start(k):
                def do(v, i):
                    step = lambda ins: chain.step(v, i, ins)
                    v.wait_ge(s_in[k], i * 96 + 96)
                    step(DV.tensor_scalar(rc8[k][:, :], backb[k][:, :, C], 1.0, None, ALU.max))
                    step(DV.reciprocal(rc8[k][:, :], rc8[k][:, :]))
                    step(DV.tensor_tensor(backb[k][:, :, 0:C], backb[k][:, :, 0:C],
                                          rc8[k][:, :].unsqueeze(2).to_broadcast([P, J, C]), ALU.mult))
                    step(DV.tensor_tensor(selfb[k][:, :, :], selfb[k][:, :, :], backb[k][:, :, 0:C], ALU.add))
                    v.wait_ge(st.s_norm, i * (2 * pl.n))
                    v.wait_ge(st.s_done["D"], i * pl.by["D"])
                    DV.scalar_tensor_tensor(out=x3b[k][:, :, :], in0=selfb[k][:, :, :], scalar=0.0, in1=x2b[k][:, :, :],
                                            op0=ALU.max, op1=ALU.add).then_inc(s_x3[k], 1)
                return do

            def end(n, k):
                def do(v, i):
                    v.wait_ge(s_xst[k], i * 32)
                    for half in range(2):
                        ps = st.part(v, i, n, half, 1)
                        DV.tensor_tensor(halves(x4b[k], half), ps, halves(x3b[k], half), ALU.add)\
                            .then_inc(st.s_done["D"], 1)
                return do
            with v.Fori(0, EIT) as i:
                st.vector(v, i, {0: end(0, "D"), 1: end(1, "S")}, {0: [start("D")], 1: [start("S")]})
            chain.close()

        @block.scalar
        def _(a):
            def proj(n, k):
                def do(a, i):
                    a.wait_ge(s_pst[k], i * 32)
                    st.copy_part(a, i, n, 0, pj[k])
                return do
            with a.Fori(0, EIT) as i:
                st.scalar(a, i, {0: proj(0, "D"), 1: proj(1, "S")})

        @block.tensor
        def _(pe):
            with pe.Fori(0, EIT) as i:
                st.tensor(pe, i)

    with ExitStack() as ctx:
        tile = lambda n, s, d=f32: ctx.enter_context(nc.sbuf_tensor("F_" + n, s, d))
        sem = lambda n: sem_of(ctx, "F_" + n)
        pu, Tr = tile("pu", [P, J, CW]), tile("Tr", [P, J, CW])
        S, M = tile("S", [P, J, P]), tile("M", [P, J, P])
        drow = tile("drow", [P, B], i32)
        d8, p8, ss8, sv8, s8 = (tile(n, [P, J], i32) for n in ("d8", "p8", "ss8", "sv8", "s8"))
        rc8, far8 = tile("rc8", [P, J]), tile("far8", [P, J])
        outs8, from8, lead8 = (tile(n, [P, J], i32) for n in ("outs8", "from8", "lead8"))
        x4d, x4s, meanb, outb = (tile(n, [P, J, C]) for n in ("x4d", "x4s", "meanb", "outb"))
        t_bank = ctx.enter_context(nc.psum_tensor("F_T", [128, 512], f32))
        s_set, s_pu, s_from, s_lead, s_dr, s_ld, s_ls = (sem(n) for n in (
            "constants_set", "src_rows", "slots_copied", "leads_copied", "dst_row", "x4_D_loaded", "x4_S_loaded"))
        s_ch, s_eq, s_T, s_Tr, s_res, s_idx = (sem(n) for n in ("dve_step", "equalities_ready", "sum_in_psum", "sum_kept",
                                                               "rows_ready", "places_ready"))
        s_out = sem("rows_written")
        chain = Chain(s_ch, 5)
        block = ctx.enter_context(nc.Block())

        @block.gpsimd
        def _(pool):
            pool.wait_ge(s_set, 1)

            def fetch(i):
                pool.wait_ge(s_T, i * J)
                pool.wait_ge(s_pu, i * (16 * J))
                GP.tensor_copy(from8[:, :], slot_s[:, bass.ds(i * J, J)]).then_inc(s_from, 1)
                wait_sw(pool, s_from, i + 1)
                for j in range(J):
                    gather(pu[:, j, 0:C], proj3[:, :], from8[:, j:j + 1]).then_inc(s_pu, 16)

            def put(i):
                pool.wait_ge(s_out, i * (32 * J))
                GP.tensor_copy(lead8[:, :], lead_i[:, bass.ds(i * J, J)]).then_inc(s_lead, 1)
                pool.wait_ge(s_lead, i + 1)
                pool.wait_ge(s_idx, i + 1)
                wait_sw(pool, s_ls, i * 32 + 32)
                for j in range(J):
                    scatter(out[:, :], outs8[:, j:j + 1], x4s[:, j, :], N - 1).then_inc(s_out, 16)
                wait_sw(pool, s_res, i + 1)
                for j in range(J):
                    scatter(out[:, :], lead8[:, j:j + 1], outb[:, j, :], N - 1).then_inc(s_out, 16)
            fetch(0)
            with pool.Fori(1, EIT) as i:
                fetch(i)
                put(i - 1)
            put(EIT - 1)
            pool.wait_ge(s_out, 32 * T)

        @block.sync
        def _(sp):
            with sp.Fori(0, EIT) as i:
                wait_sp(sp, s_eq, i * 2)
                sp.dma_start(drow[:, :], bcast_row(dst_row, i, P)).then_inc(s_dr, 16)
                wait_sp(sp, s_res, i)
                split_load(sp, x4d, own(x4["D"], i), s_ld)
                wait_sp(sp, s_out, i * (32 * J))
                split_load(sp, x4s, own(x4["S"], i), s_ls)

        @block.vector
        def _(v):
            DV.memset(Tr[:, :, :], 0.0)
            DV.memset(pu[:, :, C:CW], 1.0).then_inc(s_set, 1)
            v.wait_ge(s_set, 1)
            with v.Fori(0, EIT) as i:
                v.wait_ge(s_T, i * J)
                DV.tensor_copy(d8[:, :], dst_i[:, bass.ds(i * J, J)])
                DV.tensor_copy(p8[:, :], prev_i[:, bass.ds(i * J, J)])
                DV.tensor_copy(ss8[:, :], slot_s[:, bass.ds(i * J, J)])
                DV.tensor_copy(sv8[:, :], slot_v[:, bass.ds(i * J, J)])
                chain.step(v, i, DV.tensor_copy(s8[:, :], src_i[:, bass.ds(i * J, J)]))
                v.wait_ge(s_dr, i * 16 + 16)
                for t, c8 in ((S, d8), (M, p8)):
                    for j in range(J):
                        ins = DV.tensor_scalar(t[:, j, :], drow[:, j * P:(j + 1) * P], c8[:, j:j + 1], None, ALU.is_equal)
                    ins.then_inc(s_eq, 1)
                chain.step(v, i, DV.tensor_tensor(far8[:, :], ss8[:, :], sv8[:, :], ALU.not_equal))
                v.wait_ge(s_out, i * (32 * J))
                DV.scalar_tensor_tensor(out=outs8[:, :], in0=far8[:, :], scalar=float(N), in1=s8[:, :],
                                        op0=ALU.mult, op1=ALU.add).then_inc(s_idx, 1)
                v.wait_ge(s_Tr, i * J + J)
                chain.step(v, i, DV.tensor_scalar(rc8[:, :], Tr[:, :, C], 1.0, None, ALU.max))
                chain.step(v, i, DV.reciprocal(rc8[:, :], rc8[:, :]))
                chain.step(v, i, DV.tensor_tensor(meanb[:, :, :], Tr[:, :, 0:C],
                                                  rc8[:, :].unsqueeze(2).to_broadcast([P, J, C]), ALU.mult))
                v.wait_ge(s_ld, i * 32 + 32)
                DV.tensor_tensor(outb[:, :, :], meanb[:, :, :], x4d[:, :, :], ALU.add).then_inc(s_res, 1)
            chain.close()

        @block.scalar
        def _(a):
            with a.Fori(0, EIT) as i:
                a.wait_ge(s_res, i)
                for j in range(J):
                    a.wait_ge(s_T, i * J + j + 1)
                    AC.activation(Tr[:, j, :], t_bank[0:P, 0:CW], ACT.Copy).then_inc(s_Tr, 1)

        @block.tensor
        def _(pe):
            pe.wait_ge(s_set, 1)
            with pe.Fori(0, EIT) as i:
                pe.wait_ge(s_pu, i * (16 * J) + 16 * J)
                pe.wait_ge(s_eq, i * 2 + 2)
                for j in range(J):
                    pe.wait_ge(s_Tr, i * J + j)
                    PE_.matmul(t_bank[0:P, 0:CW], S[:, j, :], pu[:, j, :], start=True, stop=False)
                    PE_.matmul(t_bank[0:P, 0:CW], M[:, j, :], Tr[:, (j - 1) % J, :], start=False, stop=True)\
                        .then_inc(s_T, 1)
    top.close()


def kernel(x, src, dst, edge_attr_128, edge_attr_2, L0_gnn_W_gea, L0_gnn_W_lin, L0_gnn_gamma, L0_gnn_beta,
           L1_gnn_W_lin, L1_gnn_att, L1_gnn_W_eb, L1_gnn_bias, L1_gnn_W_res, L2_gnn_W, L3_gnn_W_l, L3_gnn_W_r,
           L3_gnn_b_l):
    import numpy as np
    import concourse.bacc as bacc
    from concourse.bass_utils import run_bass_kernel_spmd as run

    arrays = layout(np, x, src, dst, edge_attr_128, edge_attr_2, L0_gnn_W_gea, L0_gnn_W_lin, L0_gnn_gamma,
                    L0_gnn_beta, L1_gnn_W_lin, L1_gnn_att, L1_gnn_W_eb, L1_gnn_bias, L1_gnn_W_res, L2_gnn_W,
                    L3_gnn_W_l, L3_gnn_W_r, L3_gnn_b_l)
    nc = bacc.Bacc("TRN2", target_bir_lowering=False, num_devices=1)
    args = [nc.dram_tensor(n, a.shape, mybir.dt.from_np(a.dtype), kind="ExternalInput").ap() for n, a in arrays.items()]
    out = nc.dram_tensor("out", x.shape, f32, kind="ExternalOutput").ap()
    gnn_program(nc, *args, out)
    return run(nc, [arrays], core_ids=[0]).results[0]["out"]


def layout(np, x, src, dst, edge_attr, edge_attr2, w_gea, w_lin0, gamma, beta, w_lin1, att, w_eb, bias1, w_res1,
           w2, w_l3, w_r3, b_l3):
    c = np.ascontiguousarray
    x, src, dst, w2 = (np.asarray(a) for a in (x, src, dst, w2))
    tiles = src.shape[0] // P
    none = np.full(1, -1, dst.dtype)
    prev = np.full((P, tiles), -1, dst.dtype)
    prev[P - 1, 1:] = dst[P - 1:-1:P]
    by_tile = lambda a: c(a.reshape(tiles, P).T)
    return {
        "x": c(x), "src_pt": by_tile(src), "dst_pt": by_tile(dst), "dst_prev_pt": prev,
        "dst_next_pt": by_tile(np.concatenate([dst[1:], none])),
        "src_row": c(src[None, :]), "dst_row": c(dst[None, :]),
        "dst_prev_row": c(np.concatenate([none, dst[:-1]])[None, :]),
        "edge_attr": c(edge_attr), "edge_attr2_pt": c(np.asarray(edge_attr2).reshape(tiles, P, 2).transpose(1, 0, 2)),
        "w_gea": c(np.asarray(w_gea).T), "w_lin0": c(w_lin0), "w_lin0_t": c(np.asarray(w_lin0).T),
        "gamma": c(np.asarray(gamma)[:, None]), "beta": c(np.asarray(beta)[:, None]),
        "w_lin1": c(np.asarray(w_lin1).T), "att": c(np.asarray(att).reshape(1, C)),
        "w_eb": c(np.asarray(w_eb).reshape(1, H)), "bias1": c(np.asarray(bias1)[None, :]),
        "w_res1": c(np.asarray(w_res1).T), "w_self2": c(w2[:, 0:C].T), "w_fwd2": c(w2[:, C:2 * C].T),
        "w_bwd2": c(w2[:, 2 * C:].T), "w_l3": c(np.asarray(w_l3).T), "w_r3": c(np.asarray(w_r3).T),
        "b_l3": c(np.asarray(b_l3)[None, :]),
    }
```

```python
import concourse.bass as bass
from concourse import mybir
from contextlib import ExitStack, contextmanager

f32 = mybir.dt.float32
bf16 = mybir.dt.bfloat16
i32 = mybir.dt.int32
ALU = mybir.AluOpType
ACT = mybir.ActivationFunctionType
AX = mybir.AxisListType

P = 125
J = 8
B = P * J
C = 128
H = 4
HC = C // H
HALF = J // 2
LN_EPS = 1e-5
BN_EPS = 1e-5
GATE_EPS = 1e-8
SLOPE = 0.2
NST = 4
NH = 3
START = 64
FIRST = 16
FAR = 1e30


class Unit:

    def __init__(self, name, x, parts=(), adds=False, gram=False, ready=None, known=None, kept=None):
        self.name, self.x, self.parts, self.adds, self.gram = name, x, list(parts), adds, gram
        self.ready = ready
        self.known = known
        self.kept = kept


class Plan:

    def __init__(self, units):
        self.units = units
        self.n = len(units)
        self.part = []
        for k, u in enumerate(units):
            for half in range(2):
                for q, p in enumerate(u.parts):
                    self.part.append((k, half, q, p[2]))
        self.parts = len(self.part)
        self.by = {c: sum(p[3] == c for p in self.part) for c in "DA"}
        self.adders = sum(u.adds for u in units)
        self.plain = [k for k, u in enumerate(units) if not u.gram]

    def full(self, k):
        return sum(u.known is None for u in self.units[:k])

    def index(self, k, half, q):
        return next(n for n, p in enumerate(self.part) if p[:3] == (k, half, q))

    def consumed(self, n, c):
        return sum(p[3] == c for p in self.part[:n + 1])

    def added(self, k):
        return sum(u.adds for u in self.units[:k + 1])

    def turned(self, k):
        return sum(not u.gram for u in self.units[:k])

    def user(self, k, buffers):
        return (k - buffers, 0) if k >= buffers else (max(range(k, self.n, buffers)), 1)

    def bank_user(self, n, banks):
        return (n - banks, 0) if n >= banks else (max(range(n, self.parts, banks)), 1)

    def taken(self, c, k, half=1, q=0, back=0):
        return self.consumed(self.index(k, half, q), c) - back * self.by[c] + START


def split_load(eng, dst, src, sem):
    eng.dma_start(dst[0:112], src[0:112]).then_inc(sem, 16)
    return eng.dma_start(dst[112:P], src[112:P]).then_inc(sem, 16)


def gnn_program(nc, x, src_pt, dst_pt, run_last, run_last_before, run_end_before, dst_next_pt, src_row, dst_row, dst_prev_row,
                edge_attr, edge_attr2_pt, w_gea, w_lin0, w_lin0_t, gamma, beta, w_lin1, att, w_eb, bias1, w_res1,
                w_self2, w_fwd2, w_bwd2, w_l3, w_r3, b_l3, out):
    N, E = x.shape[0], edge_attr.shape[0]
    NB, EIT, T = N // B, E // B, E // P
    assert NB * B == N and EIT * B == E and NB == 4 * EIT
    CW = C + 1
    PE_, DV, AC, GP, SP_ = nc.tensor, nc.vector, nc.scalar, nc.gpsimd, nc.sync

    def dram(name, shape, dt=f32):
        return nc.dram_tensor(name, shape, dt, kind="Internal").ap()

    slot_of = dram("slot_of", [N, 1], i32)
    scratch = dram("scratch", [1, 1], i32)
    a0 = {s: dram(f"x_plus_h_{s}", [E, C]) for s in "DS"}
    y0 = {s: dram(f"conv_{s}", [E, C]) for s in "DS"}
    proj1 = dram("proj1", [2 * E, C])
    res1 = dram("x1_plus_res", [E, C])
    x2t = {s: dram(f"x2_{s}", [E, C]) for s in "DS"}
    self2 = {s: dram(f"self2_{s}", [E, C]) for s in "DS"}
    fwd2 = dram("fwd2", [2 * E, C])
    bwd2 = dram("bwd2", [2 * E, C])
    back = dram("back_sums", [2 * E + P, CW])
    proj3 = dram("proj3", [2 * E, C])
    x4 = {s: dram(f"x4_{s}", [E, C]) for s in "DS"}

    def own(t, i):
        return t[bass.ds(i * B, B), :].rearrange("(p j) c -> p j c", j=J)

    def rows(t, i, base=0):
        return t[bass.ds(i * B + base, B), :].rearrange("(j p) c -> p j c", p=P)

    top = ExitStack()

    pool_passed = top.enter_context(nc.semaphore("pool_passed"))
    sp_passed = top.enter_context(nc.semaphore("sp_passed"))
    pe_passed = top.enter_context(nc.semaphore("pe_passed"))

    @contextmanager
    def cleared_semaphore(name):
        sem = nc.alloc_semaphore(name)
        used.append(sem)
        fresh.append(sem)
        yield sem

    used, fresh, primed = [], [], []

    def sem_of(ctx, name):
        return ctx.enter_context(cleared_semaphore(name))

    def dma_sem(ctx, name):
        sem = sem_of(ctx, name)
        fresh.remove(sem)
        primed.append(sem)
        return sem

    def prime(pool):
        for sem in primed:
            pool.dma_start(scratch[0:1, :], slot_v[0:1, 0:1]).then_inc(sem, 16)
            pool.wait_ge(sem, FIRST)
        primed.clear()

    def start_semaphores():
        engines = [GP, SP_, DV, AC, PE_]
        for n, sem in enumerate(fresh):
            engines[n % 5].sem_inc(sem, START)
        fresh.clear()
        nc.all_engine_barrier()

    def clear_semaphores():
        nc.clear_and_free_semaphores(used)
        nc.all_engine_barrier()
        used.clear()

    def keep(name, shape, dt=f32):
        return top.enter_context(nc.sbuf_tensor(name, shape, dt))

    ident = keep("ident", [128, 128])
    W = {n: keep(f"W_{n}", [C, C]) for n in
         ("gea", "lin0", "lin0_rows", "bn0", "lin1", "res1", "sum1", "self2", "fwd2", "bwd2", "l3", "r3")}
    bias3 = {n: keep(f"bias_{n}", [3, HALF * C], bf16) for n in ("bn0", "l1", "l3")}
    ones3 = keep("ones3", [3, P], bf16)
    eps_col = keep("eps_col", [128, 1])
    gam_col = keep("gam_col", [C, 1])
    bet_col = keep("bet_col", [C, 1])
    gram_sb = keep("gram_sb", [C, CW + 2])
    bn_mul = keep("bn_mul", [P, C])
    bn_add = keep("bn_add", [P, C])
    src_i = keep("src_i", [P, T], i32)
    dst_i = keep("dst_i", [P, T], i32)
    R = J + 1
    lasts = keep("lasts", [R, EIT], i32)
    goes_on = keep("goes_on", [R, EIT])
    earlier = keep("earlier", [R, J, P])
    leads = keep("leads", [P, T])
    lead_i = keep("lead_i", [P, T], i32)
    again = keep("again", [P, T])
    once_i = keep("once_i", [P, T], i32)
    slot_e = keep("slot_e", [P, T], i32)
    slot_v = keep("slot_v", [P, T], i32)
    reduced = keep("reduced", [P, T])
    slot_s = keep("slot_s", [P, T], i32)
    slot_d = keep("slot_d", [P, T], i32)
    pads = keep("pads", [P, J])
    scale0, shift0 = keep("scale0", [P, NB * J]), keep("shift0", [P, NB * J])
    xl = [keep(f"xl{n}", [P, J, C]) for n in range(4)]

    with ExitStack() as ctx:
        def tile(name, shape, dt=f32):
            return ctx.enter_context(nc.sbuf_tensor(name, shape, dt))

        nxt = tile("nxt", [P, T], i32)
        last_before, end_before = tile("last_before", [R, EIT], i32), tile("end_before", [R, EIT], i32)
        tmp = tile("tmp", [P, T])
        tmp2 = tile("tmp2", [P, T])
        brow = {n: tile(f"brow_{n}", [1, C]) for n in ("l1", "l3")}
        rest = tile("rest", [1, HALF * C])
        piece = {n: tile(f"piece_{n}", [1, 3, HALF * C], bf16) for n in ("l1", "l3")}
        zero = tile("zero", [P, J * CW])
        ea2 = tile("ea2", [P, T, 2])
        loaded = sem_of(ctx, "c_loaded")
        dve = sem_of(ctx, "c_dve_step")
        idn = sem_of(ctx, "c_ident")
        moved = sem_of(ctx, "c_bias_moved")
        zeroed = sem_of(ctx, "c_back_zeroed")
        zset = sem_of(ctx, "c_zero_set")
        start_semaphores()
        block = ctx.enter_context(nc.Block())
        loads = [(W["gea"][:, :], w_gea), (W["lin0"][:, :], w_lin0_t), (W["lin0_rows"][:, :], w_lin0),
                 (W["lin1"][:, :], w_lin1), (W["res1"][:, :], w_res1), (W["self2"][:, :], w_self2),
                 (W["fwd2"][:, :], w_fwd2), (W["bwd2"][:, :], w_bwd2), (W["l3"][:, :], w_l3),
                 (W["r3"][:, :], w_r3), (gam_col[:, :], gamma), (bet_col[:, :], beta),
                 (src_i[:, :], src_pt), (dst_i[:, :], dst_pt), (lasts[:, :], run_last), (last_before[:, :], run_last_before),
                 (end_before[:, :], run_end_before),
                 (nxt[:, :], dst_next_pt), (ea2[:, :, :], edge_attr2_pt), (brow["l1"][:, :], bias1), (brow["l3"][:, :], b_l3)]
        NBACK = back.shape[0] // P

        @block.sync
        def _(sp):
            for to, of in loads:
                sp.dma_start(to, of).then_inc(loaded, 16)
            sp.wait_ge(dve, START + 1)
            share = back.rearrange("(p r) c -> p (r c)", p=P)
            with sp.Fori(0, NBACK // J) as i:
                sp.dma_start(share[:, bass.ds(i * (J * CW), J * CW)], zero[:, :]).then_inc(zeroed, 16)
            left = NBACK % J
            if left:
                sp.dma_start(share[:, NBACK // J * J * CW:NBACK * CW], zero[:, 0:left * CW]).then_inc(zeroed, 16)
            sp.wait_ge(zeroed, START + 16 * (NBACK // J + bool(left)))

        @block.gpsimd
        def _(pool):
            GP.memset(ident[:, :], 0.0).then_inc(idn, 1)
            pool.wait_ge(idn, START + 1)
            GP.affine_select(out=ident[:, :], in_=ident[:, :], compare_op=ALU.not_equal, fill=1.0, base=0,
                             pattern=[[-1, 128]], channel_multiplier=1).then_inc(idn, 1)
            GP.memset(earlier[:, :, :], 1.0).then_inc(idn, 1)
            pool.wait_ge(idn, START + 3)
            GP.affine_select(out=earlier[:, :, :], in_=earlier[:, :, :], compare_op=ALU.is_ge, fill=0.0, base=0,
                             pattern=[[1, J], [0, P]], channel_multiplier=-1).then_inc(idn, 1)
            GP.iota(slot_v[:, :], [[P, T]], base=E, channel_multiplier=1).then_inc(idn, 1)
            GP.iota(slot_e[:, :], [[P, T]], base=0, channel_multiplier=1).then_inc(idn, 1)
            GP.iota(pads[:, :], [[0, J]], base=2 * E, channel_multiplier=1,
                    allow_small_or_imprecise_dtypes=True).then_inc(idn, 1)

        @block.vector
        def _(v):
            n = [0]

            def step(ins):
                n[0] += 1
                ins.then_inc(dve, 1)
                v.wait_ge(dve, START + n[0])

            step(DV.memset(zero[:, :], 0.0))
            DV.memset(ones3[:, :], 1.0)
            DV.memset(eps_col[:, :], LN_EPS)
            for b in xl:
                DV.memset(b[:, :, :], 0.0)
            v.wait_ge(loaded, START + 16 * len(loads))
            step(DV.tensor_tensor(W["sum1"][:, :], W["lin1"][:, :], W["res1"][:, :], ALU.add))
            step(DV.tensor_tensor(leads[:, :], dst_i[:, :], nxt[:, :], ALU.not_equal))
            step(DV.tensor_tensor(goes_on[:, :], last_before[:, :], end_before[:, :], ALU.is_equal))
            step(DV.tensor_scalar(tmp[:, :], leads[:, :], -float(N), float(N), ALU.mult, ALU.add))
            step(DV.tensor_tensor(lead_i[:, :], tmp[:, :], dst_i[:, :], ALU.add))
            step(DV.scalar_tensor_tensor(out=reduced[:, :], in0=ea2[:, :, 1], scalar=0.35, in1=ea2[:, :, 0],
                                         op0=ALU.mult, op1=ALU.add))
            for name in ("l1", "l3"):
                for r in range(HALF):
                    step(DV.tensor_copy(rest[:, r * C:(r + 1) * C], brow[name][:, :]))
                for q in range(3):
                    step(DV.tensor_copy(piece[name][:, q, :], rest[:, :]))
                    step(DV.tensor_tensor(rest[:, :], rest[:, :], piece[name][:, q, :], ALU.subtract))
            v.sem_inc(zset, 1)

        @block.scalar
        def _(a):
            a.wait_ge(zset, START + 1)
            for name in ("l1", "l3"):
                for q in range(3):
                    a.dma_start(bias3[name][q:q + 1, :], piece[name][:, q, :]).then_inc(moved, 16)
            a.wait_ge(moved, START + 16 * 6)

    def pipeline(eng, period, steps, count=EIT, tail=0):
        steps = sorted(((s // period, s % period, r, what) for s, r, what in steps), key=lambda t: t[1:3])
        first, last = min(t[0] for t in steps), max(t[0] for t in steps)

        def peeled(n):
            for back, _, _, what in steps:
                if 0 <= n - back < count:
                    what(eng, n - back)
        for n in range(first, last):
            peeled(n)
        end = max(last, count + first - tail)
        if end > last:
            with eng.Fori(last, end) as i:
                for back, _, _, what in steps:
                    what(eng, i - back if back else i)
        for n in range(end, count + last):
            peeled(n)

    class Stage:

        def __init__(self, ctx, tag, units, when=None, period=None, gram_bank=None, banks=4):
            self.plan = Plan(units)
            self.u = units
            self.gram_bank = gram_bank
            self.when = when or list(range(len(units)))
            self.period = period or len(units)
            self.banks = banks
            t = lambda n, s, d=f32: ctx.enter_context(nc.sbuf_tensor(f"{tag}_{n}", s, d))
            p = lambda n: ctx.enter_context(nc.psum_tensor(f"{tag}_{n}", [128, 512], f32))
            s = lambda n: sem_of(ctx, f"{tag}_{n}")
            self.tile, self.sem, self.bank = t, s, p
            self.h = [t(f"h{n}", [P, J, CW]) for n in range(NH)]
            self.hT = [t(f"hT{n}", [C, B]) for n in range(2)]
            self.st = [t(f"st{n}", [P, J, 6]) for n in range(NST)]
            self.sm = [t(f"sm{n}", [P, 6, J]) for n in range(NST)]
            self.off = [t(f"off{n}", [P, J]) for n in range(NST)]
            self.tp = [p(f"tp{n}") for n in range(2)]
            self.mm = [p(f"mm{n}") for n in range(banks)]
            self.s_step = s("dve_stats_step")
            self.s_stat = s("variance_ready")
            self.s_std = s("std_ready")
            self.s_rec = s("inverse_std_ready")
            self.s_coef = s("scale_shift_ready")
            self.s_norm = s("h_half_ready")
            self.s_tps = s("h_read_by_pe")
            self.s_hT = s("hT_half_ready")
            self.s_mm = s("part_ready")
            self.s_done = {"D": s("part_taken_by_dve"), "A": s("part_taken_by_act")}
            self.s_xh = s("x_plus_h_ready")

        def stats(self, v, i, k):
            st, sm, x, n = self.st[k % NST], self.sm[k % NST], self.u[k].x, self.plan.n
            full = self.plan.full(n)
            base = i * (3 * full) + (3 * self.plan.full(k) + START)
            b, back = self.plan.user(k, NST)
            v.wait_ge(self.s_norm, i * (2 * n) + (2 * b + 2 - back * 2 * n + START))
            if self.u[k].ready:
                self.u[k].ready(v, i)
            for j in range(J):
                last = DV.bn_stats(st[:, j, :], x[:, j, :])
            last.then_inc(self.s_step, 1)
            v.wait_ge(self.s_step, base + 1)
            DV.tensor_tensor(sm[:, 0, :], st[:, :, 1], st[:, :, 4], ALU.add)
            DV.tensor_tensor(sm[:, 2, :], st[:, :, 2], st[:, :, 5], ALU.add)
            DV.tensor_tensor(sm[:, 1, :], st[:, :, 1], st[:, :, 4], ALU.subtract).then_inc(self.s_step, 1)
            v.wait_ge(self.s_step, base + 2)
            DV.tensor_tensor(sm[:, 1, :], sm[:, 1, :], sm[:, 1, :], ALU.mult).then_inc(self.s_step, 1)
            v.wait_ge(self.s_step, base + 3)
            DV.scalar_tensor_tensor(out=sm[:, 3, :], in0=sm[:, 1, :], scalar=C / 4, in1=sm[:, 2, :],
                                    op0=ALU.mult, op1=ALU.add).then_inc(self.s_stat, 1)

        def std(self, a, i, k):
            sm = self.sm[k % NST]
            a.wait_ge(self.s_stat, i * self.plan.full(self.plan.n) + (self.plan.full(k) + 1 + START))
            AC.activation(sm[:, 4, :], sm[:, 3, :], ACT.Sqrt, scale=1.0 / C, bias=eps_col[0:P, :]).then_inc(self.s_std, 1)

        def coef(self, v, i, k):
            sm, n, u = self.sm[k % NST], self.plan.n, self.u[k]
            if u.known:
                b, back = self.plan.user(k, NST)
                v.wait_ge(self.s_norm, i * (2 * n) + (2 * b + 2 - back * 2 * n + START))
                u.ready(v, i)
                scale, shift = u.known(i)
                DV.tensor_copy(sm[:, 5, :], scale)
                DV.tensor_copy(self.off[k % NST][:, :], shift).then_inc(self.s_coef, 1)
                return
            full, before = self.plan.full(n), self.plan.full(k)
            v.wait_ge(self.s_std, i * full + (before + 1 + START))
            DV.reciprocal(sm[:, 5, :], sm[:, 4, :]).then_inc(self.s_rec, 1)
            v.wait_ge(self.s_rec, i * full + (before + 1 + START))
            DV.scalar_tensor_tensor(out=self.off[k % NST][:, :], in0=sm[:, 0, :], scalar=-0.5, in1=sm[:, 5, :],
                                    op0=ALU.mult, op1=ALU.mult).then_inc(self.s_coef, 1)
            if u.kept:
                scale, shift = u.kept(i)
                DV.tensor_copy(scale, sm[:, 5, :])
                v.wait_ge(self.s_coef, i * n + (k + 1 + START))
                DV.tensor_copy(shift, self.off[k % NST][:, :])

        def norm(self, a, i, k):
            pl, h = self.plan, self.h[k % NH]
            b, back = pl.user(k, NH)
            a.wait_ge(self.s_coef, START + i * pl.n + k + 1)
            a.wait_ge(self.s_tps, i * (2 * pl.n) + (2 * b + 2 - back * 2 * pl.n + START))
            if self.u[b].adds:
                a.wait_ge(self.s_xh, i * pl.adders + (pl.added(b) - back * pl.adders + START))
            for j in range(J):
                ins = AC.activation(h[:, j, 0:C], self.u[k].x[:, j, :], ACT.Relu,
                                    scale=self.sm[k % NST][:, 5, j:j + 1], bias=self.off[k % NST][:, j:j + 1])
                if j % HALF == HALF - 1:
                    ins.then_inc(self.s_norm, 1)

        def turn(self, pe, i, k):
            pl, u, h = self.plan, self.u[k], self.h[k % NH]
            for half in range(2):
                pe.wait_ge(self.s_norm, START + i * (2 * pl.n) + 2 * k + half + 1)
                if u.gram:
                    for j in range(half * HALF, half * HALF + HALF):
                        ins = PE_.matmul(self.gram_bank[:, 0:CW], h[:, j, 0:C], h[:, j, :], start=False, stop=False)
                else:
                    m = pl.turned(k)
                    pe.wait_ge(self.s_hT, i * (2 * len(pl.plain)) + (2 * m - 1 + half + START))
                    for j in range(HALF):
                        ins = PE_.transpose(self.tp[half][:, j * P:(j + 1) * P], h[:, half * HALF + j, 0:C],
                                            ident[0:P, 0:P])
                ins.then_inc(self.s_tps, 1)

        def take_turned(self, a, i, k):
            pl, hT = self.plan, self.hT[k % 2]
            if self.u[k].gram:
                return
            b, back = pl.user(k, 2)
            done = i * pl.parts + (sum(p[0] <= b for p in pl.part) - back * pl.parts + START)
            for half in range(2):
                a.wait_ge(self.s_tps, START + i * (2 * pl.n) + 2 * k + half + 1)
                a.wait_ge(self.s_mm, done)
                AC.activation(hT[:, half * HALF * P:(half + 1) * HALF * P], self.tp[half][:, 0:HALF * P],
                              ACT.Copy).then_inc(self.s_hT, 1)

        def multiply(self, pe, i, k):
            pl, u, hT = self.plan, self.u[k], self.hT[k % 2]
            for half in range(2 if u.parts else 0):
                pe.wait_ge(self.s_hT, START + i * (2 * len(pl.plain)) + 2 * pl.turned(k) + half + 1)
                for q, (w, bias, _) in enumerate(u.parts):
                    n = pl.index(k, half, q)
                    b, back = pl.bank_user(n, self.banks)
                    c = pl.part[b][3]
                    pe.wait_ge(self.s_done[c], i * pl.by[c] + (pl.consumed(b, c) - back * pl.by[c] + START))
                    bank = self.mm[n % self.banks]
                    if bias is not None:
                        PE_.matmul(bank[0:P, :], ones3[:, :], bias[:, :], start=True, stop=False)
                    for j in range(HALF):
                        at = (half * HALF + j) * P
                        ins = PE_.matmul(bank[0:P, j * C:(j + 1) * C], hT[:, at:at + P], W[w][:, :],
                                         start=bias is None, stop=True if bias is None else j == HALF - 1)
                    ins.then_inc(self.s_mm, 1)

        def part(self, eng, i, k, half, q):
            n = self.plan.index(k, half, q)
            eng.wait_ge(self.s_mm, START + i * self.plan.parts + n + 1)
            return self.mm[n % self.banks][0:P, :].rearrange("p (j c) -> p j c", c=C)

        def vector(self, ends={}, at={}):
            steps = []
            for k, w in enumerate(self.when):
                steps.append((*at.get(("coef", k), (w + 1, 0)), lambda v, i, k=k: self.coef(v, i, k)))
                if self.u[k].known is None:
                    steps.append((*at.get(("stats", k), (w, 1)), lambda v, i, k=k: self.stats(v, i, k)))
                if k in ends:
                    steps.append((*at.get(("end", k), (w + 3, 2)), ends[k]))
            return steps

        def scalar(self, ends={}, at={}):
            steps = []
            for k, w in enumerate(self.when):
                if k in ends:
                    steps.append((*at.get(("end", k), (w + 3, 0)), ends[k]))
                steps.append((*at.get(("turned", k), (w + 2, 1)), lambda a, i, k=k: self.take_turned(a, i, k)))
                steps.append((*at.get(("norm", k), (w + 1, 2)), lambda a, i, k=k: self.norm(a, i, k)))
                if self.u[k].known is None:
                    steps.append((*at.get(("std", k), (w, 3)), lambda a, i, k=k: self.std(a, i, k)))
            return steps

        def tensor(self, at={}):
            steps = []
            for k, w in enumerate(self.when):
                steps.append((*at.get(("multiply", k), (w + 2, 0)), lambda pe, i, k=k: self.multiply(pe, i, k)))
                steps.append((*at.get(("turn", k), (w + 1, 1)), lambda pe, i, k=k: self.turn(pe, i, k)))
            return steps

        def copy_part(self, a, i, k, q, to):
            for half in range(2):
                bank = self.part(a, i, k, half, q)
                AC.activation(to[:, half * HALF:(half + 1) * HALF, :], bank, ACT.Copy).then_inc(self.s_done["A"], 1)

    def halves(b, half):
        return b[:, half * HALF:(half + 1) * HALF, :]

    class Tick:

        def __init__(self, x0, final, s_x0, s_stored, first):
            self.x0, self.final, self.s_x0, self.s_stored = x0, final, s_x0, s_stored
            self.first = first

            def from_layer(layer):
                def ready(v, i):
                    s, (writer, back) = self.stage, self.writer[layer]
                    v.wait_ge(s.s_done["D"], i * s.plan.by["D"] + s.plan.taken("D", writer, back=back))
                return ready

            def norms(i):
                g = (i * J + self.first * J) if not isinstance(i, int) else min(i + self.first, NB - 1) * J
                return scale0[:, bass.ds(g, J)], shift0[:, bass.ds(g, J)]

            def loaded(v, i):
                v.wait_ge(self.s_x0, START + i * 32 + 32)
            self.units = [Unit("l3", xl[3], [("r3", bias3["l3"], "D")], ready=from_layer(3)),
                          Unit("l2", xl[2], [("self2", None, "D")], ready=from_layer(2)),
                          Unit("l1", xl[1], [("sum1", bias3["l1"], "D")], ready=from_layer(1)),
                          Unit("l0", x0, [("bn0", bias3["bn0"], "D")], adds=True, ready=loaded, known=norms)]

        def place(self, stage, at):
            self.stage, self.k = stage, dict(zip((3, 2, 1, 0), at))
            self.writer = {n: (self.k[n - 1], 1) for n in (1, 2, 3)}

        def ends(self):
            return {self.k[n]: (lambda v, i, n=n: self.end(v, i, n)) for n in range(4)}

        def end(self, v, i, layer):
            s, k = self.stage, self.k[layer]
            if layer < 3:
                n = s.plan.index(self.k[layer + 1], 1, 0)
                v.wait_ge(s.s_done["D"], START + i * s.plan.by["D"] + s.plan.consumed(n, "D"))
            if layer == 3:
                if self.s_stored is not None:
                    v.wait_ge(self.s_stored, START + i * 32)
            if layer == 0:
                v.wait_ge(s.s_norm, START + i * (2 * s.plan.n) + 2 * k + 2)
                DV.tensor_tensor(xl[1][:, :, :], self.x0[:, :, :], s.h[k % NH][:, :, 0:C], ALU.add).then_inc(s.s_xh, 1)
                v.wait_ge(s.s_xh, START + i * s.plan.adders + s.plan.added(k))
            for half in range(2):
                ps = s.part(v, i, k, half, 0)
                if layer == 0:
                    ins = DV.scalar_tensor_tensor(out=halves(xl[1], half), in0=ps, scalar=0.0, in1=halves(xl[1], half),
                                                  op0=ALU.max, op1=ALU.add)
                elif layer == 2:
                    ins = DV.scalar_tensor_tensor(out=halves(xl[3], half), in0=ps, scalar=0.0, in1=halves(xl[2], half),
                                                  op0=ALU.max, op1=ALU.add)
                else:
                    to = xl[2] if layer == 1 else self.final
                    ins = DV.tensor_tensor(halves(to, half), ps, halves(xl[layer], half), ALU.add)
                ins.then_inc(s.s_done["D"], 1)

        def load(self, sp, i):
            s = self.stage
            wait_sp(sp, s.s_xh, i * s.plan.adders + (s.plan.added(self.k[0]) - s.plan.adders + START))
            at = min(i + self.first, NB - 1) * B if isinstance(i, int) else i * B + self.first * B
            split_load(sp, self.x0, x[bass.ds(at, B), :].rearrange("(p j) c -> p j c", j=J), self.s_x0)

        def store(self, sp, i):
            s, k = self.stage, self.k[3]
            wait_sp(sp, s.s_done["D"], i * s.plan.by["D"] + s.plan.taken("D", k))
            split_load(sp, out[bass.ds(i * B + (self.first - 3) * B, B), :].rearrange("(p j) c -> p j c", j=J),
                       self.final, self.s_stored)

        def moves(self, at={}):
            s = self.stage
            steps = [(s.when[self.k[0]] + 3 - s.period, 0, self.load)]
            last = at.get("store", (s.when[self.k[3]] + 3, 0))
            return steps + ([(*last, self.store)] if self.s_stored is not None else [])

    def wait_sw(pool, sem, value):
        pool.wait_ge(sem, value)
        pool.sem_inc(pool_passed, 1)

    def wait_sp(sp, sem, value):
        sp.wait_ge(sem, value)
        sp.sem_inc(sp_passed, 1)

    def gather(to, table, index):
        return GP.indirect_dma_start(out=to, out_offset=None, in_=table,
                                     in_offset=bass.IndirectOffsetOnAxis(ap=index, axis=0))

    def scatter(table, index, of, limit):
        return GP.indirect_dma_start(out=table, out_offset=bass.IndirectOffsetOnAxis(ap=index, axis=0), in_=of,
                                     in_offset=None, bounds_check=limit, oob_is_err=False)

    def by_tile(row):
        return row[:, :].rearrange("p (j q) -> p j q", q=P)

    def to_rows(c8):
        return c8[:, :].unsqueeze(2).to_broadcast([P, J, P])

    def bcast_row(t, i, n):
        return t[:, bass.ds(i * B, B)].to_broadcast([n, B])

    class Chain:

        def __init__(self, sem, steps):
            self.sem, self.steps, self.n, self.i, self.eng = sem, steps, 0, None, None

        def start(self, eng, i):
            assert self.n in (0, self.steps), self.n
            self.eng, self.i, self.n = eng, i, 0
            return self.step

        def step(self, ins):
            self.n += 1
            assert self.n <= self.steps
            ins.then_inc(self.sem, 1)
            self.eng.wait_ge(self.sem, self.i * self.steps + (self.n + START))

    class Runs:

        def __init__(self, ctx, tag, V, width, drow, s_row, carry_bank, banks):
            self.V, self.width, self.drow, self.s_row = V, width, drow, s_row
            self.carry_bank, self.banks = carry_bank, banks
            per = 512 // width
            self.groups = [range(g, min(g + per, J)) for g in range(0, J, per)]
            self.n = len(self.groups)
            t = lambda n, s, d=f32: ctx.enter_context(nc.sbuf_tensor(f"{tag}_run_{n}", s, d))
            s = lambda n: sem_of(ctx, f"{tag}_run_{n}")
            self.S, self.M, self.ends = t("S", [P, J, P]), t("M", [R, J, P]), t("ends", [P, J * R])
            self.on, self.kept, self.total = t("on", [R, R]), t("kept", [R, width]), t("total", [P, J, width])
            self.d8, self.last = t("d8", [P, J], i32), t("last", [R, 1], i32)
            self.s_eq, self.s_step = s("equalities_ready"), s("step")
            self.s_carry, self.s_kept, self.s_sum, self.s_total = s("carry_in_psum"), s("carry_kept"), s("sum_in_psum"), s("sum_kept")
            self.ch = Chain(self.s_step, 2)

        def clear(self):
            DV.memset(self.ends[:, :], 0.0)
            DV.memset(self.on[:, :], 0.0)
            return DV.memset(self.kept[:, :], 0.0)

        def equalities(self, v, i):
            step = self.ch.start(v, i)
            v.wait_ge(self.s_sum, START + i * self.n)
            DV.tensor_copy(self.d8[:, :], dst_i[:, bass.ds(i * J, J)])
            DV.tensor_copy(self.on[:, 0:1], goes_on[:, bass.ds(i, 1)])
            step(DV.tensor_copy(self.last[:, :], lasts[:, bass.ds(i, 1)]))
            v.wait_ge(self.s_row, START + i * 16 + 16)
            DV.scalar_tensor_tensor(out=self.M[:, :, :], in0=by_tile(self.drow)[0:R], scalar=self.last[:, 0:1],
                                    in1=earlier[:, :, :], op0=ALU.is_equal, op1=ALU.mult)
            step(DV.tensor_tensor(self.S[:, :, :], by_tile(self.drow), to_rows(self.d8), ALU.is_equal))
            DV.tensor_copy(self.ends[:, 1:J * R:R + 1], self.S[:, :, P - 1]).then_inc(self.s_eq, 1)

        def carry(self, pe, i):
            pe.wait_ge(self.s_eq, START + i + 1)
            pe.wait_ge(self.s_kept, START + i)
            out_ = self.carry_bank[0:R, :]
            for j in range(J):
                PE_.matmul(out_, self.ends[:, j * R:(j + 1) * R], self.V[:, j, :], start=j == 0, stop=False)
            PE_.matmul(out_, self.on[:, :], self.kept[:, :], start=False, stop=True).then_inc(self.s_carry, 1)

        def keep_carry(self, a, i):
            a.wait_ge(self.s_carry, START + i + 1)
            AC.activation(self.kept[:, :], self.carry_bank[0:R, :], ACT.Copy).then_inc(self.s_kept, 1)

        def bank(self, g):
            n = len(self.groups[g]) * self.width
            return self.banks[g % len(self.banks)][0:P, 0:n].rearrange("p (j c) -> p j c", c=self.width)

        def sums(self, *gs):
            def do(pe, i):
                if gs[0] == 0:
                    pe.wait_ge(self.s_kept, START + i + 1)
                for g in gs:
                    b = (g - len(self.banks), 0) if g >= len(self.banks) else (max(range(g, self.n, len(self.banks))), 1)
                    pe.wait_ge(self.s_total, i * self.n + (b[0] + 1 - b[1] * self.n + START))
                    for j in self.groups[g]:
                        to = self.bank(g)[:, j - self.groups[g][0], :]
                        PE_.matmul(to, self.S[:, j, :], self.V[:, j, :], start=True, stop=False)
                        ins = PE_.matmul(to, self.M[:, j, :], self.kept[:, :], start=False, stop=True)
                    ins.then_inc(self.s_sum, 1)
            return do

        def keep_sums(self, *gs):
            def do(a, i):
                for g in gs:
                    a.wait_ge(self.s_sum, i * self.n + (g + 1 + START))
                    js = self.groups[g]
                    AC.activation(self.total[:, js[0]:js[-1] + 1, :], self.bank(g), ACT.Copy).then_inc(self.s_total, 1)
            return do

        def used(self, eng, i):
            eng.wait_ge(self.s_sum, START + i * self.n)

        def ready(self, eng, i, g=None):
            g = self.n - 1 if g is None else g
            eng.wait_ge(self.s_total, i * self.n + (g + 1 + START))

    with ExitStack() as ctx:
        tile = lambda n, s, d=f32: ctx.enter_context(nc.sbuf_tensor("A_" + n, s, d))
        xu, xv = tile("xu", [P, J, C]), tile("xv", [P, J, C])
        xg = [tile(f"xg{n}", [P, J, C]) for n in range(4)]
        gram_bank = ctx.enter_context(nc.psum_tensor("A_gram", [128, 512], f32))
        t_bank, c_bank = (ctx.enter_context(nc.psum_tensor("A_" + n, [128, 512], f32)) for n in ("T", "carry"))
        s_u, s_v = dma_sem(ctx, "A_src_rows"), dma_sem(ctx, "A_dst_rows")
        s_xg = [sem_of(ctx, f"A_x_block{n}") for n in range(4)]
        uU = Unit("U", xu, [("lin0", None, "A"), ("gea", None, "D")], adds=True,
                  ready=lambda v, i: v.wait_ge(s_u, FIRST + i * (16 * J) + 16 * J))
        uV = Unit("V", xv, [("lin0", None, "A")], adds=True,
                  ready=lambda v, i: v.wait_ge(s_v, FIRST + i * (16 * J) + 16 * J))
        grams = [Unit(f"g{n}", xg[n], gram=True, ready=lambda v, i, n=n: v.wait_ge(s_xg[n], START + i * 32 + 32),
                       kept=lambda i, n=n: [t[:, bass.ds(i * (4 * J) + n * J, J)] for t in (scale0, shift0)])
                  for n in range(4)]
        kU, kV, kG = 0, 2, (1, 3, 4, 5)
        st = Stage(ctx, "A", [uU, grams[0], uV, *grams[1:]], gram_bank=gram_bank, banks=3)
        pl = st.plan
        gate = tile("gate", [P, J, C])
        V = tile("V", [P, J, 2 * C])
        junk = tile("junk", [P, J, P])
        upper = tile("upper", [P, P])
        drow, srow = tile("drow", [P, B], i32), tile("srow", [P, B], i32)
        a0b = {k: tile("a0" + k, [P, J, C]) for k in "DS"}
        yb = {k: tile("y0" + k, [P, J, C]) for k in "DS"}
        agg = tile("agg", [P, J, C])
        cor = tile("cor", [P, J, C])
        hh = tile("hh", [P, J, C])
        none = tile("none", [P, CW + 2])
        s8, l8 = tile("s8", [P, J], i32), tile("l8", [P, J])
        later = tile("later", [P, J])
        src8, dst8 = tile("src8", [P, J], i32), tile("dst8", [P, J], i32)
        once8, slot8 = tile("once8", [P, J], i32), tile("slot8", [P, J], i32)
        s_upper, s_set = sem_of(ctx, "A_upper_set"), sem_of(ctx, "A_constants_set")
        s_gl, s_dr, s_sr = sem_of(ctx, "A_gate_loaded"), sem_of(ctx, "A_dst_row"), sem_of(ctx, "A_src_row")
        s_gate = sem_of(ctx, "A_gate_ready")
        counting = Chain(sem_of(ctx, "A_counting_step"), 2)
        s_once, s_cnt = sem_of(ctx, "A_once_ready"), sem_of(ctx, "A_later_counted")
        runs = Runs(ctx, "A", V, 2 * C, drow, s_dr, c_bank[:, 0:2 * C], [t_bank])
        s_ag, s_cr, s_crd = sem_of(ctx, "A_end_step"), sem_of(ctx, "A_correction_ready"), sem_of(ctx, "A_correction_read")
        division = [Chain(sem_of(ctx, f"A_division_step{n}"), 3) for n in range(2)]
        s_sta = {k: sem_of(ctx, "A_stored_x_plus_h_" + k) for k in "DS"}
        s_sty = {k: sem_of(ctx, "A_stored_y_" + k) for k in "DS"}
        s_cols2 = sem_of(ctx, "A_once_columns")
        s_cols, s_map = sem_of(ctx, "A_pool_columns"), dma_sem(ctx, "A_slot_named")
        s_gram = sem_of(ctx, "A_gram_done")
        start_semaphores()
        block = ctx.enter_context(nc.Block())

        @block.gpsimd
        def _(pool):
            GP.memset(upper[:, :], 1.0).then_inc(s_upper, 1)
            pool.wait_ge(s_upper, START + 1)
            GP.affine_select(out=upper[:, :], in_=upper[:, :], compare_op=ALU.is_gt, fill=0.0, base=0,
                             pattern=[[1, P]], channel_multiplier=-1).then_inc(s_upper, 1)
            prime(pool)

            def slots(pool, i):
                pool.wait_ge(s_once, START + i + 1)
                pool.wait_ge(s_map, FIRST + i * (16 * J))
                GP.tensor_copy(once8[:, :], once_i[:, bass.ds(i * J, J)]).then_inc(s_cols2, 1)
                GP.tensor_copy(slot8[:, :], slot_v[:, bass.ds(i * J, J)]).then_inc(s_cols2, 1)
                wait_sw(pool, s_cols2, START + i * 2 + 2)

            def name_slot(pool, i, j):
                wait_sw(pool, s_map, FIRST + i * (16 * J) + 16 * j)
                scatter(slot_of[:, :], once8[:, j:j + 1], slot8[:, j:j + 1], N - 1).then_inc(s_map, 16)

            def fetch(pool, i):
                pool.wait_ge(s_u, FIRST + i * (16 * J))
                pool.wait_ge(s_v, FIRST + i * (16 * J))
                GP.tensor_copy(src8[:, :], src_i[:, bass.ds(i * J, J)]).then_inc(s_cols, 1)
                GP.tensor_copy(dst8[:, :], dst_i[:, bass.ds(i * J, J)]).then_inc(s_cols, 1)
                wait_sw(pool, s_cols, START + i * 2 + 2)
                slots(pool, i)
                wait_sw(pool, st.s_norm, i * (2 * pl.n) + (2 * kU + 2 - 2 * pl.n + START))
                wait_sw(pool, st.s_xh, i * pl.adders + (START - 1))
                for j in range(J):
                    gather(xu[:, j, :], x[:, :], src8[:, j:j + 1]).then_inc(s_u, 16)
                    if j % 2:
                        name_slot(pool, i, j // 2)
                wait_sw(pool, st.s_norm, i * (2 * pl.n) + (2 * kV + 2 - 2 * pl.n + START))
                wait_sw(pool, st.s_xh, START + i * pl.adders)
                for j in range(J):
                    gather(xv[:, j, :], x[:, :], dst8[:, j:j + 1]).then_inc(s_v, 16)
                    if j % 2:
                        name_slot(pool, i, HALF + j // 2)
            with pool.Fori(0, EIT) as i:
                fetch(pool, i)
            pool.wait_ge(s_map, FIRST + 16 * T)

        @block.sync
        def _(sp):
            def load_gate(sp, i):
                wait_sp(sp, s_gate, START + i)
                split_load(sp, gate, rows(edge_attr, i), s_gl)

            def load_targets(sp, i):
                wait_sp(sp, runs.s_eq, START + i)
                sp.dma_start(drow[:, :], bcast_row(dst_row, i, P)).then_inc(s_dr, 16)

            def load_sources(sp, i):
                wait_sp(sp, s_cnt, START + i)
                sp.dma_start(srow[:, :], bcast_row(src_row, i, P)).then_inc(s_sr, 16)

            def load_block(n):
                def do(sp, i):
                    wait_sp(sp, st.s_norm, i * (2 * pl.n) + (2 * kG[n] + 2 - 2 * pl.n + START))
                    split_load(sp, xg[n], x[bass.ds(i * (4 * B) + n * B, B), :].rearrange("(p j) c -> p j c", j=J),
                               s_xg[n])
                return do

            def store_sum(k, n):
                def do(sp, i):
                    wait_sp(sp, st.s_xh, START + i * 2 + n)
                    split_load(sp, own(a0[k], i), a0b[k], s_sta[k])
                return do

            def store_y(sp, i):
                wait_sp(sp, st.s_done["A"], i * pl.by["A"] + pl.taken("A", kU))
                split_load(sp, own(y0["S"], i), yb["S"], s_sty["S"])

            def store_conv(sp, i):
                wait_sp(sp, s_ag, START + i * 2 + 1)
                split_load(sp, own(y0["D"], i), hh, s_sty["D"])
            pipeline(sp, st.period, [(2 - 6, 0, load_gate), (2 - 6, -1, load_targets), (-4 - 6, -0.5, load_sources),
                                     (3, 1, store_sum("S", 1)), (5, 3.5, store_sum("D", 2)), (3, 2, store_y),
                                     (7, 2, store_conv)]
                     + [(kG[n] + 2 - 6, 3, load_block(n)) for n in range(4)])
            for k in "DS":
                sp.wait_ge(s_sta[k], START + 32 * EIT)
                sp.wait_ge(s_sty[k], START + 32 * EIT)

        @block.vector
        def _(v):
            DV.memset(none[:, :], 0.0)
            runs.clear()
            for n in range(NH):
                last = DV.memset(st.h[n][:, :, C:CW], 1.0)
            last.then_inc(s_set, 1)
            v.wait_ge(s_upper, START + 2)

            def repeats(v, i):
                step = counting.start(v, i)
                v.wait_ge(s_once, START + i)
                step(DV.tensor_copy(s8[:, :], src_i[:, bass.ds(i * J, J)]))
                v.wait_ge(s_sr, START + i * 16 + 16)
                for j in range(J):
                    ins = DV.scalar_tensor_tensor(out=junk[:, j, :], in0=srow[:, j * P:(j + 1) * P], scalar=s8[:, j:j + 1],
                                                  in1=upper[:, :], op0=ALU.is_equal, op1=ALU.mult,
                                                  accum_out=later[:, j:j + 1])
                ins.then_inc(s_cnt, 1)
                v.wait_ge(s_cnt, START + i + 1)
                step(DV.tensor_scalar(again[:, bass.ds(i * J, J)], later[:, :], 1.0, None, ALU.min))
                DV.scalar_tensor_tensor(out=once_i[:, bass.ds(i * J, J)], in0=again[:, bass.ds(i * J, J)],
                                        scalar=float(N), in1=s8[:, :], op0=ALU.mult, op1=ALU.add).then_inc(s_once, 1)

            def add_h(v, i, k, to, x_, s_stored):
                v.wait_ge(s_stored, START + i * 32)
                v.wait_ge(st.s_norm, START + i * (2 * pl.n) + 2 * k + 2)
                DV.tensor_tensor(to[:, :, :], x_[:, :, :], st.h[k % NH][:, :, 0:C], ALU.add).then_inc(st.s_xh, 1)

            def end_u(v, i):
                add_h(v, i, kU, a0b["S"], xu, s_sta["S"])
                v.wait_ge(s_gate, START + i + 1)
                for half in range(2):
                    ps = st.part(v, i, kU, half, 1)
                    sl = slice(half * HALF, half * HALF + HALF)
                    DV.tensor_tensor(V[:, sl, C:2 * C], ps, V[:, sl, 0:C], ALU.mult).then_inc(st.s_done["D"], 1)

            def end_v(v, i):
                add_h(v, i, kV, a0b["D"], xv, s_sta["D"])

            def divide(half):
                def do(v, i):
                    step = division[half].start(v, i)
                    a_ = halves(agg, half)
                    runs.ready(v, i, 2 * half + 1)
                    v.wait_ge(s_crd, START + i * (2 * J))
                    step(DV.tensor_scalar(a_, halves(runs.total, half)[:, :, 0:C], GATE_EPS, None, ALU.add))
                    step(DV.reciprocal(a_, a_))
                    step(DV.tensor_tensor(a_, a_, halves(runs.total, half)[:, :, C:2 * C], ALU.mult))
                return do

            def finish(v, i):
                v.wait_ge(s_sty["D"], START + i * 32)
                DV.tensor_copy(l8[:, :], leads[:, bass.ds(i * J, J)])
                v.wait_ge(st.s_done["A"], i * pl.by["A"] + pl.taken("A", kV))
                DV.tensor_tensor(hh[:, :, :], agg[:, :, :], yb["D"][:, :, :], ALU.add).then_inc(s_ag, 1)
                v.wait_ge(s_ag, START + i * 2 + 1)
                DV.tensor_tensor(cor[:, :, :], hh[:, :, :], yb["D"][:, :, :], ALU.add).then_inc(s_ag, 1)
                v.wait_ge(s_ag, START + i * 2 + 2)
                DV.tensor_tensor(cor[:, :, :], cor[:, :, :], agg[:, :, :], ALU.mult).then_inc(s_cr, 1)
            pipeline(v, st.period, st.vector({kU: end_u, kV: end_v}, {("end", 2): (4, 1.5)})
                     + [(-3, 3, repeats), (2, 4, runs.equalities), (5, 3, divide(0)), (6, 3, divide(1)), (7, 3, finish)])
            v.wait_ge(s_gram, START + 1)
            DV.tensor_copy(gram_sb[:, :], gram_bank[:, 0:CW + 2])

        @block.scalar
        def _(a):
            a.wait_ge(s_set, START + 1)

            def gates(a, i):
                a.wait_ge(s_gl, START + i * 32 + 32)
                runs.used(a, i)
                AC.activation(V[:, :, 0:C], gate[:, :, :], ACT.Sigmoid).then_inc(s_gate, 1)

            def take_u(a, i):
                a.wait_ge(s_sty["S"], START + i * 32)
                st.copy_part(a, i, kU, 0, yb["S"])

            def take_v(a, i):
                a.wait_ge(s_cr, START + i)
                st.copy_part(a, i, kV, 0, yb["D"])

            def keep_sums(a, i):
                a.wait_ge(s_cr, START + i)
                runs.keep_sums(0)(a, i)
            pipeline(a, st.period, st.scalar({kV: take_v}, {("turned", 2): (4, 0)})
                     + [(kU + 2, 2.5, take_u), (2, 4, gates), (4, 0.5, runs.keep_carry), (4, 4, keep_sums), (5, 0.5, runs.keep_sums(1)),
                        (5, 4, runs.keep_sums(2)), (6, 0.5, runs.keep_sums(3))])

        @block.tensor
        def _(pe):
            pe.wait_ge(s_set, START + 1)
            PE_.matmul(gram_bank[:, 0:CW + 2], none[:, 0:C], none[:, :], start=True, stop=False)

            def carry(pe, i):
                pe.wait_ge(st.s_done["D"], i * pl.by["D"] + pl.taken("D", kU, 1, 1))
                runs.carry(pe, i)

            def corrections(pe, i):
                pe.wait_ge(s_cr, START + i + 1)
                for j in range(J):
                    PE_.matmul(gram_bank[:, CW:CW + 1], agg[:, j, :], l8[:, j:j + 1], start=False, stop=False)\
                        .then_inc(s_crd, 1)
                    PE_.matmul(gram_bank[:, CW + 1:CW + 2], cor[:, j, :], l8[:, j:j + 1], start=False, stop=False)\
                        .then_inc(s_crd, 1)
            pipeline(pe, st.period, st.tensor({("turn", 3): (5, -1.5), ("turn", 4): (6, -0.5), ("multiply", 5): (6, -1.5)})
                     + [(4, -1, carry), (4, 2, runs.sums(0)), (4, 2.5, runs.sums(1)),
                        (5, 2, runs.sums(2)), (6, -1, runs.sums(3)), (8, 2, corrections)])
            PE_.matmul(gram_bank[:, 0:CW + 2], none[:, 0:C], none[:, :], start=False, stop=True).then_inc(s_gram, 1)

    clear_semaphores()

    with ExitStack() as ctx:
        tile = lambda n, s, d=f32: ctx.enter_context(nc.sbuf_tensor("N_" + n, s, d))
        bank = [ctx.enter_context(nc.psum_tensor(f"N_p{n}", [128, 512], f32)) for n in range(4)]
        col = tile("col", [C, 12])
        ws = tile("ws", [C, C])
        junk = tile("junk", [C, C])
        full = [tile(f"full{n}", [C, P]) for n in range(2)]
        rest = tile("rest", [1, HALF * C])
        piece = tile("piece", [1, 3, HALF * C], bf16)
        step_ = sem_of(ctx, "N_dve_step")
        s_mm, s_std, s_moved = sem_of(ctx, "N_matmul"), sem_of(ctx, "N_std"), sem_of(ctx, "N_bias_moved")
        s_full = sem_of(ctx, "N_scaled")
        s_piece = sem_of(ctx, "N_pieces")
        start_semaphores()
        block = ctx.enter_context(nc.Block())

        VAR_STEP = 7

        @block.tensor
        def _(pe):
            PE_.matmul(bank[0][:, 0:1], W["lin0"][:, :], gram_sb[:, C:C + 1], start=True, stop=True)
            PE_.matmul(bank[1][:, 0:C], W["lin0"][:, :], gram_sb[:, 0:C], start=True, stop=True).then_inc(s_mm, 1)
            pe.wait_ge(s_full, START + 1)
            PE_.transpose(bank[2][:, 0:C], ws[:, :], ident[:, :])
            PE_.matmul(bank[3][0:P, 0:C], full[0][:, :], ident[:, :], start=True, stop=True)
            PE_.matmul(bank[3][0:P, C:2 * C], full[1][:, :], ident[:, :], start=True, stop=True).then_inc(s_mm, 1)

        @block.scalar
        def _(a):
            a.wait_ge(step_, START + VAR_STEP)
            AC.activation(col[:, 5:6], col[:, 4:5], ACT.Sqrt, bias=col[:, 11:12]).then_inc(s_std, 1)
            a.wait_ge(s_piece, START + 1)
            for q in range(3):
                a.dma_start(bias3["bn0"][q:q + 1, :], piece[:, q, :]).then_inc(s_moved, 16)
            a.wait_ge(s_moved, START + 48)

        @block.vector
        def _(v):
            n = [0]

            def step(ins):
                n[0] += 1
                ins.then_inc(step_, 1)
                v.wait_ge(step_, START + n[0])

            v.wait_ge(s_mm, START + 1)
            step(DV.memset(col[:, 11:12], BN_EPS))
            step(DV.tensor_tensor(col[:, 0:1], bank[0][:, 0:1], gram_sb[:, CW:CW + 1], ALU.add))
            step(DV.scalar_tensor_tensor(out=junk[:, :], in0=bank[1][:, 0:C], scalar=1.0, in1=W["lin0_rows"][:, :],
                                         op0=ALU.mult, op1=ALU.mult, accum_out=col[:, 1:2]))
            step(DV.tensor_tensor(col[:, 1:2], col[:, 1:2], gram_sb[:, CW + 1:CW + 2], ALU.add))
            step(DV.tensor_scalar(col[:, 2:3], col[:, 0:1], 1.0 / N, None, ALU.mult))
            step(DV.tensor_tensor(col[:, 3:4], col[:, 2:3], col[:, 2:3], ALU.mult))
            step(DV.scalar_tensor_tensor(out=col[:, 4:5], in0=col[:, 1:2], scalar=1.0 / N, in1=col[:, 3:4],
                                         op0=ALU.mult, op1=ALU.subtract))
            assert n[0] == VAR_STEP
            v.wait_ge(s_std, START + 1)
            step(DV.reciprocal(col[:, 6:7], col[:, 5:6]))
            step(DV.tensor_tensor(col[:, 7:8], col[:, 6:7], gam_col[:, :], ALU.mult))
            step(DV.tensor_tensor(col[:, 8:9], col[:, 7:8], col[:, 2:3], ALU.mult))
            step(DV.tensor_tensor(col[:, 9:10], bet_col[:, :], col[:, 8:9], ALU.subtract))
            step(DV.tensor_scalar(ws[:, :], W["lin0_rows"][:, :], col[:, 7:8], None, ALU.mult))
            for q in range(2):
                step(DV.memset(full[q][:, :], 1.0))
                step(DV.tensor_scalar(full[q][:, :], full[q][:, :], col[:, 7 + 2 * q:8 + 2 * q], None, ALU.mult))
            v.sem_inc(s_full, 1)
            v.wait_ge(s_mm, START + 2)
            DV.tensor_copy(W["bn0"][:, :], bank[2][:, 0:C])
            DV.tensor_copy(bn_mul[:, :], bank[3][0:P, 0:C])
            step(DV.tensor_copy(bn_add[:, :], bank[3][0:P, C:2 * C]))
            for r in range(HALF):
                step(DV.tensor_copy(rest[:, r * C:(r + 1) * C], bn_add[0:1, :]))
            for q in range(3):
                step(DV.tensor_copy(piece[:, q, :], rest[:, :]))
                step(DV.tensor_tensor(rest[:, :], rest[:, :], piece[:, q, :], ALU.subtract))
            v.sem_inc(s_piece, 1)

    with ExitStack() as ctx:
        tile = lambda n, s, d=f32: ctx.enter_context(nc.sbuf_tensor("W_" + n, s, d))
        x0, final = tile("x0", [P, J, C]), tile("final", [P, J, C])
        s_x0 = sem_of(ctx, "W_x_block")
        tick = Tick(x0, final, s_x0, None, 0)
        st = Stage(ctx, "W", tick.units, period=5)
        tick.place(st, range(4))
        start_semaphores()
        block = ctx.enter_context(nc.Block())

        @block.sync
        def _(sp):
            pipeline(sp, st.period, tick.moves(), 3)

        @block.vector
        def _(v):
            pipeline(v, st.period, st.vector(tick.ends()), 3)

        @block.scalar
        def _(a):
            pipeline(a, st.period, st.scalar(), 3)

        @block.tensor
        def _(pe):
            pipeline(pe, st.period, st.tensor(), 3)

    with ExitStack() as ctx:
        tile = lambda n, s, d=f32: ctx.enter_context(nc.sbuf_tensor("B_" + n, s, d))
        sem = lambda n: sem_of(ctx, "B_" + n)
        x0, final = tile("x0", [P, J, C]), tile("final", [P, J, C])
        s_x0, s_fin = sem("x_block"), sem("out_stored")
        a0b = {k: tile("a0" + k, [P, J, C]) for k in "DS"}
        yb = {k: tile("y0" + k, [P, J, C]) for k in "DS"}
        pj = {k: tile("proj" + k, [P, J, C]) for k in "DS"}
        res = tile("res", [P, J, C])
        x2s = tile("x2s", [P, J, C])
        part2 = [tile(f"part2{n}", [P, J, C]) for n in range(3)]
        lead8, slot8 = tile("lead8", [P, J], i32), tile("slot8", [P, J], i32)
        s_in = {k: sem("loaded_" + k) for k in "DS"}
        s_x1 = {k: sem("x1_ready_" + k) for k in "DS"}
        bn_step = {k: Chain(sem("bn_step_" + k), 2) for k in "DS"}
        s_pst = {k: sem("stored_proj_" + k) for k in "DS"}
        s_rst, s_xst = sem("stored_res"), sem("stored_x2")
        s_2st = [sem(f"stored_part2{n}") for n in range(3)]
        s_cols, s_map = sem("pool_columns"), dma_sem(ctx, "B_slot_named")
        tick = Tick(x0, final, s_x0, s_fin, 3)
        uD = Unit("D1", a0b["D"], [("lin1", None, "A"), ("res1", bias3["l1"], "D")],
                  ready=lambda v, i: v.wait_ge(s_x1["D"], START + i + 1))
        uS = Unit("S1", a0b["S"], [("lin1", None, "A"), ("sum1", bias3["l1"], "D")],
                  ready=lambda v, i: v.wait_ge(s_x1["S"], START + i + 1))
        uT = Unit("S2", x2s, [("self2", None, "A"), ("fwd2", None, "A"), ("bwd2", None, "A")],
                  ready=lambda v, i: v.wait_ge(st.s_done["D"], i * pl.by["D"] + pl.taken("D", kS, 1, 1)))
        t3, t2, t1, t0 = tick.units
        st = Stage(ctx, "B", [uS, t3, t2, t1, uT, t0, uD])
        kS, kT, kD = 0, 4, 6
        tick.place(st, (1, 2, 3, 5))
        pl = st.plan
        start_semaphores()
        block = ctx.enter_context(nc.Block())

        @block.gpsimd
        def _(pool):
            prime(pool)
            with pool.Fori(0, EIT) as i:
                pool.wait_ge(s_map, FIRST + i * (16 * J))
                GP.tensor_copy(lead8[:, :], lead_i[:, bass.ds(i * J, J)]).then_inc(s_cols, 1)
                GP.tensor_copy(slot8[:, :], slot_e[:, bass.ds(i * J, J)]).then_inc(s_cols, 1)
                wait_sw(pool, s_cols, START + i * 2 + 2)
                for j in range(J):
                    scatter(slot_of[:, :], lead8[:, j:j + 1], slot8[:, j:j + 1], N - 1).then_inc(s_map, 16)
            pool.wait_ge(s_map, FIRST + 16 * T)

        @block.sync
        def _(sp):
            def load(k, unit):
                def do(sp, i):
                    wait_sp(sp, st.s_done["D"], i * pl.by["D"] + pl.taken("D", unit, 1, 1, back=1))
                    split_load(sp, a0b[k], own(a0[k], i), s_in[k])
                    split_load(sp, yb[k], own(y0[k], i), s_in[k])
                return do

            def store(k, unit):
                def do(sp, i):
                    wait_sp(sp, st.s_done["A"], i * pl.by["A"] + pl.taken("A", unit))
                    split_load(sp, rows(proj1, i, E if k == "S" else 0), pj[k], s_pst[k])
                    wait_sp(sp, st.s_done["D"], i * pl.by["D"] + pl.taken("D", unit, 1, 1))
                    if k == "S":
                        split_load(sp, own(x2t["S"], i), x2s, s_xst)
                    else:
                        split_load(sp, own(res1, i), res, s_rst)
                return do

            def store_parts(sp, i):
                for q, to in enumerate((own(self2["S"], i), rows(fwd2, i, E), rows(bwd2, i, E))):
                    wait_sp(sp, st.s_done["A"], i * pl.by["A"] + pl.taken("A", kT, 1, q))
                    split_load(sp, to, part2[q], s_2st[q])
            n = st.period
            pipeline(sp, n, tick.moves() + [(kS + 3 - n, 1, load("S", kS)), (kD + 3 - n, 1, load("D", kD)),
                                            (kS + 3, 2, store("S", kS)), (kD + 3, 2, store("D", kD)),
                                            (kT + 3, 3, store_parts)])
            for s_ in (s_fin, s_pst["D"], s_pst["S"], s_rst, s_xst, *s_2st):
                sp.wait_ge(s_, START + 32 * EIT)

        @block.vector
        def _(v):
            def start(k):
                def do(v, i):
                    step = bn_step[k].start(v, i)
                    v.wait_ge(s_in[k], START + i * 64 + 64)
                    mul = bn_mul[:, :].unsqueeze(1).to_broadcast([P, J, C])
                    add = bn_add[:, :].unsqueeze(1).to_broadcast([P, J, C])
                    step(DV.tensor_tensor(yb[k][:, :, :], yb[k][:, :, :], mul, ALU.mult))
                    step(DV.tensor_tensor(yb[k][:, :, :], yb[k][:, :, :], add, ALU.add))
                    DV.scalar_tensor_tensor(out=a0b[k][:, :, :], in0=yb[k][:, :, :], scalar=0.0, in1=a0b[k][:, :, :],
                                            op0=ALU.max, op1=ALU.add).then_inc(s_x1[k], 1)
                return do

            def end(k, unit, to, s_stored):
                def do(v, i):
                    v.wait_ge(s_stored, START + i * 32)
                    for half in range(2):
                        ps = st.part(v, i, unit, half, 1)
                        DV.tensor_tensor(halves(to, half), ps, halves(a0b[k], half), ALU.add)\
                            .then_inc(st.s_done["D"], 1)
                return do
            pipeline(v, st.period, st.vector({kS: end("S", kS, x2s, s_xst), kD: end("D", kD, res, s_rst), **tick.ends()},
                                           {("end", 0): (3, 0.5), ("stats", 1): (0, 1.5), ("stats", 2): (2, 2.5),
                                            ("stats", 6): (6, 2.5)})
                     + [(kS - 1, 3, start("S")), (kD - 1, 3, start("D"))])

        @block.scalar
        def _(a):
            def proj(k, unit):
                def do(a, i):
                    a.wait_ge(s_pst[k], START + i * 32)
                    st.copy_part(a, i, unit, 0, pj[k])
                return do

            def second(a, i):
                for half in range(2):
                    for q in range(3):
                        if half == 0:
                            a.wait_ge(s_2st[q], START + i * 32)
                        bank = st.part(a, i, kT, half, q)
                        AC.activation(halves(part2[q], half), bank, ACT.Copy).then_inc(st.s_done["A"], 1)
            pipeline(a, st.period, st.scalar({kS: proj("S", kS), kD: proj("D", kD), kT: second}, {("std", 1): (1, 1.5)}))

        @block.tensor
        def _(pe):
            pipeline(pe, st.period, st.tensor())

    clear_semaphores()

    with ExitStack() as ctx:
        tile = lambda n, s, d=f32: ctx.enter_context(nc.sbuf_tensor("C_" + n, s, d))
        sem = lambda n: sem_of(ctx, "C_" + n)
        psum = lambda n, w=512: ctx.enter_context(nc.psum_tensor("C_" + n, [128, w], f32))
        x0, final = tile("x0", [P, J, C]), tile("final", [P, J, C])
        s_x0, s_fin = sem("x_block"), sem("out_stored")
        pu, pv = tile("pu", [P, J, C]), tile("pv", [P, J, C])
        pv_kept = tile("pv_kept", [P, J, C])
        z, mixed = tile("z", [P, J, C]), tile("mixed", [P, J, C])
        CH = C + H
        V = tile("V", [P, J, CH])
        drow = tile("drow", [P, B], i32)
        drow4, dprev = tile("drow4", [H, B], i32), tile("dprev", [H, B], i32)
        s_seg, s_dr4 = sem("segments_ready"), sem("segment_rows")
        apart = tile("apart", [H, B + 1])
        lgT, F, G = tile("lgT", [H, B]), tile("F", [H, B]), tile("G", [H, B])
        f_last, f_diff, f_diag = tile("f_last", [H, 1]), tile("f_diff", [H, 1]), tile("f_diag", [H, H])
        ones_h = tile("ones_h", [H, P])
        att_b, eb_b = tile("att_b", [P, C]), tile("eb_b", [P, H])
        lg, ls, ew, mf = (tile(n, [P, J, H]) for n in ("lg", "ls", "ew", "mf"))
        red8 = tile("red8", [P, J])
        JH = J * H
        arg, ex = tile("arg", [P, 3 * JH + H]), tile("ex", [P, 3 * JH + H])
        den, gd, ed = (tile(n, [P, J, H]) for n in ("den", "gd", "ed"))
        resb, x2b = tile("resb", [P, J, C]), tile("x2b", [P, J, C])
        part2 = [tile(f"part2{n}", [P, J, C]) for n in range(3)]
        src8, dst8 = tile("src8", [P, J], i32), tile("dst8", [P, J], i32)
        ss8, sd8 = tile("ss8", [P, J], i32), tile("sd8", [P, J], i32)
        t_bank, r_bank = psum("T"), psum("R")
        l_bank = psum("L")
        s_con, s_con2, s_set = sem("att_loaded"), sem("eb_loaded"), sem("constants_set")
        s_pu, s_pv, s_slots = (dma_sem(ctx, "C_" + n) for n in ("src_rows", "dst_rows", "slots_fetched"))
        s_cols = sem("pool_columns")
        s_dr, s_rl = sem("index_rows"), sem("res_loaded")
        s_lg, s_ls, s_kept = sem("logits_ready"), sem("self_logits_ready"), sem("pv_kept")
        s_lT, s_lgT, s_G, s_R = sem("logits_turned"), sem("logits_row_ready"), sem("maximum_ready"), sem("maximum_turned")
        s_arg, s_ex, s_V = sem("exponents_ready"), sem("exp_ready"), sem("values_ready")
        s_x2 = sem("x2_ready")
        runs = Runs(ctx, "C", V, CH, drow, s_dr, r_bank[:, 64:64 + CH], [t_bank])
        s_xst, s_2st = sem("stored_x2"), [sem(f"stored_part2{n}") for n in range(3)]
        tick = Tick(x0, final, s_x0, s_fin, 3 + EIT)
        uD = Unit("D2", x2b, [("self2", None, "A"), ("fwd2", None, "A"), ("bwd2", None, "A")],
                  ready=lambda v, i: v.wait_ge(s_x2, START + i + 1))
        st = Stage(ctx, "C", tick.units + [uD], period=6, when=[0, 1, 2, 3, 5], banks=3)
        kD = 4
        tick.place(st, range(4))
        pl = st.plan
        ch = {n: Chain(sem("step_" + n), c) for n, c in (("logits", 4), ("self", 3), ("segments", 1), ("maxima", 3),
                                                         ("exponents", 1), ("finish", 7))}
        start_semaphores()
        block = ctx.enter_context(nc.Block())

        @block.gpsimd
        def _(pool):
            prime(pool)

            def fetch(i):
                pool.wait_ge(s_pu, FIRST + i * (16 * J))
                pool.wait_ge(s_pv, FIRST + i * (16 * J))
                pool.wait_ge(s_slots, FIRST + i * (32 * J))
                GP.tensor_copy(src8[:, :], src_i[:, bass.ds(i * J, J)]).then_inc(s_cols, 1)
                GP.tensor_copy(dst8[:, :], dst_i[:, bass.ds(i * J, J)]).then_inc(s_cols, 1)
                wait_sw(pool, s_cols, START + i * 4 + 2)
                for j in range(J):
                    gather(ss8[:, j:j + 1], slot_of[:, :], src8[:, j:j + 1]).then_inc(s_slots, 16)
                    gather(sd8[:, j:j + 1], slot_of[:, :], dst8[:, j:j + 1]).then_inc(s_slots, 16)
                wait_sw(pool, s_slots, FIRST + i * (32 * J) + 32 * J)
                GP.tensor_copy(slot_s[:, bass.ds(i * J, J)], ss8[:, :]).then_inc(s_cols, 1)
                GP.tensor_copy(slot_d[:, bass.ds(i * J, J)], sd8[:, :]).then_inc(s_cols, 1)
                pool.wait_ge(s_kept, START + i)
                wait_sw(pool, s_lg, START + i)
                for j in range(J):
                    gather(pv[:, j, :], proj1[:, :], sd8[:, j:j + 1]).then_inc(s_pv, 16)
                wait_sw(pool, s_V, START + i)
                for j in range(J):
                    gather(pu[:, j, :], proj1[:, :], ss8[:, j:j + 1]).then_inc(s_pu, 16)
            with pool.Fori(0, EIT) as i:
                fetch(i)
            pool.wait_ge(s_cols, START + 4 * EIT)

        @block.sync
        def _(sp):
            sp.dma_start(att_b[:, :], att.to_broadcast([P, C])).then_inc(s_con, 16)
            sp.dma_start(eb_b[:, :], w_eb.to_broadcast([P, H])).then_inc(s_con2, 16)

            def load_targets(sp, i):
                wait_sp(sp, runs.s_eq, START + i)
                sp.dma_start(drow[:, :], bcast_row(dst_row, i, P)).then_inc(s_dr, 16)

            def load_segments(sp, i):
                wait_sp(sp, s_seg, START + i)
                sp.dma_start(drow4[:, :], bcast_row(dst_row, i, H)).then_inc(s_dr4, 16)
                sp.dma_start(dprev[:, :], bcast_row(dst_prev_row, i, H)).then_inc(s_dr4, 16)

            def load_res(sp, i):
                wait_sp(sp, s_x2, START + i)
                split_load(sp, resb, own(res1, i), s_rl)

            def store_x2(sp, i):
                wait_sp(sp, s_x2, START + i + 1)
                split_load(sp, own(x2t["D"], i), x2b, s_xst)

            def store_parts(sp, i):
                for q, to in enumerate((own(self2["D"], i), rows(fwd2, i), rows(bwd2, i))):
                    wait_sp(sp, st.s_done["A"], i * pl.by["A"] + pl.taken("A", kD, 1, q))
                    split_load(sp, to, part2[q], s_2st[q])
            pipeline(sp, st.period, tick.moves() + [(1 - 6, 1, load_targets), (-7, 1, load_segments), (-1, 1.5, load_res), (1, 1.5, store_x2),
                                                    (8, 3, store_parts)])
            for s_ in (s_fin, s_xst, *s_2st):
                sp.wait_ge(s_, START + 32 * EIT)

        @block.vector
        def _(v):
            runs.clear()
            DV.memset(ones_h[:, :], 1.0)
            DV.memset(apart[:, B:B + 1], -FAR)
            DV.memset(f_last[:, :], -FAR).then_inc(s_set, 1)
            v.wait_ge(s_set, START + 1)
            v.wait_ge(s_con, START + 16)
            v.wait_ge(s_con2, START + 16)
            heads = lambda t: t.rearrange("p j (h c) -> p j h c", c=HC)
            spread = lambda t: t.unsqueeze(3).to_broadcast([P, J, H, HC])
            a_row = att_b[:, :].unsqueeze(1).to_broadcast([P, J, C])
            e_row = eb_b[:, :].unsqueeze(1).to_broadcast([P, J, H])
            part = lambda t, n: t[:, n * JH:(n + 1) * JH].rearrange("p (j h) -> p j h", h=H)

            def logits(v, i):
                step = ch["logits"].start(v, i)
                v.wait_ge(s_ls, START + i + 1)
                v.wait_ge(s_pv, FIRST + i * (16 * J) + 16 * J)
                v.wait_ge(s_pu, FIRST + i * (16 * J) + 16 * J)
                DV.tensor_copy(red8[:, :], reduced[:, bass.ds(i * J, J)])
                step(DV.tensor_tensor(z[:, :, :], pu[:, :, :], pv[:, :, :], ALU.add))
                step(DV.scalar_tensor_tensor(out=z[:, :, :], in0=z[:, :, :], scalar=SLOPE, in1=z[:, :, :],
                                             op0=ALU.mult, op1=ALU.max))
                DV.tensor_tensor(ew[:, :, :], red8[:, :].unsqueeze(2).to_broadcast([P, J, H]), e_row, ALU.mult)
                step(DV.tensor_tensor(z[:, :, :], z[:, :, :], a_row, ALU.mult))
                step(DV.tensor_reduce(lg[:, :, :], heads(z[:, :, :]), AX.X, ALU.add))
                DV.tensor_tensor(lg[:, :, :], lg[:, :, :], ew[:, :, :], ALU.add).then_inc(s_lg, 1)

            def self_logits(v, i):
                step = ch["self"].start(v, i)
                v.wait_ge(s_pv, FIRST + i * (16 * J) + 16 * J)
                v.wait_ge(s_arg, START + i)
                v.wait_ge(s_lg, START + i)
                step(DV.scalar_tensor_tensor(out=z[:, :, :], in0=pv[:, :, :], scalar=SLOPE, in1=pv[:, :, :],
                                             op0=ALU.mult, op1=ALU.max))
                step(DV.tensor_tensor(z[:, :, :], z[:, :, :], a_row, ALU.mult))
                step(DV.tensor_reduce(ls[:, :, :], heads(z[:, :, :]), AX.X, ALU.add))
                DV.scalar_tensor_tensor(out=ls[:, :, :], in0=ls[:, :, :], scalar=2.0, in1=e_row,
                                        op0=ALU.mult, op1=ALU.add).then_inc(s_ls, 1)

            def segments(v, i):
                step = ch["segments"].start(v, i)
                v.wait_ge(s_dr4, START + i * 32 + 32)
                step(DV.tensor_tensor(apart[:, 0:B], drow4[:, :], dprev[:, :], ALU.not_equal))
                DV.tensor_scalar(apart[:, 0:B], apart[:, 0:B], -FAR, None, ALU.mult).then_inc(s_seg, 1)
                v.wait_ge(s_seg, START + i + 1)

            def maxima(v, i):
                step = ch["maxima"].start(v, i)
                v.wait_ge(s_lgT, START + i * 2 + 2)
                step(DV.tensor_tensor_scan(F[:, :], apart[:, 0:B], lgT[:, :], f_last[:, 0:1], ALU.add, ALU.max))
                step(DV.tensor_tensor_scan(G[:, ::-1], apart[:, B:0:-1], F[:, ::-1], -FAR, ALU.add, ALU.max))
                step(DV.tensor_tensor(f_diff[:, :], f_last[:, :], G[:, 0:1], ALU.subtract))
                DV.tensor_copy(f_last[:, :], F[:, B - 1:B])
                DV.tensor_scalar(f_diag[:, :], ident[0:H, 0:H], f_diff[:, 0:1], None, ALU.mult).then_inc(s_G, 1)

            def exponents(v, i):
                step = ch["exponents"].start(v, i)
                v.wait_ge(s_lg, START + i + 1)
                v.wait_ge(s_ls, START + i + 1)
                v.wait_ge(s_R, START + i + 1)
                m = part(r_bank[0:P, :], 0)
                step(DV.tensor_tensor(mf[:, :, :], m, ls[:, :, :], ALU.max))
                DV.tensor_tensor(part(arg, 0), lg[:, :, :], m, ALU.subtract)
                DV.tensor_tensor(part(arg, 1), m, mf[:, :, :], ALU.subtract)
                DV.tensor_tensor(part(arg, 2), ls[:, :, :], mf[:, :, :], ALU.subtract)
                DV.tensor_scalar(arg[:, 3 * JH:], r_bank[0:P, JH:JH + H], 0.0, None, ALU.min).then_inc(s_arg, 1)

            def values(v, i):
                v.wait_ge(s_ex, START + i + 1)
                DV.tensor_tensor(heads(V[:, :, 0:C]), heads(pu[:, :, :]), spread(part(ex, 0)), ALU.mult)
                DV.tensor_copy(V[:, :, C:CH], part(ex, 0))
                f, kept = ex[0:R, 3 * JH:3 * JH + H], runs.kept
                DV.tensor_tensor(kept[:, C:CH], kept[:, C:CH], f, ALU.mult)
                before = kept[:, 0:C].rearrange("p (h c) -> p h c", c=HC)
                DV.tensor_tensor(before, before, f.unsqueeze(2).to_broadcast([R, H, HC]), ALU.mult).then_inc(s_V, 1)

            def finish(v, i):
                step = ch["finish"].start(v, i)
                g, es, total = part(ex, 1), part(ex, 2), runs.total[:, :, C:CH]
                runs.ready(v, i)
                step(DV.tensor_tensor(den[:, :, :], total, g, ALU.mult))
                step(DV.tensor_tensor(den[:, :, :], den[:, :, :], es, ALU.add))
                step(DV.tensor_scalar(den[:, :, :], den[:, :, :], 1e-12, None, ALU.max))
                step(DV.reciprocal(den[:, :, :], den[:, :, :]))
                DV.tensor_tensor(gd[:, :, :], den[:, :, :], g, ALU.mult)
                step(DV.tensor_tensor(ed[:, :, :], den[:, :, :], es, ALU.mult))
                v.wait_ge(s_kept, START + i + 1)
                DV.tensor_tensor(heads(mixed[:, :, :]), heads(runs.total[:, :, 0:C]), spread(gd[:, :, :]), ALU.mult)
                step(DV.tensor_tensor(heads(z[:, :, :]), heads(pv_kept[:, :, :]), spread(ed[:, :, :]), ALU.mult))
                v.wait_ge(s_rl, START + i * 32 + 32)
                step(DV.tensor_tensor(z[:, :, :], z[:, :, :], resb[:, :, :], ALU.add))
                v.wait_ge(s_xst, START + i * 32)
                v.wait_ge(st.s_norm, i * (2 * pl.n) + (2 * kD + 2 - 2 * pl.n + START))
                DV.tensor_tensor(x2b[:, :, :], mixed[:, :, :], z[:, :, :], ALU.add).then_inc(s_x2, 1)
            pipeline(v, st.period, st.vector(tick.ends(), {("stats", 2): (2, -0.5), ("end", 2): (4, 3.5), ("coef", 3): (3, 2.5), ("end", 3): (6, 0.5)})
                     + [(-4, 3, self_logits), (-3, 3, logits), (-1, 3, segments), (-1, 4, maxima), (0, 3, exponents),
                        (1, 3, values), (1, 4, runs.equalities), (4, 3, finish)])

        @block.scalar
        def _(a):
            def keep_pv(a, i):
                a.wait_ge(s_pv, FIRST + i * (16 * J) + 16 * J)
                a.wait_ge(s_x2, START + i)
                AC.activation(pv_kept[:, :, :], pv[:, :, :], ACT.Copy).then_inc(s_kept, 1)

            def logit_rows(n):
                def do(a, i):
                    a.wait_ge(s_lT, START + i * 2 + n + 1)
                    AC.activation(lgT[:, n * (B // 2):(n + 1) * (B // 2)], l_bank[0:H, 0:B // 2], ACT.Copy)\
                        .then_inc(s_lgT, 1)
                return do

            def exponentials(a, i):
                a.wait_ge(s_arg, START + i + 1)
                AC.activation(ex[:, :], arg[:, :], ACT.Exp).then_inc(s_ex, 1)

            def second(a, i):
                for half in range(2):
                    for q in range(3):
                        if half == 0:
                            a.wait_ge(s_2st[q], START + i * 32)
                        bank = st.part(a, i, kD, half, q)
                        AC.activation(halves(part2[q], half), bank, ACT.Copy).then_inc(st.s_done["A"], 1)
            def keep_first(a, i):
                a.wait_ge(s_x2, START + i)
                runs.keep_sums(0)(a, i)
            pipeline(a, st.period, st.scalar(at={("turned", 2): (3, 3), ("turned", 3): (4, 4.5), ("turned", 4): (6, 2.5)})
                     + [(7, 2.5, second), (-2, 1.5, logit_rows(0)), (-2, 4, logit_rows(1)), (-2, 5, keep_pv), (1, 0.5, exponentials),
                        (2, 1.5, runs.keep_carry), (2, 4, keep_first),
                        (3, 1.5, runs.keep_sums(1)), (3, 4, runs.keep_sums(2))])

        @block.tensor
        def _(pe):
            pe.wait_ge(s_set, START + 1)

            def turn_logits(half):
                def do(pe, i):
                    pe.wait_ge(s_lg, START + i + 1)
                    pe.wait_ge(s_lgT, START + i * 2 + half)
                    for j in range(HALF):
                        ins = PE_.transpose(l_bank[0:H, j * P:(j + 1) * P], lg[:, half * HALF + j, :], ident[0:P, 0:P])
                    ins.then_inc(s_lT, 1)
                return do

            def turn_maxima(pe, i):
                pe.wait_ge(s_G, START + i + 1)
                pe.sem_inc(pe_passed, 1)
                for j in range(J):
                    PE_.transpose(r_bank[0:P, j * H:(j + 1) * H], G[:, j * P:(j + 1) * P], ident[0:H, 0:H])
                PE_.matmul(r_bank[0:P, JH:JH + H], ones_h[:, :], f_diag[:, :], start=True, stop=True).then_inc(s_R, 1)

            def carry(pe, i):
                pe.wait_ge(s_V, START + i + 1)
                runs.carry(pe, i)
            pipeline(pe, st.period, st.tensor({("turn", 1): (3, -0.5)})
                     + [(-2, -1, turn_logits(0)), (-2, 0.5, turn_logits(1)), (1, -0.5, turn_maxima), (2, -1, carry), (2, 2, runs.sums(0)),
                        (3, -0.25, runs.sums(1)), (3, 2, runs.sums(2))])

    clear_semaphores()

    with ExitStack() as ctx:
        tile = lambda n, s, d=f32: ctx.enter_context(nc.sbuf_tensor("D_" + n, s, d))
        sem = lambda n: sem_of(ctx, "D_" + n)
        psum = lambda n: ctx.enter_context(nc.psum_tensor("D_" + n, [128, 512], f32))
        x0, final = tile("x0", [P, J, C]), tile("final", [P, J, C])
        s_x0, s_fin = sem("x_block"), sem("out_stored")
        fu, bv = tile("fu", [P, J, CW]), tile("bv", [P, J, CW])
        bs, Q = tile("bs", [P, J, CW]), tile("Q", [P, J, P])
        drow, srow = tile("drow", [P, B], i32), tile("srow", [P, B], i32)
        s8, ss8 = (tile(n, [P, J], i32) for n in ("s8", "ss8"))
        a8, pd8, rc8 = (tile(n, [P, J]) for n in ("a8", "pd8", "rc8"))
        idx8 = tile("idx8", [P, J], i32)
        from8, to8 = tile("from8", [P, J], i32), tile("to8", [P, J], i32)
        selfb, meanb, sumb = tile("selfb", [P, J, C]), tile("meanb", [P, J, C]), tile("sumb", [P, J, C])
        PER = 3
        GROUPS = [range(g, min(g + PER, J)) for g in range(0, J, PER)]
        t_bank, b_bank = psum("T"), [psum(f"B{n}") for n in range(len(GROUPS))]
        s_set, s_cols, s_col = sem("constants_set"), sem("pool_columns"), sem("back_columns")
        s_fu, s_bv, s_add = (dma_sem(ctx, "D_" + n) for n in ("src_rows", "dst_rows", "back_added"))
        s_dr, s_sr, s_sl, s_eq = sem("dst_row"), sem("src_row"), sem("self_loaded"), sem("equalities_ready")
        s_B, s_Bs = sem("back_in_psum"), sem("back_kept")
        runs = Runs(ctx, "D", fu, CW, drow, s_dr, b_bank[-1][:, 2 * CW:3 * CW], [t_bank])
        s_idx, s_sum, s_sst = sem("back_index_ready"), sem("self_plus_mean"), sem("stored_self")
        tick = Tick(x0, final, s_x0, s_fin, 3 + 2 * EIT)
        st = Stage(ctx, "D", tick.units, period=5, banks=2)
        tick.place(st, range(4))
        pl = st.plan
        ch = {n: Chain(sem("step_" + n), c) for n, c in (("source", 1), ("index", 2), ("finish", 3))}
        start_semaphores()
        block = ctx.enter_context(nc.Block())

        @block.gpsimd
        def _(pool):
            prime(pool)
            pool.wait_ge(s_set, START + 1)

            def fetch(pool, i):
                more = not isinstance(i, int) or i < EIT
                adds = not isinstance(i, int) or i > 0
                if more:
                    pool.wait_ge(s_fu, FIRST + i * (16 * J))
                    pool.wait_ge(s_bv, FIRST + i * (16 * J))
                    GP.tensor_copy(from8[:, :], slot_s[:, bass.ds(i * J, J)]).then_inc(s_cols, 1)
                    GP.tensor_copy(to8[:, :], slot_d[:, bass.ds(i * J, J)]).then_inc(s_cols, 1)
                    wait_sw(pool, s_cols, START + i * 2 + 2)
                    wait_sw(pool, runs.s_sum, START + i * runs.n)
                    for j in range(J):
                        gather(fu[:, j, 0:C], fwd2[:, :], from8[:, j:j + 1]).then_inc(s_fu, 16)
                    wait_sw(pool, s_B, START + i * len(GROUPS))
                if adds:
                    wait_sw(pool, s_idx, START + i)
                    wait_sw(pool, s_Bs, START + i * len(GROUPS))
                for j in range(J):
                    if more:
                        gather(bv[:, j, 0:C], bwd2[:, :], to8[:, j:j + 1]).then_inc(s_bv, 16)
                    if adds:
                        wait_sw(pool, s_add, i * (16 * J) + (16 * j + FIRST - 16 * J))
                        GP.indirect_dma_start(out=back[:, :], in_=bs[:, j, :], in_offset=None, compute_op=ALU.add,
                                              out_offset=bass.IndirectOffsetOnAxis(ap=idx8[:, j:j + 1], axis=0))\
                            .then_inc(s_add, 16)
            fetch(pool, 0)
            with pool.Fori(1, EIT) as i:
                fetch(pool, i)
            fetch(pool, EIT)
            pool.wait_ge(s_add, FIRST + 16 * T)

        @block.sync
        def _(sp):
            def load_indices(sp, i):
                wait_sp(sp, runs.s_eq, START + i)
                wait_sp(sp, s_eq, START + i)
                sp.dma_start(drow[:, :], bcast_row(dst_row, i, P)).then_inc(s_dr, 16)
                sp.dma_start(srow[:, :], bcast_row(src_row, i, P)).then_inc(s_sr, 16)

            def load_self(sp, i):
                wait_sp(sp, s_sum, START + i)
                split_load(sp, selfb, own(self2["D"], i), s_sl)

            def store_sum(sp, i):
                wait_sp(sp, s_sum, START + i + 1)
                split_load(sp, own(self2["D"], i), sumb, s_sst)
            pipeline(sp, st.period, tick.moves({"store": (1, 0.5)}) + [(-4, 1, load_indices), (-2, 1, load_self), (3, 2, store_sum)])
            for s_ in (s_fin, s_sst):
                sp.wait_ge(s_, START + 32 * EIT)

        @block.vector
        def _(v):
            runs.clear()
            DV.memset(fu[:, :, C:CW], 1.0)
            DV.memset(bv[:, :, C:CW], 1.0).then_inc(s_set, 1)
            v.wait_ge(s_set, START + 1)

            def same_source(v, i):
                step = ch["source"].start(v, i)
                v.wait_ge(s_B, START + i * len(GROUPS))
                step(DV.tensor_copy(s8[:, :], src_i[:, bass.ds(i * J, J)]))
                v.wait_ge(s_sr, START + i * 16 + 16)
                DV.tensor_tensor(Q[:, :, :], by_tile(srow), to_rows(s8), ALU.is_equal).then_inc(s_eq, 1)

            def back_index(v, i):
                step = ch["index"].start(v, i)
                v.wait_ge(s_add, FIRST + i * (16 * J))
                DV.tensor_copy(a8[:, :], again[:, bass.ds(i * J, J)])
                DV.tensor_copy(ss8[:, :], slot_s[:, bass.ds(i * J, J)]).then_inc(s_col, 1)
                v.wait_ge(s_col, START + i + 1)
                step(DV.tensor_tensor(pd8[:, :], pads[:, :], ss8[:, :], ALU.subtract))
                step(DV.tensor_tensor(pd8[:, :], pd8[:, :], a8[:, :], ALU.mult))
                DV.tensor_tensor(idx8[:, :], pd8[:, :], ss8[:, :], ALU.add).then_inc(s_idx, 1)

            def finish(v, i):
                step = ch["finish"].start(v, i)
                runs.ready(v, i)
                step(DV.tensor_scalar(rc8[:, :], runs.total[:, :, C], 1.0, None, ALU.max))
                step(DV.reciprocal(rc8[:, :], rc8[:, :]))
                step(DV.tensor_tensor(meanb[:, :, :], runs.total[:, :, 0:C], rc8[:, :].unsqueeze(2).to_broadcast([P, J, C]),
                                      ALU.mult))
                v.wait_ge(s_sl, START + i * 32 + 32)
                v.wait_ge(s_sst, START + i * 32)
                DV.tensor_tensor(sumb[:, :, :], meanb[:, :, :], selfb[:, :, :], ALU.add).then_inc(s_sum, 1)
            pipeline(v, st.period, st.vector(tick.ends(), {("stats", 0): (-1, 4.5), ("stats", 1): (0, 3.5)})
                     + [(0, 3, runs.equalities), (1, 3, same_source), (3, 3, finish), (4, 4, back_index)])

        @block.scalar
        def _(a):
            def keep_first(a, i):
                a.wait_ge(s_sum, START + i)
                runs.keep_sums(0)(a, i)

            def keep_back(a, i):
                a.wait_ge(s_add, FIRST + i * (16 * J))
                for n, g in enumerate(GROUPS):
                    a.wait_ge(s_B, START + i * len(GROUPS) + n + 1)
                    AC.activation(bs[:, g[0]:g[-1] + 1, :],
                                  b_bank[n][0:P, 0:len(g) * CW].rearrange("p (j c) -> p j c", c=CW), ACT.Copy)\
                        .then_inc(s_Bs, 1)
            pipeline(a, st.period, st.scalar() + [(1, 0.5, runs.keep_carry), (1, 4, keep_first), (2, 0.5, runs.keep_sums(1)),
                                                  (2, 4, runs.keep_sums(2)), (3, 4, keep_back)])

        @block.tensor
        def _(pe):
            pe.wait_ge(s_set, START + 1)

            def carry(pe, i):
                pe.wait_ge(s_fu, FIRST + i * (16 * J) + 16 * J)
                runs.carry(pe, i)

            def backs(pe, i):
                pe.wait_ge(s_bv, FIRST + i * (16 * J) + 16 * J)
                pe.wait_ge(s_eq, START + i + 1)
                pe.wait_ge(s_Bs, START + i * len(GROUPS))
                for n, g in enumerate(GROUPS):
                    for j in g:
                        at = (j - g[0]) * CW
                        ins = PE_.matmul(b_bank[n][0:P, at:at + CW], Q[:, j, :], bv[:, j, :], start=True, stop=True)
                    ins.then_inc(s_B, 1)
            pipeline(pe, st.period, st.tensor({("turn", 0): (2, -1.5)})
                     + [(1, -1, carry), (1, 2, runs.sums(0)), (2, -1, runs.sums(1)),
                        (2, 0.5, runs.sums(2)), (3, -0.5, backs)])

    with ExitStack() as ctx:
        tile = lambda n, s, d=f32: ctx.enter_context(nc.sbuf_tensor("E_" + n, s, d))
        sem = lambda n: sem_of(ctx, "E_" + n)
        x2b = {k: tile("x2" + k, [P, J, C]) for k in "DS"}
        selfb = {k: tile("self" + k, [P, J, C]) for k in "DS"}
        backb = {k: tile("back" + k, [P, J, CW]) for k in "DS"}
        x3b = {k: tile("x3" + k, [P, J, C]) for k in "DS"}
        x4b = {k: tile("x4" + k, [P, J, C]) for k in "DS"}
        pj = {k: tile("proj" + k, [P, J, C]) for k in "DS"}
        rc8 = {k: tile("rc8" + k, [P, J]) for k in "DS"}
        s_in = {k: sem("loaded_" + k) for k in "DS"}
        s_x3 = {k: sem("x3_ready_" + k) for k in "DS"}
        s_pst = {k: sem("stored_proj_" + k) for k in "DS"}
        s_xst = {k: sem("stored_x4_" + k) for k in "DS"}
        x0, final = tile("x0", [P, J, C]), tile("final", [P, J, C])
        s_x0, s_fin = sem("x_block"), sem("out_stored")
        tick = Tick(x0, final, s_x0, s_fin, 3 + 3 * EIT)
        units = [Unit(k + "3", x3b[k], [("l3", None, "A"), ("r3", bias3["l3"], "D")],
                      ready=lambda v, i, k=k: v.wait_ge(s_x3[k], START + i + 1)) for k in "DS"]
        st = Stage(ctx, "E", tick.units + units)
        kk = {"D": 4, "S": 5}
        tick.place(st, range(4))
        pl = st.plan
        ch = {k: Chain(sem("dve_step_" + k), 4) for k in "DS"}
        start_semaphores()
        block = ctx.enter_context(nc.Block())

        @block.sync
        def _(sp):
            def load(k, base):
                def do(sp, i):
                    wait_sp(sp, s_x3[k], START + i)
                    split_load(sp, x2b[k], own(x2t[k], i), s_in[k])
                    split_load(sp, selfb[k], own(self2[k], i), s_in[k])
                    split_load(sp, backb[k], rows(back, i, base), s_in[k])
                return do

            def store(k, base):
                def do(sp, i):
                    wait_sp(sp, st.s_done["A"], i * pl.by["A"] + pl.taken("A", kk[k]))
                    split_load(sp, rows(proj3, i, base), pj[k], s_pst[k])
                    wait_sp(sp, st.s_done["D"], i * pl.by["D"] + pl.taken("D", kk[k], 1, 1))
                    split_load(sp, own(x4[k], i), x4b[k], s_xst[k])
                return do
            pipeline(sp, st.period, tick.moves() + [(3 - 6, 4, load("D", 0)), (4 - 6, 4, load("S", E)),
                                                    (4 + 3, 2, store("D", 0)), (5 + 3, 2, store("S", E))], tail=3)
            sp.wait_ge(s_fin, START + 32 * EIT)
            for k in "DS":
                sp.wait_ge(s_pst[k], START + 32 * EIT)
                sp.wait_ge(s_xst[k], START + 32 * EIT)

        @block.vector
        def _(v):
            def start(k):
                def do(v, i):
                    step = ch[k].start(v, i)
                    v.wait_ge(s_in[k], START + i * 96 + 96)
                    step(DV.tensor_scalar(rc8[k][:, :], backb[k][:, :, C], 1.0, None, ALU.max))
                    step(DV.reciprocal(rc8[k][:, :], rc8[k][:, :]))
                    step(DV.tensor_tensor(backb[k][:, :, 0:C], backb[k][:, :, 0:C],
                                          rc8[k][:, :].unsqueeze(2).to_broadcast([P, J, C]), ALU.mult))
                    step(DV.tensor_tensor(selfb[k][:, :, :], selfb[k][:, :, :], backb[k][:, :, 0:C], ALU.add))
                    n = kk[k]
                    v.wait_ge(st.s_norm, i * (2 * pl.n) + (2 * n + 2 - 2 * pl.n + START))
                    v.wait_ge(st.s_done["D"], i * pl.by["D"] + pl.taken("D", n, 1, 1, back=1))
                    DV.scalar_tensor_tensor(out=x3b[k][:, :, :], in0=selfb[k][:, :, :], scalar=0.0, in1=x2b[k][:, :, :],
                                            op0=ALU.max, op1=ALU.add).then_inc(s_x3[k], 1)
                return do

            def end(k):
                def do(v, i):
                    n = kk[k]
                    v.wait_ge(s_xst[k], START + i * 32)
                    for half in range(2):
                        ps = st.part(v, i, n, half, 1)
                        DV.tensor_tensor(halves(x4b[k], half), ps, halves(x3b[k], half), ALU.add)\
                            .then_inc(st.s_done["D"], 1)
                return do
            pipeline(v, st.period, st.vector({4: end("D"), 5: end("S"), **tick.ends()},
                                                     {("coef", 2): (3, 2.5), ("stats", 2): (2, -0.5)})
                     + [(3, 3, start("D")), (4, 3, start("S"))], tail=3)

        @block.scalar
        def _(a):
            def proj(k):
                def do(a, i):
                    a.wait_ge(s_pst[k], START + i * 32)
                    st.copy_part(a, i, kk[k], 0, pj[k])
                return do
            pipeline(a, st.period, st.scalar({4: proj("D"), 5: proj("S")}))

        @block.tensor
        def _(pe):
            pipeline(pe, st.period, st.tensor())

    with ExitStack() as ctx:
        tile = lambda n, s, d=f32: ctx.enter_context(nc.sbuf_tensor("F_" + n, s, d))
        sem = lambda n: sem_of(ctx, "F_" + n)
        pu = tile("pu", [P, J, CW])
        drow = tile("drow", [P, B], i32)
        ss8, sv8, s8 = (tile(n, [P, J], i32) for n in ("ss8", "sv8", "s8"))
        rc8, far8 = tile("rc8", [P, J]), tile("far8", [P, J])
        outs8, from8, lead8 = (tile(n, [P, J], i32) for n in ("outs8", "from8", "lead8"))
        x4d, x4s, meanb, outb = (tile(n, [P, J, C]) for n in ("x4d", "x4s", "meanb", "outb"))
        t_banks = [ctx.enter_context(nc.psum_tensor(f"F_T{n}", [128, 512], f32)) for n in range(3)]
        c_bank = ctx.enter_context(nc.psum_tensor("F_carry", [128, 512], f32))
        s_pu, s_out = dma_sem(ctx, "F_src_rows"), dma_sem(ctx, "F_rows_written")
        s_set, s_from, s_lead, s_dr, s_ld, s_ls = (sem(n) for n in (
            "constants_set", "slots_copied", "leads_copied", "dst_row", "x4_D_loaded", "x4_S_loaded"))
        s_res, s_idx = sem("rows_ready"), sem("places_ready")
        runs = Runs(ctx, "F", pu, CW, drow, s_dr, c_bank[:, 0:CW], t_banks)
        ch = {n: Chain(sem("step_" + n), c) for n, c in (("places", 2), ("finish", 3))}
        start_semaphores()
        block = ctx.enter_context(nc.Block())

        @block.gpsimd
        def _(pool):
            prime(pool)
            pool.wait_ge(s_set, START + 1)

            def fetch(pool, i):
                runs.used(pool, i)
                pool.wait_ge(s_pu, FIRST + i * (16 * J))
                GP.tensor_copy(from8[:, :], slot_s[:, bass.ds(i * J, J)]).then_inc(s_from, 1)
                wait_sw(pool, s_from, START + i + 1)
                for j in range(J):
                    gather(pu[:, j, 0:C], proj3[:, :], from8[:, j:j + 1]).then_inc(s_pu, 16)

            def put(pool, i):
                pool.wait_ge(s_out, FIRST + i * (32 * J))
                GP.tensor_copy(lead8[:, :], lead_i[:, bass.ds(i * J, J)]).then_inc(s_lead, 1)
                pool.wait_ge(s_lead, START + i + 1)
                pool.wait_ge(s_idx, START + i + 1)
                wait_sw(pool, s_ls, START + i * 32 + 32)
                for j in range(J):
                    scatter(out[:, :], outs8[:, j:j + 1], x4s[:, j, :], N - 1).then_inc(s_out, 16)
                wait_sw(pool, s_res, START + i + 1)
                for j in range(J):
                    scatter(out[:, :], lead8[:, j:j + 1], outb[:, j, :], N - 1).then_inc(s_out, 16)
            pipeline(pool, 1, [(-1, 0, fetch), (0, 1, put)])
            pool.wait_ge(s_out, FIRST + 32 * T)

        @block.sync
        def _(sp):
            with sp.Fori(0, EIT) as i:
                wait_sp(sp, runs.s_eq, START + i)
                sp.dma_start(drow[:, :], bcast_row(dst_row, i, P)).then_inc(s_dr, 16)
                wait_sp(sp, s_res, START + i)
                split_load(sp, x4d, own(x4["D"], i), s_ld)
                wait_sp(sp, s_out, FIRST + i * (32 * J))
                split_load(sp, x4s, own(x4["S"], i), s_ls)

        @block.vector
        def _(v):
            runs.clear()
            DV.memset(pu[:, :, C:CW], 1.0).then_inc(s_set, 1)
            v.wait_ge(s_set, START + 1)

            def places(v, i):
                step = ch["places"].start(v, i)
                DV.tensor_copy(ss8[:, :], slot_s[:, bass.ds(i * J, J)])
                DV.tensor_copy(sv8[:, :], slot_v[:, bass.ds(i * J, J)])
                step(DV.tensor_copy(s8[:, :], src_i[:, bass.ds(i * J, J)]))
                step(DV.tensor_tensor(far8[:, :], ss8[:, :], sv8[:, :], ALU.not_equal))
                v.wait_ge(s_out, FIRST + i * (32 * J))
                DV.scalar_tensor_tensor(out=outs8[:, :], in0=far8[:, :], scalar=float(N), in1=s8[:, :],
                                        op0=ALU.mult, op1=ALU.add).then_inc(s_idx, 1)

            def finish(v, i):
                step = ch["finish"].start(v, i)
                runs.ready(v, i)
                step(DV.tensor_scalar(rc8[:, :], runs.total[:, :, C], 1.0, None, ALU.max))
                step(DV.reciprocal(rc8[:, :], rc8[:, :]))
                step(DV.tensor_tensor(meanb[:, :, :], runs.total[:, :, 0:C], rc8[:, :].unsqueeze(2).to_broadcast([P, J, C]),
                                      ALU.mult))
                v.wait_ge(s_ld, START + i * 32 + 32)
                v.wait_ge(s_out, FIRST + i * (32 * J))
                DV.tensor_tensor(outb[:, :, :], meanb[:, :, :], x4d[:, :, :], ALU.add).then_inc(s_res, 1)
            pipeline(v, 1, [(0, 0, runs.equalities), (0, 1, finish), (0, 2, places)])

        @block.scalar
        def _(a):
            def keep(a, i):
                runs.keep_carry(a, i)
                a.wait_ge(s_res, START + i)
                runs.keep_sums(0, 1, 2)(a, i)
            pipeline(a, 1, [(0, 0, keep)])

        @block.tensor
        def _(pe):
            pe.wait_ge(s_set, START + 1)

            def add_up(pe, i):
                pe.wait_ge(s_pu, FIRST + i * (16 * J) + 16 * J)
                runs.carry(pe, i)
                runs.sums(0, 1, 2)(pe, i)
            pipeline(pe, 1, [(0, 0, add_up)])
    top.close()


def kernel(x, src, dst, edge_attr_128, edge_attr_2, L0_gnn_W_gea, L0_gnn_W_lin, L0_gnn_gamma, L0_gnn_beta,
           L1_gnn_W_lin, L1_gnn_att, L1_gnn_W_eb, L1_gnn_bias, L1_gnn_W_res, L2_gnn_W, L3_gnn_W_l, L3_gnn_W_r,
           L3_gnn_b_l):
    import numpy as np
    import concourse.bacc as bacc
    from concourse.bass_utils import run_bass_kernel_spmd as run

    arrays = layout(np, x, src, dst, edge_attr_128, edge_attr_2, L0_gnn_W_gea, L0_gnn_W_lin, L0_gnn_gamma,
                    L0_gnn_beta, L1_gnn_W_lin, L1_gnn_att, L1_gnn_W_eb, L1_gnn_bias, L1_gnn_W_res, L2_gnn_W,
                    L3_gnn_W_l, L3_gnn_W_r, L3_gnn_b_l)
    nc = bacc.Bacc("TRN2", target_bir_lowering=False, num_devices=1)
    args = [nc.dram_tensor(n, a.shape, mybir.dt.from_np(a.dtype), kind="ExternalInput").ap() for n, a in arrays.items()]
    out = nc.dram_tensor("out", x.shape, f32, kind="ExternalOutput").ap()
    gnn_program(nc, *args, out)
    return run(nc, [arrays], core_ids=[0]).results[0]["out"]


def layout(np, x, src, dst, edge_attr, edge_attr2, w_gea, w_lin0, gamma, beta, w_lin1, att, w_eb, bias1, w_res1,
           w2, w_l3, w_r3, b_l3):
    c = np.ascontiguousarray
    x, src, dst, w2 = (np.asarray(a) for a in (x, src, dst, w2))
    tiles = src.shape[0] // P
    none = np.full(1, -1, dst.dtype)
    ends = dst[P - 1::P].reshape(tiles // J, J)
    before = np.concatenate([none, ends[:-1, J - 1]])[None, :]
    run_last = np.concatenate([before, ends.T])
    first = np.full((J + 1, 1), -1, dst.dtype)
    by_tile = lambda a: c(a.reshape(tiles, P).T)
    return {
        "x": c(x), "src_pt": by_tile(src), "dst_pt": by_tile(dst), 
        "run_last": c(run_last), "run_last_before": c(np.concatenate([first, run_last[:, :-1]], axis=1)),
        "run_end_before": c(np.broadcast_to(before, run_last.shape)),
        "dst_next_pt": by_tile(np.concatenate([dst[1:], none])),
        "src_row": c(src[None, :]), "dst_row": c(dst[None, :]),
        "dst_prev_row": c(np.concatenate([none, dst[:-1]])[None, :]),
        "edge_attr": c(edge_attr), "edge_attr2_pt": c(np.asarray(edge_attr2).reshape(tiles, P, 2).transpose(1, 0, 2)),
        "w_gea": c(np.asarray(w_gea).T), "w_lin0": c(w_lin0), "w_lin0_t": c(np.asarray(w_lin0).T),
        "gamma": c(np.asarray(gamma)[:, None]), "beta": c(np.asarray(beta)[:, None]),
        "w_lin1": c(np.asarray(w_lin1).T), "att": c(np.asarray(att).reshape(1, C)),
        "w_eb": c(np.asarray(w_eb).reshape(1, H)), "bias1": c(np.asarray(bias1)[None, :]),
        "w_res1": c(np.asarray(w_res1).T), "w_self2": c(w2[:, 0:C].T), "w_fwd2": c(w2[:, C:2 * C].T),
        "w_bwd2": c(w2[:, 2 * C:].T), "w_l3": c(np.asarray(w_l3).T), "w_r3": c(np.asarray(w_r3).T),
        "b_l3": c(np.asarray(b_l3)[None, :]),
    }
```
